# Optimizing a Trainium2 kernel written in Bass

```python
import numpy as np
import jax
import jax.numpy as jnp

def _softmax(x, axis=-1):
    return jax.nn.softmax(x, axis=axis)

def _gelu(x):
    return jax.nn.gelu(x, approximate=True)

def _silu(x):
    return jax.nn.silu(x)

def _sigmoid(x):
    return jax.nn.sigmoid(x)

def _layernorm(x, axis=-1, eps=1e-05):
    m = jnp.mean(x, axis=axis, keepdims=True)
    v = jnp.var(x, axis=axis, keepdims=True)
    return (x - m) / jnp.sqrt(v + eps)

def _scatter_add(tgt, idx, src, axis=0):
    return tgt.at[idx].add(src)

def _segment_sum(src, seg, n):
    return jax.ops.segment_sum(src, seg, n)
kernel_name = 'mk_gnn_preln_d2_gnn_r8_776128'

def setup_inputs(seed: int=0):
    np.random.seed(seed)
    _w = jnp.asarray

    def _rec_inputs():
        import jax
        import jax.numpy as jnp
        _gk = jax.random.key(seed)
        x = -0.000202 + 1 * jax.random.normal(jax.random.fold_in(_gk, 1), (6250, 128), jnp.float32)
        _s = jax.random.randint(jax.random.fold_in(_gk, 2), (50000,), 0, 6250, jnp.int32)
        _d = jax.random.randint(jax.random.fold_in(_gk, 3), (50000,), 0, 6250, jnp.int32)
        _loop = jnp.arange(6250, dtype=jnp.int32)
        src = jnp.concatenate([_s, _d, _loop])
        dst = jnp.concatenate([_d, _s, _loop])
        _o = jnp.argsort(dst, stable=True)
        src = src[_o]
        dst = dst[_o]
        edge_type_4 = jax.random.randint(jax.random.fold_in(_gk, 12), (106250,), 0, 4, jnp.int32)
        return (x, src, dst, edge_type_4)
    x, src, dst, edge_type_4 = _rec_inputs()

    def _L0_gnn_setup():
        import jax, jax.numpy as jnp
        import numpy as np
        N, E, IN, OUT = (6250, 100000, 128, 128)
        R = 5
        key = jax.random.key(seed)
        k = jax.random.split(key, 6)
        x = jax.random.normal(k[0], (N, IN), jnp.float32)
        src = jax.random.randint(k[1], (E,), 0, N)
        dst = jax.random.randint(k[2], (E,), 0, N)
        rel = jax.random.randint(k[3], (E,), 0, R - 1)
        xavier = np.sqrt(2.0) * np.sqrt(6.0 / (IN + OUT))
        weight = jax.random.uniform(k[4], (R, IN, OUT), jnp.float32, -xavier, xavier)
        bias = jax.random.uniform(k[5], (R, OUT), jnp.float32, -xavier, xavier)
        return dict(x=x, weight=weight, bias=bias, src=src, dst=dst, rel=rel)
    _L0_gnn_all = _L0_gnn_setup()
    _L0_gnn_in = {k: v for k, v in _L0_gnn_all.items() if k in ('weight', 'bias')}
    del _L0_gnn_all

    def _L1_gnn_setup():
        import jax, jax.numpy as jnp
        import numpy as np
        N = 6250
        E = 100000
        D = 128
        L = 4
        key = jax.random.key(seed)
        ks = jax.random.split(key, 8)
        in_feat = jax.random.normal(ks[0], (N, D), dtype=jnp.float32)
        src = jax.random.randint(ks[1], (E,), 0, N, dtype=jnp.int32)
        off = jax.random.randint(ks[2], (E,), 1, N, dtype=jnp.int32)
        dst = ((src + off) % N).astype(jnp.int32)
        s = 1.0 / np.sqrt(D)
        conv_w = jax.random.normal(ks[3], (L, D, D), dtype=jnp.float32) * s
        conv_b = jnp.zeros((L, D), dtype=jnp.float32)
        gate_w1 = jax.random.normal(ks[4], (D, D), dtype=jnp.float32) * s
        gate_w2 = jax.random.normal(ks[5], (D, D), dtype=jnp.float32) * s
        gate_b = jnp.zeros((D,), dtype=jnp.float32)
        return {'in_feat': in_feat, 'src': src, 'dst': dst, 'conv_w': conv_w, 'conv_b': conv_b, 'gate_w1': gate_w1, 'gate_w2': gate_w2, 'gate_b': gate_b}
    _L1_gnn_all = _L1_gnn_setup()
    _L1_gnn_in = {k: v for k, v in _L1_gnn_all.items() if k in ('conv_w', 'conv_b', 'gate_w1', 'gate_w2', 'gate_b')}
    del _L1_gnn_all
    return {'x': x, 'src': src, 'dst': dst, 'edge_type_4': edge_type_4, 'L0_gnn_weight': _L0_gnn_in['weight'], 'L0_gnn_bias': _L0_gnn_in['bias'], 'L1_gnn_conv_w': _L1_gnn_in['conv_w'], 'L1_gnn_conv_b': _L1_gnn_in['conv_b'], 'L1_gnn_gate_w1': _L1_gnn_in['gate_w1'], 'L1_gnn_gate_w2': _L1_gnn_in['gate_w2'], 'L1_gnn_gate_b': _L1_gnn_in['gate_b']}

def reference(x, src, dst, edge_type_4, L0_gnn_weight, L0_gnn_bias, L1_gnn_conv_w, L1_gnn_conv_b, L1_gnn_gate_w1, L1_gnn_gate_w2, L1_gnn_gate_b):
    import jax
    import jax.numpy as jnp

    def _L0_gnn_ref(x, weight, bias, src, dst, rel):
        import jax, jax.numpy as jnp
        import numpy as np
        N, E, IN, OUT = (6250, 100000, 128, 128)
        R = 5
        num_nodes = x.shape[0]
        num_edge_rels = weight.shape[0] - 1
        x_src = x[src]
        msg = jnp.zeros((src.shape[0], weight.shape[2]), x.dtype)
        for r in range(num_edge_rels):
            hr = x_src @ weight[r] + bias[r]
            msg = jnp.where((rel == r)[:, None], hr, msg)
        agg = jax.ops.segment_max(msg, dst, num_segments=num_nodes)
        deg = jax.ops.segment_sum(jnp.ones_like(dst, jnp.float32), dst, num_segments=num_nodes)
        agg = jnp.where((deg > 0)[:, None], agg, jnp.zeros((), x.dtype))
        h = x @ weight[-1] + bias[-1] + agg
        return h

    def _L1_gnn_ref(in_feat, src, dst, conv_w, conv_b, gate_w1, gate_w2, gate_b):
        import jax, jax.numpy as jnp
        import numpy as np
        N = 6250
        E = 100000
        D = 128
        L = 4
        n = in_feat.shape[0]
        loop = jnp.arange(n, dtype=src.dtype)
        s_idx = jnp.concatenate([src, loop])
        d_idx = jnp.concatenate([dst, loop])
        ones = jnp.ones(s_idx.shape[0], dtype=in_feat.dtype)
        out_deg = jax.ops.segment_sum(ones, s_idx, num_segments=n)
        in_deg = jax.ops.segment_sum(ones, d_idx, num_segments=n)
        inv_out = jax.lax.rsqrt(jnp.maximum(out_deg, 1.0))[:, None]
        inv_in = jax.lax.rsqrt(jnp.maximum(in_deg, 1.0))[:, None]
        x = in_feat
        for l in range(conv_w.shape[0]):
            h = x * inv_out
            agg = jax.ops.segment_sum(h[s_idx], d_idx, num_segments=n) * inv_in
            h = agg @ conv_w[l] + conv_b[l]
            h = jax.nn.leaky_relu(h, negative_slope=0.01)
            scale = jax.nn.sigmoid(x @ gate_w1.T + h @ gate_w2.T + gate_b)
            x = x * scale + h * (1.0 - scale)
        return x
    h = jnp.maximum(_layernorm(x, axis=-1), 0.0)
    x = x + _L0_gnn_ref(h, L0_gnn_weight, L0_gnn_bias, src, dst, edge_type_4)
    h = jnp.maximum(_layernorm(x, axis=-1), 0.0)
    x = x + _L1_gnn_ref(h, src, dst, L1_gnn_conv_w, L1_gnn_conv_b, L1_gnn_gate_w1, L1_gnn_gate_w2, L1_gnn_gate_b)
    return x

_drawn_inputs = setup_inputs


def setup_inputs(seed=0):
    import zlib

    import numpy as np

    out = dict(_drawn_inputs(seed))
    spreads = {'L1_gnn_conv_b': (0.0, 0.485), 'L1_gnn_gate_b': (0.0, 0.8)}
    factors = {'L1_gnn_gate_w1': 3.673, 'L1_gnn_gate_w2': 8.0}
    for name, (base, spread) in spreads.items():
        noise = np.random.default_rng([zlib.crc32(name.encode()), seed]).standard_normal(out[name].shape)
        drawn = base * np.exp(spread * noise) if base else spread * noise
        out[name] = jnp.asarray(drawn.astype(out[name].dtype))
    for name, factor in factors.items():
        out[name] = (out[name] * factor).astype(out[name].dtype)
    return out
```

```python
from contextlib import ExitStack

import concourse.bass as bass
from concourse import mybir

F32 = mybir.dt.float32
BF16 = mybir.dt.bfloat16
I32 = mybir.dt.int32
ALU = mybir.AluOpType
ACT = mybir.ActivationFunctionType

P = 128
N = 6250
E = 106250
D = 128
RELS = 4
LAYERS = 4
NODE_TILES = -(-N // P)
NPAD = NODE_TILES * P
LAST = N - (NODE_TILES - 1) * P
EDGE_TILES = -(-E // P)
EDGE_ROWS = EDGE_TILES + 1
BLK = 256
BLK_SHIFT = 8
BLOCKS = -(-N // BLK)
ACC_COLS = BLOCKS * BLK
VISITS = EDGE_TILES + BLOCKS - 1
GRP = 3
BODY = 15
GPB = BODY // GRP
RING = 3
ITERS = VISITS // BODY
GROUPS = VISITS // GRP
HALF = 9
VC = -(-(VISITS + BODY) // P)
VPAD = VC * P
PLANES = 5
CHUNK = 4
CHUNKS = -(-NODE_TILES // CHUNK)
ZERO_ROW = NPAD * RELS
HI = 64
BIG = 3.3895313892515355e38
EPS = 1e-5
SLOPE = 0.01
LAG0 = 2 * GRP
LAG1 = GRP
assert VISITS % BODY == 0 and VPAD >= VISITS + BODY


def chunk_tiles(c):
    return min(CHUNK, NODE_TILES - c * CHUNK)


def behind(g):
    return RING if g >= RING - 1 else GPB % RING


def build(nc, x, edges, w0, b0, conv_w, conv_b, gate_w1, gate_w2, gate_b, out):
    with ExitStack() as ctx:
        def sb(name, shape, dt):
            return ctx.enter_context(nc.sbuf_tensor(name, shape, dt))

        def sem(name):
            return ctx.enter_context(nc.semaphore(name))

        msg_table = nc.dram_tensor("msg_table", (ZERO_ROW + P, D), F32, kind="Internal").ap()
        node_table = nc.dram_tensor("node_table", (NPAD, D), F32, kind="Internal").ap()
        keep_dram = nc.dram_tensor("keep_dram", (VPAD, P), BF16, kind="Internal").ap()
        col_dram = nc.dram_tensor("col_dram", (VPAD, 1), I32, kind="Internal").ap()

        xres = sb("xres", [P, NODE_TILES, D], F32)
        xT = sb("xT", [P, NPAD], F32)
        acc = sb("acc", [P, ACC_COLS], F32)
        inv_out = sb("inv_out", [P, NPAD], F32)
        inv_in = sb("inv_in", [P, NPAD], F32)
        key_end = sb("key_end", [P, VPAD], F32)
        key_all = sb("key_all", [P, VPAD], F32)
        idx_msg = sb("idx_msg", [P, VPAD], I32)
        idx_src = sb("idx_src", [P, VPAD], I32)
        src_lo = sb("src_lo", [P, VPAD], BF16)
        src_hi = sb("src_hi", [P, VPAD], BF16)
        cols0 = sb("cols0", [1, ITERS + 1, 16], I32)
        cols1 = sb("cols1", [1, ITERS + 1, 16], I32)
        iota = sb("iota", [P, BLK], F32)
        iota_b = sb("iota_b", [P, P], BF16)
        ident = sb("ident", [P, P], F32)
        upper = sb("upper", [P, P], F32)
        ones = sb("ones", [P, P], F32)
        w0_sb = sb("w0_sb", [P, RELS + 1, D], F32)
        conv_sb = sb("conv_sb", [P, LAYERS, D], F32)
        g1T = sb("g1T", [P, D], F32)
        g2T = sb("g2T", [P, D], F32)
        bcols = sb("bcols", [P, LAYERS + 2], F32)
        brow = sb("brow", [P, RELS, D], F32)
        stats = sb("stats", [P, NODE_TILES, 6], F32)
        mv = sb("mv", [P, NODE_TILES, 2], F32)
        rstd = sb("rstd", [P, NODE_TILES], F32)
        nmr = sb("nmr", [P, NODE_TILES], F32)
        deg = sb("deg", [P, 2, HI], F32)
        idx_a = sb("idx_a", [P, HALF], I32)
        idx_b = sb("idx_b", [P, BODY - HALF], I32)
        ring = sb("ring", [P, BODY, D], F32)
        hot = sb("hot", [P, RING, GRP, BLK], F32)
        work = sb("work", [P, 11, CHUNK * P], F32)

        W3 = GRP * P
        scanned = inv_in[:, 0:RING * W3].rearrange("p (b w) -> p b w", b=RING)
        ends = inv_in[:, RING * W3:2 * RING * W3].rearrange("p (b g d) -> p b g d", b=RING, g=GRP)
        at = 2 * RING * W3
        keep_a = inv_in[:, at:at + HALF * P // 2].bitcast(BF16)
        keep_b = inv_in[:, at + HALF * P // 2:at + BODY * P // 2].bitcast(BF16)
        at += BODY * P // 2
        hlo = inv_in[:, at:at + RING * W3 // 2].bitcast(BF16).rearrange("p (b g k) -> p b g k", b=RING, g=GRP)
        at += RING * W3 // 2
        hhi = inv_in[:, at:at + RING * GRP * HI // 2].bitcast(BF16).rearrange("p (b g k) -> p b g k", b=RING, g=GRP)
        at += RING * GRP * HI // 2
        assert at <= NPAD

        bank = [ctx.enter_context(nc.psum_tensor(f"bank{i}", [P, 512], F32)) for i in range(8)]

        s_edges = sem("s_edges")
        s_gates = sem("s_gates")
        s_load = sem("s_load")
        s_const = sem("s_const")
        s_dve = sem("s_dve")
        s_pe = sem("s_pe")
        s_act = sem("s_act")
        s_rows = sem("s_rows")
        s_scr = sem("s_scr")
        s_cols = sem("s_cols")
        counts = {"dve": 0, "pe": 0, "act": 0}

        etab = inv_out[:, 0:VC * 2 * P].bitcast(I32).rearrange("p (c k e) -> p c k e", c=VC, k=2)
        big = inv_in[:, 0:VC * PLANES * P].bitcast(I32).rearrange("p (c k e) -> p c k e", c=VC, k=PLANES)
        f_a = acc[:, 0 * VPAD:1 * VPAD].rearrange("p (c e) -> p c e", c=VC)
        f_b = acc[:, 1 * VPAD:2 * VPAD].rearrange("p (c e) -> p c e", c=VC)
        f_c = acc[:, 2 * VPAD:3 * VPAD].rearrange("p (c e) -> p c e", c=VC)
        f_d = acc[:, 3 * VPAD:4 * VPAD].rearrange("p (c e) -> p c e", c=VC)
        f_e = acc[:, 4 * VPAD:5 * VPAD].rearrange("p (c e) -> p c e", c=VC)
        f_f = acc[:, 5 * VPAD:6 * VPAD].rearrange("p (c e) -> p c e", c=VC)
        cum = xT[:, 0:VPAD]
        dif = xT[:, VPAD:2 * VPAD]
        junk = xT[:, 2 * VPAD:3 * VPAD]
        iota_t = xT[:, 3 * VPAD:4 * VPAD]
        keep_bf = xT[:, 4 * VPAD:4 * VPAD + VPAD // 2].bitcast(BF16).rearrange("p (c e) -> p c e", c=VC)
        gload = xT[:, 5 * VPAD:5 * VPAD + 2 * D].rearrange("p (k d) -> p k d", k=2)
        small = xT[:, 6 * VPAD:6 * VPAD + 256]
        lo_i = hot[:, 0:2, :, :].rearrange("p a b c -> p (a b c)")[:, 0:VPAD].bitcast(I32).rearrange("p (c e) -> p c e", c=VC)
        hi_i = ring[:, :, :].rearrange("p a b -> p (a b)")[:, 0:VPAD].bitcast(I32).rearrange("p (c e) -> p c e", c=VC)
        fi = small[:, 0:14].bitcast(I32).rearrange("p (k c) -> p k c", k=2)
        first = small[:, 16:23]
        nvis = small[:, 24:31]
        fpn = small[:, 32:39]
        tcount = small[:, 40:47]
        djs = small[:, 48:55]
        valid = small[:, 56:63]
        jcol = small[:, 64:71]
        blkj = small[:, 72:79]
        bcol = small[:, 80:87]
        trow = small[:, 88:95].bitcast(I32)
        coli = small[:, 96:103].bitcast(I32)
        tclip = small[:, 104:111]
        setup_ready = sem("setup_ready")
        setup_pe = sem("setup_pe")
        setup_ev = sem("setup_ev")
        n_load_a = 2
        n_load_b = 13

        with nc.Block() as block:
            @block.sync
            def _(sp):
                sp.wait_ge(s_const, 1)
                full = EDGE_ROWS // P
                for k, plane in enumerate((0, 2)):
                    src = edges[0:full * P, plane * P:(plane + 1) * P].rearrange("(c p) e -> p c e", p=P)
                    sp.dma_start(etab[:, 0:full, k, :], src).then_inc(s_edges, 16)
                    sp.dma_start(etab[0:EDGE_ROWS - full * P, full, k, :],
                                 edges[full * P:EDGE_ROWS, plane * P:(plane + 1) * P]).then_inc(s_edges, 16)
                sp.dma_start(gload[:, 0, :], gate_w1).then_inc(s_gates, 16)
                sp.dma_start(gload[:, 1, :], gate_w2).then_inc(s_gates, 16)
                sp.dma_start(w0_sb[:, :, :], w0.rearrange("r i o -> i r o")).then_inc(s_load, 16)
                sp.dma_start(conv_sb[:, :, :], conv_w.rearrange("l i o -> i l o")).then_inc(s_load, 16)
                sp.dma_start(brow[:, :, :].rearrange("p r d -> p (r d)"),
                             b0[0:RELS, :].rearrange("r d -> (r d)").partition_broadcast(P)).then_inc(s_load, 16)
                with nc.allow_non_contiguous_dma(reason="six bias columns"):
                    for l in range(LAYERS):
                        sp.dma_start(bcols[:, l:l + 1], conv_b[l, :].unsqueeze(1)).then_inc(s_load, 16)
                    sp.dma_start(bcols[:, LAYERS:LAYERS + 1], gate_b.unsqueeze(1)).then_inc(s_load, 16)
                    sp.dma_start(bcols[:, LAYERS + 1:LAYERS + 2], b0[RELS, :].unsqueeze(1)).then_inc(s_load, 16)
                    sp.dma_start(xres[:, 0:NODE_TILES - 1, :],
                                 x[0:(NODE_TILES - 1) * P, :].rearrange("(t p) d -> p t d", p=P)).then_inc(s_load, 16)
                    sp.dma_start(xres[0:LAST, NODE_TILES - 1, :], x[(NODE_TILES - 1) * P:N, :]).then_inc(s_load, 16)
                    sp.wait_ge(setup_ready, 3)
                    sp.dma_start(col_dram.rearrange("(c p) o -> p (c o)", p=P), coli).then_inc(s_scr, 16)
                    sp.wait_ge(s_scr, 16)
                    flat = col_dram.rearrange("v o -> o v")
                    for dst, lag in ((cols0, LAG0), (cols1, LAG1)):
                        sp.dma_start(dst[0:1, 0, lag:BODY], flat[0:1, 0:BODY - lag]).then_inc(s_cols, 16)
                        sp.dma_start(dst[0:1, 1:ITERS + 1, 0:BODY],
                                     flat[0:1, BODY - lag:BODY - lag + ITERS * BODY].rearrange(
                                         "o (i s) -> o i s", s=BODY)).then_inc(s_cols, 16)
                sp.wait_ge(setup_ready, 4)
                sp.dma_start(keep_dram.rearrange("(c p) e -> p c e", p=P), keep_bf).then_inc(s_scr, 16)
                sp.wait_ge(s_cols, 64)
                sp.wait_ge(s_scr, 32)

            @block.gpsimd
            def _(pool):
                pool.memset(etab[:, VC - 1, :, :], N)
                pool.memset(xres[:, NODE_TILES - 1, :], 0.0)
                pool.memset(cols0[:, :, :], 0)
                pool.memset(cols1[:, :, :], 0).then_inc(s_const, 1)
                pool.iota(iota[:, :], [[1, BLK]], base=0, channel_multiplier=0,
                          allow_small_or_imprecise_dtypes=True)
                pool.iota(iota_b[:, :], [[1, P]], base=0, channel_multiplier=0,
                          allow_small_or_imprecise_dtypes=True)
                pool.iota(iota_t, [[1, VPAD]], base=0, channel_multiplier=0,
                          allow_small_or_imprecise_dtypes=True)
                pool.iota(jcol, [[P, VC]], base=0, channel_multiplier=1,
                          allow_small_or_imprecise_dtypes=True)
                pool.memset(ident[:, :], 0.0)
                pool.memset(upper[:, :], 1.0)
                pool.memset(ones[:, :], 1.0).then_inc(s_const, 1)
                pool.wait_ge(s_const, 2)
                pool.affine_select(out=ident[:, :], in_=ident[:, :], compare_op=ALU.not_equal, fill=1.0,
                                   base=0, pattern=[[-1, P]], channel_multiplier=1)
                pool.affine_select(out=upper[:, :], in_=upper[:, :], compare_op=ALU.is_ge, fill=0.0,
                                   base=0, pattern=[[1, P]], channel_multiplier=-1).then_inc(s_const, 1)
                pool.wait_ge(setup_ready, 2)
                for c in range(VC):
                    pool.indirect_dma_start(big[:, c, :, :].rearrange("p k e -> p (k e)"), None, edges,
                                            bass.IndirectOffsetOnAxis(ap=trow[:, c:c + 1], axis=0)
                                            ).then_inc(s_rows, 16)

            @block.vector
            def _(dve):
                chain = [0]

                def link(ins):
                    chain[0] += 1
                    ins.then_inc(s_dve, 1)
                    dve.wait_ge(s_dve, chain[0])

                dve.wait_ge(s_const, 3)
                dve.wait_ge(s_edges, 64)
                link(dve.tensor_scalar(fi[:, 0, :], etab[:, :, 1, 0], BLK_SHIFT, None, ALU.arith_shift_right))
                link(dve.tensor_scalar(fi[:, 1, :], etab[:, :, 1, P - 1], BLK_SHIFT, None, ALU.arith_shift_right))
                link(dve.tensor_copy(first, fi[:, 0, :]))
                link(dve.scalar_tensor_tensor(nvis, fi[:, 1, :], 1.0, first, ALU.add, ALU.subtract))
                link(dve.tensor_tensor(fpn, first, nvis, ALU.add))
                dve.tensor_copy(tclip, nvis).then_inc(setup_ready, 1)
                dve.wait_ge(setup_pe, 1)
                for h in range(2):
                    w = min(512, VPAD - 512 * h)
                    link(dve.tensor_copy(cum[:, 512 * h:512 * h + w], bank[h][:, 0:w]))
                    link(dve.tensor_tensor(dif[:, 512 * h:512 * h + w], bank[2 + h][:, 0:w],
                                           cum[:, 512 * h:512 * h + w], ALU.subtract))
                for c in range(VC):
                    link(dve.tensor_scalar(junk[:, 0:EDGE_TILES], cum[:, 0:EDGE_TILES], jcol[:, c:c + 1], 0.0,
                                           ALU.is_le, ALU.add, accum_out=tcount[:, c:c + 1]))
                link(dve.tensor_scalar(tclip, tcount, float(EDGE_TILES - 1), None, ALU.min))
                dve.tensor_copy(trow, tclip).then_inc(setup_ready, 1)
                for c in range(VC):
                    link(dve.scalar_tensor_tensor(junk[:, 0:EDGE_TILES], iota_t[:, 0:EDGE_TILES],
                                                  tcount[:, c:c + 1], dif[:, 0:EDGE_TILES],
                                                  ALU.is_equal, ALU.mult, accum_out=djs[:, c:c + 1]))
                link(dve.tensor_scalar(valid, tcount, float(EDGE_TILES), None, ALU.is_lt))
                link(dve.tensor_tensor(blkj, djs, jcol, ALU.add))
                link(dve.scalar_tensor_tensor(blkj, blkj, float(BLOCKS - 1), valid, ALU.subtract, ALU.mult))
                link(dve.tensor_scalar(blkj, blkj, float(BLOCKS - 1), float(BLK // P), ALU.add, ALU.mult))
                link(dve.tensor_scalar(bcol, blkj, float(P), 1.0, ALU.mult, ALU.subtract))
                dve.tensor_copy(coli, blkj).then_inc(setup_ready, 1)

                dve.wait_ge(s_rows, 16 * VC)
                src, rel, dst, before, after = (big[:, :, k, :] for k in range(PLANES))

                def wide(v):
                    return v.unsqueeze(2).to_broadcast([P, VC, P])

                link(dve.tensor_tensor(f_f, before, dst, ALU.is_equal))
                link(dve.tensor_scalar(f_f, f_f, 2.0, 1.0, ALU.mult, ALU.subtract))
                dve.tensor_scalar(keep_bf, f_f, BIG, None, ALU.mult).then_inc(setup_ready, 1)
                link(dve.scalar_tensor_tensor(f_a, src, float(RELS), rel, ALU.mult, ALU.add))
                link(dve.tensor_scalar(f_b, rel, 0.0, None, ALU.is_ge))
                link(dve.scalar_tensor_tensor(f_c, rel, float(RELS - 1), f_b, ALU.is_le, ALU.mult))
                link(dve.scalar_tensor_tensor(f_b, f_a, float(ZERO_ROW), f_c, ALU.subtract, ALU.mult))
                link(dve.tensor_scalar(f_a, f_b, float(ZERO_ROW), None, ALU.add))
                link(dve.tensor_copy(f_b, src))
                link(dve.tensor_tensor(f_c, dst, wide(bcol), ALU.subtract))
                link(dve.tensor_tensor(f_d, f_c, wide(valid), ALU.mult))
                link(dve.tensor_tensor(f_c, after, dst, ALU.not_equal))
                link(dve.tensor_tensor(f_e, f_c, f_d, ALU.mult))
                link(dve.tensor_scalar(f_c, f_e, 1.0, None, ALU.subtract))
                link(dve.tensor_scalar(f_e, f_d, 1.0, None, ALU.subtract))
                link(dve.tensor_scalar(lo_i, etab[:, :, 0, :], P - 1, None, ALU.bitwise_and))
                link(dve.tensor_scalar(hi_i, etab[:, :, 0, :], 7, None, ALU.arith_shift_right))
                link(dve.tensor_scalar(f_f, lo_i, 1.0, None, ALU.add))
                link(dve.scalar_tensor_tensor(f_d, etab[:, :, 1, :], float(N), f_f, ALU.is_lt, ALU.mult))
                link(dve.tensor_scalar(f_f, f_d, 1.0, None, ALU.subtract))
                link(dve.tensor_copy(f_d, hi_i))
                dve.tensor_copy(tclip, tcount).then_inc(setup_ready, 1)
                for c in range(VC):
                    b = 4 * (c % 2)
                    dve.wait_ge(setup_pe, 3 * c + 2)
                    sl = slice(c * P, (c + 1) * P)
                    dve.tensor_copy(idx_msg[:, sl], bank[b][:, 0:P])
                    dve.tensor_copy(idx_src[:, sl], bank[b][:, P:2 * P]).then_inc(setup_ev, 1)
                    dve.wait_ge(setup_pe, 3 * c + 3)
                    dve.tensor_copy(key_end[:, sl], bank[b + 1][:, 0:P])
                    dve.tensor_copy(key_all[:, sl], bank[b + 1][:, P:2 * P]).then_inc(setup_ev, 1)
                    dve.wait_ge(setup_pe, 3 * c + 4)
                    dve.tensor_copy(src_lo[:, sl], bank[b + 2][:, 0:P])
                    dve.tensor_copy(src_hi[:, sl], bank[b + 2][:, P:2 * P]).then_inc(setup_ev, 1)
                dve.wait_ge(setup_pe, 3 * VC + 2)
                dve.tensor_copy(g1T[:, :], bank[7][:, 0:P])
                dve.tensor_copy(g2T[:, :], bank[7][:, P:2 * P])

            @block.tensor
            def _(pe):
                pe.wait_ge(s_const, 3)
                pe.wait_ge(setup_ready, 1)
                for c in range(VC):
                    h, o = c // 4, (c % 4) * P
                    for k in range(c + 1):
                        pe.matmul(bank[h][:, o:o + P], nvis[:, k:k + 1].to_broadcast([P, P]),
                                  upper[:, :] if k == c else ones[:, :], start=(k == 0), stop=(k == c))
                    mm = pe.matmul(bank[2 + h][:, o:o + P], fpn[:, c:c + 1].to_broadcast([P, P]), ident[:, :],
                                   start=True, stop=True)
                mm.then_inc(setup_pe, 1)
                pe.wait_ge(setup_ready, 5)
                for c in range(VC):
                    for k, (a, b) in enumerate(((f_a, f_b), (f_c, f_e), (f_f, f_d))):
                        if c >= 2:
                            pe.wait_ge(setup_ev, 3 * (c - 2) + k + 1)
                        t = bank[4 * (c % 2) + k]
                        pe.transpose(t[:, 0:P], a[:, c, :], ident[:, :])
                        pe.transpose(t[:, P:2 * P], b[:, c, :], ident[:, :]).then_inc(setup_pe, 1)
                pe.wait_ge(s_gates, 32)
                pe.transpose(bank[7][:, 0:P], gload[:, 0, :], ident[:, :])
                pe.transpose(bank[7][:, P:2 * P], gload[:, 1, :], ident[:, :]).then_inc(setup_pe, 1)

        ln_stat = sem("ln_stat")
        ln_tiles = sem("ln_tiles")
        ln_rows = sem("ln_rows")
        ln_t = sem("ln_t")
        ln_ev = sem("ln_ev")
        rows = [work[:, 0, :].rearrange("p (t d) -> p t d", t=CHUNK),
                work[:, 1, :].rearrange("p (t d) -> p t d", t=CHUNK)]

        def ln_dve_stats(dve, use, each):
            base = use * 5
            for t in range(NODE_TILES):
                each(t)
                dve.bn_stats(stats[:, t, :], xres[:, t, :]).then_inc(ln_tiles, 1)
            dve.wait_ge(ln_tiles, (use + 1) * NODE_TILES)
            for t in range(NODE_TILES):
                last = dve.bn_aggr(mv[:, t, :], stats[:, t, :])
            last.then_inc(ln_stat, 1)
            dve.wait_ge(ln_stat, base + 1)
            dve.tensor_scalar(rstd[:, :], mv[:, :, 1], EPS, None, ALU.add).then_inc(ln_stat, 1)
            dve.wait_ge(ln_stat, base + 3)
            dve.reciprocal(rstd[:, :], rstd[:, :]).then_inc(ln_stat, 1)
            dve.wait_ge(ln_stat, base + 4)
            dve.scalar_tensor_tensor(nmr[:, :], mv[:, :, 0], -1.0, rstd[:, :], ALU.mult, ALU.mult
                                     ).then_inc(ln_stat, 1)

        def ln_act(act, use):
            base = use * 5
            act.wait_ge(ln_stat, base + 2)
            act.activation(rstd[:, :], rstd[:, :], ACT.Sqrt).then_inc(ln_stat, 1)
            act.wait_ge(ln_stat, base + 5)

        def ln_act_rows(act, use, c):
            if c >= 2:
                act.wait_ge(ln_t, use * CHUNKS + c - 1)
            for k in range(chunk_tiles(c)):
                t = c * CHUNK + k
                last = act.activation(rows[c % 2][:, k, :], xres[:, t, :], ACT.Relu,
                                      bias=nmr[:, t:t + 1], scale=rstd[:, t:t + 1])
            last.then_inc(ln_rows, 1)

        def ln_pe(pe, use, c):
            pe.wait_ge(ln_rows, use * CHUNKS + c + 1)
            if c >= 2:
                pe.wait_ge(ln_ev, use * CHUNKS + c - 1)
            for k in range(chunk_tiles(c)):
                mm = pe.transpose(bank[c % 2][:, k * P:(k + 1) * P], rows[c % 2][:, k, :], ident[:, :])
            mm.then_inc(ln_t, 1)

        def ln_dve_cols(dve, use, c):
            dve.wait_ge(ln_t, use * CHUNKS + c + 1)
            w = chunk_tiles(c) * P
            dve.tensor_copy(xT[:, c * CHUNK * P:c * CHUNK * P + w], bank[c % 2][:, 0:w]).then_inc(ln_ev, 1)

        tab_mm = sem("tab_mm")
        tab_ev = sem("tab_ev")
        tab_out = [sem(f"tab_out{k}") for k in range(4)]
        zero_out = sem("zero_out")
        self_mm = sem("self_mm")
        self_ev = sem("self_ev")
        with nc.Block() as block:
            @block.sync
            def _(sp):
                sp.wait_ge(s_load, 16 * 11)
                for t in range(NODE_TILES):
                    sp.wait_ge(tab_ev, t + 1)
                    sp.dma_start(msg_table[t * P * RELS:(t + 1) * P * RELS, :].rearrange("(p r) d -> p (r d)", r=RELS),
                                 work[:, 2 + t % 4, :]).then_inc(tab_out[t % 4], 16)
                sp.wait_ge(tab_ev, NODE_TILES + 1)
                sp.dma_start(msg_table[ZERO_ROW:ZERO_ROW + P, :], work[:, 6, 0:D]).then_inc(zero_out, 16)
                sp.wait_ge(zero_out, 16)
                for k in range(4):
                    sp.wait_ge(tab_out[k], 16 * len(range(k, NODE_TILES, 4)))

            @block.vector
            def _(dve):
                dve.wait_ge(s_load, 16 * 11)
                dve.memset(acc[:, NPAD:ACC_COLS], 0.0)
                ln_dve_stats(dve, 0, lambda t: None)

                def table(c):
                    for k in range(chunk_tiles(c)):
                        t = c * CHUNK + k
                        dve.wait_ge(tab_mm, t + 1)
                        if t >= 4:
                            dve.wait_ge(tab_out[t % 4], 16 * (t // 4))
                        dve.tensor_tensor(work[:, 2 + t % 4, :], bank[2 + t % 2][:, :],
                                          brow[:, :, :].rearrange("p r d -> p (r d)"), ALU.add).then_inc(tab_ev, 1)

                for c in range(CHUNKS):
                    ln_dve_cols(dve, 0, c)
                    if c:
                        table(c - 1)
                table(CHUNKS - 1)
                dve.memset(work[:, 6, 0:D], 0.0).then_inc(tab_ev, 1)

            @block.scalar
            def _(act):
                def self_term(c):
                    w = chunk_tiles(c) * P
                    act.wait_ge(self_mm, c + 1)
                    act.activation(acc[:, c * CHUNK * P:c * CHUNK * P + w], bank[4 + c % 2][:, 0:w], ACT.Identity,
                                   bias=bcols[:, LAYERS + 1:LAYERS + 2]).then_inc(self_ev, 1)

                ln_act(act, 0)
                for c in range(CHUNKS):
                    ln_act_rows(act, 0, c)
                    if c >= 2:
                        self_term(c - 2)
                self_term(CHUNKS - 2)
                self_term(CHUNKS - 1)

            @block.tensor
            def _(pe):
                def products(c):
                    pe.wait_ge(ln_ev, c + 1)
                    if c >= 2:
                        pe.wait_ge(self_ev, c - 1)
                    w = chunk_tiles(c) * P
                    pe.matmul(bank[4 + c % 2][:, 0:w], w0_sb[:, RELS, :], xT[:, c * CHUNK * P:c * CHUNK * P + w],
                              start=True, stop=True).then_inc(self_mm, 1)
                    for k in range(chunk_tiles(c)):
                        t = c * CHUNK + k
                        if t >= 2:
                            pe.wait_ge(tab_ev, t - 1)
                        pe.matmul(bank[2 + t % 2][:, :], xT[:, t * P:(t + 1) * P],
                                  w0_sb[:, 0:RELS, :].rearrange("p r d -> p (r d)"),
                                  start=True, stop=True).then_inc(tab_mm, 1)

                for c in range(CHUNKS):
                    ln_pe(pe, 0, c)
                    if c:
                        products(c - 1)
                products(CHUNKS - 1)

        landed = [sem(f"landed{s}") for s in range(BODY)]
        idx_ready_a = sem("idx_ready_a")
        bodies = sem("bodies")
        idx_ready_b = sem("idx_ready_b")
        keep_ready_a = sem("keep_ready_a")
        keep_ready_b = sem("keep_ready_b")
        turned = sem("turned")
        scan_done = sem("scan_done")
        back = sem("back")
        ends_ready = sem("ends_ready")
        hot_ready = sem("hot_ready")
        hist_ready = sem("hist_ready")
        hist_done = sem("hist_done")
        part_ready = sem("part_ready")
        added = sem("added")
        mz = sem("mz")

        def gathers(pool, i, use, table):
            pool.wait_ge(idx_ready_a, i + (1 + use * (ITERS + 1)))
            pool.sem_inc(bodies, 1)
            for s in range(HALF):
                pool.indirect_dma_start(ring[:, s, :], None, table,
                                        bass.IndirectOffsetOnAxis(ap=idx_a[:, s:s + 1], axis=0)
                                        ).then_inc(landed[s], 16)
            pool.wait_ge(idx_ready_b, i + (1 + use * (ITERS + 1)))
            pool.sem_inc(bodies, 1)
            for s in range(HALF, BODY):
                pool.indirect_dma_start(ring[:, s, :], None, table,
                                        bass.IndirectOffsetOnAxis(ap=idx_b[:, s - HALF:s - HALF + 1], axis=0)
                                        ).then_inc(landed[s], 16)

        def copy_idx_a(act, i, idx):
            act.activation(idx_a[:, :], idx[:, bass.ds(i * BODY, HALF)], ACT.Copy).then_inc(idx_ready_a, 1)

        def copy_idx_b(act, i, idx):
            act.activation(idx_b[:, :], idx[:, bass.ds(i * BODY + HALF, BODY - HALF)], ACT.Copy).then_inc(idx_ready_b, 1)

        def add_visits(dve, first_visit, s0, base, degrees=False):
            for s in range(GRP):
                n = first_visit + s
                tile = dve.snap(dve_regs[s0 + s], min_val=0, max_val=(ACC_COLS - BLK) // P)
                dve.wait_ge(part_ready, n + (base + 1))
                if not (isinstance(n, int) and n + base == 0):
                    dve.wait_ge(added, n + base)
                dst = acc[:, bass.ds(tile * P, BLK)]
                if degrees:
                    cnt = deg[:, 1, bass.ds(tile, BLK // P)]
                    dve.tensor_tensor(cnt, cnt, bank[s][:, 0:BLK // P], ALU.add)
                dve.tensor_tensor(dst, dst, part[s][:, 0:BLK], ALU.add).then_inc(added, 1)

        part = [bank[4], bank[5], bank[6]]
        hist = bank[7]
        def load_cols(dve, cols, i):
            dve.load(dve_regs, cols[0:1, bass.ds(i, 1), 0:BODY].rearrange("o a b -> o (a b)"))

        def build_hot(dve, keys, q, g):
            dve.tensor_tensor(hot[:, g % RING, :, :], iota[:, :].unsqueeze(1).to_broadcast([P, GRP, BLK]),
                              keys[:, bass.ds(q * GRP, GRP)].unsqueeze(2).to_broadcast([P, GRP, BLK]),
                              ALU.is_equal).then_inc(hot_ready, 1)

        dve_regs = [nc.vector.alloc_register(f"visit_col{s}") for s in range(BODY)]

        with nc.Block() as block:
            @block.sync
            def _(sp):
                def load_keep(i, lo, hi, dst, done):
                    v = keep_dram[bass.ds(i * BODY + lo, hi - lo), :].rearrange("v e -> (v e)")
                    sp.dma_start(dst, v.partition_broadcast(P)).then_inc(done, 16)

                load_keep(0, 0, HALF, keep_a, keep_ready_a)
                load_keep(0, HALF, BODY, keep_b, keep_ready_b)
                with sp.Fori(1, ITERS) as i:
                    sp.wait_ge(scan_done, i * GPB - 2)
                    load_keep(i, 0, HALF, keep_a, keep_ready_a)
                    sp.wait_ge(scan_done, i * GPB)
                    load_keep(i, HALF, BODY, keep_b, keep_ready_b)

            @block.gpsimd
            def _(pool):
                with pool.Fori(0, ITERS) as i:
                    gathers(pool, i, 0, msg_table)

            @block.scalar
            def _(act):
                def body(i, first):
                    for g in range(GPB):
                        q = i * GPB + g
                        act.wait_ge(back, q + 1)
                        if not (first and g < RING):
                            act.wait_ge(part_ready, q * GRP - GRP * (behind(g) - 1))
                        act.activation(ends[:, g % RING, :, :], bank[3][:, 0:GRP * P].rearrange("p (g d) -> p g d", g=GRP),
                                       ACT.Copy).then_inc(ends_ready, 1)
                        if g == 2:
                            copy_idx_a(act, i + 1, idx_msg)
                        if g == 4:
                            copy_idx_b(act, i + 1, idx_msg)

                copy_idx_a(act, 0, idx_msg)
                copy_idx_b(act, 0, idx_msg)
                body(0, True)
                with act.Fori(1, ITERS) as i:
                    body(i, False)

            @block.tensor
            def _(pe):
                def turn(i, g, first):
                    q = i * GPB + g
                    for s in range(GRP * g, GRP * g + GRP):
                        pe.wait_ge(landed[s], 16 * i + 16)
                    if not (first and g < RING):
                        pe.wait_ge(scan_done, q - (behind(g) - 1))
                    for k in range(GRP):
                        mm = pe.transpose(bank[g % RING][:, k * P:(k + 1) * P], ring[:, GRP * g + k, :], ident[:, :])
                    mm.then_inc(turned, 1)

                def turn_back(q, g, first, last=False):
                    pe.wait_ge(scan_done, q + 1)
                    if not first:
                        pe.wait_ge(ends_ready, q)
                    for k in range(GRP):
                        mm = pe.transpose(bank[3][:, k * P:(k + 1) * P], scanned[:, g % RING, k * P:(k + 1) * P],
                                          ident[:, :])
                    mm.then_inc(back, 1)
                    pe.wait_ge(hist_ready, q + 1)
                    for k in range(GRP):
                        mm = pe.matmul(hist[:, 0:HI], hlo[:, g % RING, k, :], hhi[:, g % RING, k, :],
                                       start=False, stop=(last and k == GRP - 1), skip_group_check=True)
                    mm.then_inc(hist_done, 1)

                def sums(q, g, first):
                    pe.wait_ge(ends_ready, q + 1)
                    pe.wait_ge(hot_ready, q + 1)
                    for k in range(GRP):
                        if not first:
                            pe.wait_ge(added, GRP * q + k - (GRP - 1))
                        pe.matmul(part[k][:, 0:BLK], ends[:, g % RING, k, :], hot[:, g % RING, k, :],
                                  start=True, stop=True).then_inc(part_ready, 1)

                def body(i, first):
                    for g in range(GPB):
                        q = i * GPB + g
                        turn(i, g, first)
                        if not (first and g < 1):
                            turn_back(q - 1, (g - 1) % GPB, first and g == 1)
                        if not (first and g < 2):
                            sums(q - 2, (g - 2) % GPB, first and g == 2)

                pe.wait_ge(mz, 2)
                pe.matmul(hist[:, 0:HI], hlo[:, 0, 0, :], hhi[:, 0, 0, :], start=True, stop=False,
                          skip_group_check=True).then_inc(mz, 1)
                body(0, True)
                with pe.Fori(1, ITERS) as i:
                    body(i, False)
                turn_back(GROUPS - 1, GPB - 1, False, True)
                sums(GROUPS - 2, GPB - 2, False)
                sums(GROUPS - 1, GPB - 1, False)

            @block.vector
            def _(dve):
                def body(i, first):
                    load_cols(dve, cols0, i)
                    for g in range(GPB):
                        q = i * GPB + g
                        dve.wait_ge(turned, q + 1)
                        if g in (0, HALF // GRP):
                            dve.wait_ge(keep_ready_b if g else keep_ready_a, i * 16 + 16)
                        if not (first and g == 0):
                            dve.wait_ge(scan_done, q)
                        if not (first and g < RING):
                            dve.wait_ge(back, q - (behind(g) - 1))
                        keep = keep_a[:, GRP * g * P:GRP * (g + 1) * P] if GRP * g < HALF else \
                            keep_b[:, (GRP * g - HALF) * P:(GRP * (g + 1) - HALF) * P]
                        carry = -BIG if first and g == 0 else \
                            scanned[:, (g - 1) % GPB % RING, W3 - 1:W3]
                        dve.tensor_tensor_scan(scanned[:, g % RING, :], keep, bank[g % RING][:, 0:W3], carry,
                                               ALU.min, ALU.max).then_inc(scan_done, 1)
                        if not (first and g < RING):
                            dve.wait_ge(part_ready, q * GRP - GRP * (behind(g) - 1))
                        build_hot(dve, key_end, q, g)
                        if first and g == 0:
                            dve.wait_ge(mz, 3)
                        if not (first and g < RING):
                            dve.wait_ge(hist_done, q - (behind(g) - 1))
                        dve.tensor_tensor(hlo[:, g % RING, :, :], iota_b[:, :].unsqueeze(1).to_broadcast([P, GRP, P]),
                                          src_lo[:, bass.ds(q * GRP, GRP)].unsqueeze(2).to_broadcast([P, GRP, P]),
                                          ALU.is_equal)
                        dve.tensor_tensor(hhi[:, g % RING, :, :], iota_b[:, 0:HI].unsqueeze(1).to_broadcast([P, GRP, HI]),
                                          src_hi[:, bass.ds(q * GRP, GRP)].unsqueeze(2).to_broadcast([P, GRP, HI]),
                                          ALU.is_equal).then_inc(hist_ready, 1)
                        if not (first and g < 2):
                            add_visits(dve, (q - 2) * GRP, GRP * g, 0)

                dve.memset(hlo[:, 0, 0, :], 0.0).then_inc(mz, 1)
                dve.memset(hhi[:, 0, 0, :], 0.0).then_inc(mz, 1)
                body(0, True)
                with dve.Fori(1, ITERS) as i:
                    body(i, False)
                load_cols(dve, cols0, ITERS)
                add_visits(dve, (GROUPS - 2) * GRP, 0, 0)
                add_visits(dve, (GROUPS - 1) * GRP, GRP, 0)
                dve.wait_ge(hist_done, GROUPS)
                dve.tensor_copy(deg[:, 0, :], hist[:, 0:HI])

        inv_step = sem("inv_step")
        inv_diag = sem("inv_diag")
        inv_mm = sem("inv_mm")
        inv_ev = sem("inv_ev")

        def inv_block(which, dst):
            d = deg[:, which, :]
            base, cb = 3 * which, CHUNKS * which
            with nc.Block() as block:
                @block.vector
                def _(dve):
                    dve.tensor_scalar(d, d, 1.0, 1.0, ALU.add, ALU.max).then_inc(inv_step, 1)
                    dve.wait_ge(inv_step, base + 2)
                    dve.reciprocal(d, d).then_inc(inv_step, 1)
                    dve.wait_ge(inv_step, base + 3)
                    for c in range(CHUNKS):
                        k = chunk_tiles(c)
                        if c >= 2:
                            dve.wait_ge(inv_mm, cb + c - 1)
                        dve.tensor_tensor(rows[c % 2][:, 0:k, :], ident[:, :].unsqueeze(1).to_broadcast([P, k, P]),
                                          d[:, c * CHUNK:c * CHUNK + k].unsqueeze(2).to_broadcast([P, k, P]),
                                          ALU.mult).then_inc(inv_diag, 1)

                @block.scalar
                def _(act):
                    act.wait_ge(inv_step, base + 1)
                    act.activation(d, d, ACT.Sqrt).then_inc(inv_step, 1)
                    for c in range(CHUNKS):
                        w = chunk_tiles(c) * P
                        act.wait_ge(inv_mm, cb + c + 1)
                        act.activation(dst[:, c * CHUNK * P:c * CHUNK * P + w], bank[c % 2][:, 0:w],
                                       ACT.Copy).then_inc(inv_ev, 1)

                @block.tensor
                def _(pe):
                    for c in range(CHUNKS):
                        w = chunk_tiles(c) * P
                        pe.wait_ge(inv_diag, cb + c + 1)
                        if c >= 2:
                            pe.wait_ge(inv_ev, cb + c - 1)
                        pe.matmul(bank[c % 2][:, 0:w], ones[:, :],
                                  rows[c % 2].rearrange("p t d -> p (t d)")[:, 0:w], start=True, stop=True
                                  ).then_inc(inv_mm, 1)

        inv_block(0, inv_out)

        res_t = sem("res_t")
        res_add = sem("res_add")
        with nc.Block() as block:
            @block.tensor
            def _(pe):
                for c in range(CHUNKS):
                    if c >= 2:
                        pe.wait_ge(res_add, c - 1)
                    for k in range(chunk_tiles(c)):
                        t = c * CHUNK + k
                        mm = pe.transpose(bank[4 + c % 2][:, k * P:(k + 1) * P], acc[:, t * P:(t + 1) * P], ident[:, :])
                    mm.then_inc(res_t, 1)
                for c in range(CHUNKS):
                    ln_pe(pe, 1, c)

            @block.vector
            def _(dve):
                def residual(t):
                    c = t // CHUNK
                    if t % CHUNK == 0:
                        k = chunk_tiles(c)
                        dve.wait_ge(res_t, c + 1)
                        xc = xres[:, t:t + k, :].rearrange("p t d -> p (t d)")
                        dve.tensor_tensor(xc, xc, bank[4 + c % 2][:, 0:k * P], ALU.add).then_inc(res_add, 1)
                        dve.wait_ge(res_add, c + 1)

                ln_dve_stats(dve, 1, residual)
                for c in range(CHUNKS):
                    ln_dve_cols(dve, 1, c)

            @block.scalar
            def _(act):
                ln_act(act, 1)
                for c in range(CHUNKS):
                    ln_act_rows(act, 1, c)

        scaled = sem("scaled")
        tab_t = sem("tab_t")
        row_ev = sem("row_ev")
        row_out = [sem(f"row_out{k}") for k in range(2)]
        row_stage = [work[:, 9, :], work[:, 10, :]]

        def cols(c):
            return slice(c * CHUNK * P, c * CHUNK * P + chunk_tiles(c) * P)

        def stores_before(use, c):
            return use * len(range(c % 2, CHUNKS, 2)) + c // 2

        def pub_scale(pool, c):
            pool.tensor_tensor(acc[:, cols(c)], xT[:, cols(c)], inv_out[:, cols(c)], ALU.mult).then_inc(scaled, 1)

        def pub_turn(pe, use, c, src):
            if use * CHUNKS + c >= 2:
                pe.wait_ge(row_ev, use * CHUNKS + c - 1)
            for k in range(chunk_tiles(c)):
                t = c * CHUNK + k
                mm = pe.transpose(bank[4 + c % 2][:, k * P:(k + 1) * P], src[:, t * P:(t + 1) * P], ident[:, :])
            mm.then_inc(tab_t, 1)

        def pub_rows(act, use, c):
            n = use * CHUNKS + c
            act.wait_ge(tab_t, n + 1)
            if stores_before(use, c):
                act.wait_ge(row_out[c % 2], 16 * stores_before(use, c))
            act.activation(row_stage[c % 2][:, 0:chunk_tiles(c) * P], bank[4 + c % 2][:, 0:chunk_tiles(c) * P],
                           ACT.Copy).then_inc(row_ev, 1)

        def pub_store(sp, use, c):
            k = chunk_tiles(c)
            sp.wait_ge(row_ev, use * CHUNKS + c + 1)
            sp.dma_start(node_table[c * CHUNK * P:(c * CHUNK + k) * P, :].rearrange("(t p) d -> p t d", p=P),
                         row_stage[c % 2][:, 0:k * P].rearrange("p (t d) -> p t d", t=k)).then_inc(row_out[c % 2], 16)

        with nc.Block() as block:
            @block.gpsimd
            def _(pool):
                pool.memset(deg[:, 1, :], 0.0)
                for c in range(CHUNKS):
                    pub_scale(pool, c)

            @block.tensor
            def _(pe):
                for c in range(CHUNKS):
                    pe.wait_ge(scaled, c + 1)
                    pub_turn(pe, 0, c, acc)

            @block.scalar
            def _(act):
                for c in range(CHUNKS):
                    pub_rows(act, 0, c)

            @block.sync
            def _(sp):
                for c in range(CHUNKS):
                    pub_store(sp, 0, c)
                for k in range(2):
                    sp.wait_ge(row_out[k], 16 * stores_before(1, k))

        def aggregate(layer):
            use = layer + 1
            vbase, gbase, lbase = use * VISITS, use * GROUPS, use * ITERS * 16
            degrees = layer == 0
            with nc.Block() as block:
                @block.gpsimd
                def _(pool):
                    with pool.Fori(0, ITERS) as i:
                        gathers(pool, i, use, node_table)

                @block.scalar
                def _(act):
                    copy_idx_a(act, 0, idx_src)
                    copy_idx_b(act, 0, idx_src)
                    with act.Fori(0, ITERS) as i:
                        act.wait_ge(part_ready, i * BODY + (vbase + HALF))
                        copy_idx_a(act, i + 1, idx_src)
                        act.wait_ge(part_ready, i * BODY + (vbase + BODY))
                        copy_idx_b(act, i + 1, idx_src)

                @block.tensor
                def _(pe):
                    with pe.Fori(0, ITERS) as i:
                        for g in range(GPB):
                            pe.wait_ge(hot_ready, i * GPB + (g + 1 + gbase))
                            for k in range(GRP):
                                s = GRP * g + k
                                pe.wait_ge(landed[s], i * 16 + (16 + lbase))
                                pe.wait_ge(added, i * BODY + (s + 1 - GRP + vbase))
                                if degrees:
                                    for h in range(BLK // P):
                                        pe.matmul(bank[k][:, h:h + 1],
                                                  hot[:, g % RING, k, h * P:(h + 1) * P], ones[:, 0:1],
                                                  start=True, stop=True)
                                pe.matmul(part[k][:, 0:BLK], ring[:, s, :], hot[:, g % RING, k, :],
                                          start=True, stop=True).then_inc(part_ready, 1)

                @block.vector
                def _(dve):
                    def body(i, first):
                        load_cols(dve, cols1, i)
                        for g in range(GPB):
                            q = i * GPB + g
                            if not (first and g < RING):
                                dve.wait_ge(part_ready, q * GRP + (vbase - GRP * (behind(g) - 1)))
                            build_hot(dve, key_all, q, g)
                            if not (first and g < 1):
                                add_visits(dve, q * GRP - GRP, GRP * g, vbase, degrees)

                    body(0, True)
                    with dve.Fori(1, ITERS) as i:
                        body(i, False)
                    load_cols(dve, cols1, ITERS)
                    add_visits(dve, (GROUPS - 1) * GRP, 0, vbase, degrees)

        norm_in = sem("norm_in")
        conv_mm = sem("conv_mm")
        conv_ev = sem("conv_ev")
        leaky = sem("leaky")
        less = sem("less")
        gate_mm = sem("gate_mm")
        gate_ev = sem("gate_ev")
        mixed = sem("mixed")
        state = sem("state")
        out_ev = sem("out_ev")
        final = [sem(f"final{k}") for k in range(2)]

        def update(layer):
            last = layer == LAYERS - 1
            b = layer * CHUNKS
            agg = [work[:, k, :] for k in range(3)]
            hid = [work[:, 3 + k, :] for k in range(2)]
            sca = [work[:, 5 + k, :] for k in range(2)]
            mix = [work[:, 7 + k, :] for k in range(2)]

            def wd(c):
                return chunk_tiles(c) * P

            with nc.Block() as block:
                @block.gpsimd
                def _(pool):
                    for c in range(CHUNKS + 3):
                        if c < CHUNKS:
                            if c >= 3:
                                pool.wait_ge(conv_mm, b + c - 2)
                            pool.tensor_tensor(agg[c % 3][:, 0:wd(c)], acc[:, cols(c)], inv_in[:, cols(c)],
                                               ALU.mult).then_inc(norm_in, 1)
                        if c >= 3 and not last:
                            pool.wait_ge(state, b + c - 2)
                            pool.wait_ge(norm_in, b + c - 2)
                            pub_scale(pool, c - 3)

                @block.tensor
                def _(pe):
                    def conv(c):
                        pe.wait_ge(norm_in, b + c + 1)
                        if b + c >= 2:
                            pe.wait_ge(conv_ev, b + c - 1)
                        pe.matmul(bank[c % 2][:, 0:wd(c)], conv_sb[:, layer, :], agg[c % 3][:, 0:wd(c)],
                                  start=True, stop=True).then_inc(conv_mm, 1)

                    def gate(c):
                        if b + c >= 2:
                            pe.wait_ge(gate_ev, b + c - 1)
                        pe.matmul(bank[2 + c % 2][:, 0:wd(c)], g1T[:, :], xT[:, cols(c)], start=True, stop=False)
                        pe.wait_ge(leaky, b + c + 1)
                        pe.matmul(bank[2 + c % 2][:, 0:wd(c)], g2T[:, :], hid[c % 2][:, 0:wd(c)],
                                  start=False, stop=True).then_inc(gate_mm, 1)

                    def turn(c):
                        if last:
                            pe.wait_ge(state, b + c + 1)
                            if c >= 2:
                                pe.wait_ge(out_ev, c - 1)
                            for k in range(chunk_tiles(c)):
                                t = c * CHUNK + k
                                mm = pe.transpose(bank[4 + c % 2][:, k * P:(k + 1) * P], xT[:, t * P:(t + 1) * P],
                                                  ident[:, :])
                            mm.then_inc(tab_t, 1)
                        else:
                            pe.wait_ge(scaled, b + CHUNKS + c + 1)
                            pub_turn(pe, layer + 1, c, acc)

                    for c in range(CHUNKS + 4):
                        if c < CHUNKS:
                            conv(c)
                        if 1 <= c <= CHUNKS:
                            gate(c - 1)
                        if c >= 4:
                            turn(c - 4)

                @block.scalar
                def _(act):
                    for c in range(CHUNKS + 5):
                        if c < CHUNKS:
                            act.wait_ge(conv_mm, b + c + 1)
                            if b + c >= 2:
                                act.wait_ge(state, b + c - 1)
                            act.activation(hid[c % 2][:, 0:wd(c)], bank[c % 2][:, 0:wd(c)], ACT.Identity,
                                           bias=bcols[:, layer:layer + 1]).then_inc(conv_ev, 1)
                        if 1 <= c <= CHUNKS:
                            act.wait_ge(gate_mm, b + c)
                            if b + c >= 3:
                                act.wait_ge(mixed, b + c - 2)
                            act.activation(sca[(c - 1) % 2][:, 0:wd(c - 1)], bank[2 + (c - 1) % 2][:, 0:wd(c - 1)],
                                           ACT.Sigmoid, bias=bcols[:, LAYERS:LAYERS + 1]).then_inc(gate_ev, 1)
                        if c >= 5 and not last:
                            pub_rows(act, layer + 1, c - 5)

                @block.vector
                def _(dve):
                    for c in range(CHUNKS + 5):
                        if c < CHUNKS:
                            h, m = hid[c % 2][:, 0:wd(c)], mix[c % 2][:, 0:wd(c)]
                            dve.wait_ge(conv_ev, b + c + 1)
                            dve.scalar_tensor_tensor(h, h, SLOPE, h, ALU.mult, ALU.max).then_inc(leaky, 1)
                            dve.wait_ge(leaky, b + c + 1)
                            dve.tensor_tensor(m, xT[:, cols(c)], h, ALU.subtract).then_inc(less, 1)
                        if 1 <= c <= CHUNKS:
                            d = c - 1
                            h, m, g = hid[d % 2][:, 0:wd(d)], mix[d % 2][:, 0:wd(d)], sca[d % 2][:, 0:wd(d)]
                            dve.wait_ge(gate_ev, b + d + 1)
                            dve.wait_ge(less, b + d + 1)
                            dve.tensor_tensor(m, m, g, ALU.mult).then_inc(mixed, 1)
                            dve.wait_ge(mixed, b + d + 1)
                            dve.tensor_tensor(xT[:, cols(d)], h, m, ALU.add).then_inc(state, 1)
                        if c >= 5 and last:
                            d = c - 5
                            k = chunk_tiles(d)
                            dve.wait_ge(tab_t, (LAYERS * CHUNKS) + d + 1)
                            if d >= 2:
                                dve.wait_ge(final[d % 2], 16 * (d // 2))
                            dve.tensor_tensor(row_stage[d % 2][:, 0:k * P],
                                              xres[:, d * CHUNK:d * CHUNK + k, :].rearrange("p t d -> p (t d)"),
                                              bank[4 + d % 2][:, 0:k * P], ALU.add).then_inc(out_ev, 1)

                @block.sync
                def _(sp):
                    for c in range(CHUNKS):
                        if not last:
                            pub_store(sp, layer + 1, c)
                        elif c < CHUNKS - 1:
                            sp.wait_ge(out_ev, c + 1)
                            sp.dma_start(out[c * CHUNK * P:(c + 1) * CHUNK * P, :].rearrange("(t p) d -> p t d", p=P),
                                         row_stage[c % 2].rearrange("p (t d) -> p t d", t=CHUNK)).then_inc(final[c % 2], 16)
                        else:
                            sp.wait_ge(out_ev, c + 1)
                            sp.dma_start(out[(NODE_TILES - 1) * P:N, :], row_stage[c % 2][0:LAST, 0:D]).then_inc(final[c % 2], 16)
                    if last:
                        for k in range(2):
                            sp.wait_ge(final[k], 16 * len(range(k, CHUNKS, 2)))
                    else:
                        for k in range(2):
                            sp.wait_ge(row_out[k], 16 * stores_before(layer + 2, k))

        for layer in range(LAYERS):
            aggregate(layer)
            if layer == 0:
                inv_block(1, inv_in)
            update(layer)


def kernel(**inputs):
    import numpy as np
    import concourse.bacc as bacc
    from concourse.bass_utils import run_bass_kernel_spmd as run

    x, src, dst, rel = (np.asarray(inputs[k]) for k in ("x", "src", "dst", "edge_type_4"))

    def rows(a, fill):
        return np.concatenate([a, np.full(EDGE_ROWS * P - E, fill, a.dtype)]).reshape(EDGE_ROWS, 1, P)

    before = np.concatenate([np.full(1, -1, dst.dtype), dst[:-1]])
    after = np.concatenate([dst[1:], np.full(1, N, dst.dtype)])
    edges = np.concatenate([rows(src, 0), rows(rel, 0), rows(dst, N), rows(before, N), rows(after, N)],
                           axis=1).reshape(EDGE_ROWS, PLANES * P)
    arrays = {"x": x, "edges": edges}
    for name, key in (("w0", "L0_gnn_weight"), ("b0", "L0_gnn_bias"), ("conv_w", "L1_gnn_conv_w"),
                      ("conv_b", "L1_gnn_conv_b"), ("gate_w1", "L1_gnn_gate_w1"),
                      ("gate_w2", "L1_gnn_gate_w2"), ("gate_b", "L1_gnn_gate_b")):
        arrays[name] = np.asarray(inputs[key])
    nc = bacc.Bacc("TRN2", target_bir_lowering=False, num_devices=1)
    arrays = {f"in_{k}": np.ascontiguousarray(a) for k, a in arrays.items()}
    args = [nc.dram_tensor(k, a.shape, mybir.dt.from_np(a.dtype), kind="ExternalInput").ap()
            for k, a in arrays.items()]
    out = nc.dram_tensor("out_x", (N, D), F32, kind="ExternalOutput").ap()
    build(nc, *args, out)
    r = run(nc, [arrays], core_ids=[0])
    return r.results[0]["out_x"]
```

```python
from contextlib import ExitStack

import concourse.bass as bass
from concourse import mybir

F32 = mybir.dt.float32
BF16 = mybir.dt.bfloat16
F16 = mybir.dt.float16
I32 = mybir.dt.int32
ALU = mybir.AluOpType
ACT = mybir.ActivationFunctionType
AX_X = mybir.AxisListType.X

P = 128
N = 6250
E = 106250
D = 128
RELS = 4
LAYERS = 4
NODE_TILES = -(-N // P)
NPAD = NODE_TILES * P
LAST = N - (NODE_TILES - 1) * P
EDGE_TILES = -(-E // P)
EDGE_ROWS = EDGE_TILES + 1
QUAD = 4
STEPS = 3
BODY = QUAD * STEPS
ITERS = -(-EDGE_TILES // BODY)
TILES = ITERS * BODY
HALF = 2 * QUAD
TC = -(-(TILES + BODY) // P)
TPAD = TC * P
VN = NODE_TILES + 2
GW = 10
GROUPS = ITERS * 9
GPS = 3
GC = -(-GROUPS // P)
WIN = 2 * P
ALIGN = 32
ALIGN_SHIFT = 5
WIN_ROWS = EDGE_ROWS * P // ALIGN
CW = 450
CG = CW // GW
CB = CG // 9
CHUNKS_A = GROUPS // CG
CHUNK = 4
CHUNKS = -(-NODE_TILES // CHUNK)
ZERO_ROW = NPAD * RELS
ZERO_EDGE = TILES * P
BIG = 3.3895313892515355e38
EPS = 1e-5
SLOPE = 0.01
W4 = QUAD * P
NW = NODE_TILES * GW
S_A = 25
assert CG % 9 == 0 and CHUNKS_A * CG == GROUPS and GROUPS * GW >= N and TPAD >= TILES + BODY
assert STEPS * GPS == 9


def chunk_tiles(c):
    return min(CHUNK, NODE_TILES - c * CHUNK)


def tiles_done(c):
    return NODE_TILES if c == CHUNKS_A else c * CW // P


def build(nc, x, src_in, rel_in, dst_in, before_in, after_in, windows, w0, b0, conv_w, conv_b,
          gate_w1, gate_w2, gate_b, out):
    with ExitStack() as ctx:
        def sb(name, shape, dt):
            return ctx.enter_context(nc.sbuf_tensor(name, shape, dt))

        def sem(name):
            return ctx.enter_context(nc.semaphore(name))

        def dram(name, shape, dt):
            return nc.dram_tensor(name, shape, dt, kind="Internal").ap()

        msg_table = dram("msg_table", (ZERO_ROW + P, D), F32)
        node_table = dram("node_table", (NPAD, D), F32)
        edge_rows = dram("edge_rows", (ZERO_EDGE + P, D), F32)
        keep_max = dram("keep_max", (TPAD, P), BF16)
        keep_sum = dram("keep_sum", (TPAD, P), BF16)
        bounds = dram("bounds", (VN, P), I32)
        src_idx = dram("src_idx", (P, TPAD), I32)
        adj = dram("adj", (CHUNKS_A, P, NODE_TILES, CW), BF16)
        inv_dram = dram("inv_dram", (2, NPAD), F32)
        res_dram = dram("res_dram", (NODE_TILES, P, D), F32)

        xT = sb("xT", [P, NPAD], F32)
        ident = sb("ident", [P, P], F32)
        conv_sb = sb("conv_sb", [P, LAYERS, D], F32)
        g1T = sb("g1T", [P, D], F32)
        g2T = sb("g2T", [P, D], F32)
        bcols = sb("bcols", [P, LAYERS + 1], F32)
        mv = sb("mv", [P, NODE_TILES, 2], F32)
        rstd = sb("rstd", [P, NODE_TILES], F32)
        nmr = sb("nmr", [P, NODE_TILES], F32)
        deg = sb("deg", [P, 2, NODE_TILES], F32)
        idx_end = sb("idx_end", [P, NODE_TILES], I32)
        idx_a = sb("idx_a", [P, HALF], I32)
        idx_b = sb("idx_b", [P, BODY - HALF], I32)
        flag = sb("flag", [1, 1], I32)
        arena = sb("arena", [P, 44600], F32)

        class Region:

            def __init__(self, at=0):
                self.at = at

            def take(self, words):
                self.at += words
                assert self.at <= 44600, self.at
                return arena[:, self.at - words:self.at]

        bank = [ctx.enter_context(nc.psum_tensor(f"bank{i}", [P, 512], F32)) for i in range(8)]

        R = Region()
        stage = R.take(NODE_TILES * CW).bitcast(BF16).rearrange("p (b s w) -> p b s w", b=2, s=NODE_TILES)
        xres = R.take(NODE_TILES * D).rearrange("p (t d) -> p t d", t=NODE_TILES)
        keyt = R.take(GC * P * 6).rearrange("p (g w k) -> p g w k", w=2, k=3)
        idx_msg = R.take(TPAD).bitcast(I32)
        iota_h = R.take(256).bitcast(F16)
        ring = R.take(BODY * D).rearrange("p (t d) -> p t d", t=BODY)
        scanned = R.take(STEPS * W4).rearrange("p (s w) -> p s w", s=STEPS)
        ends = R.take(STEPS * W4).rearrange("p (s w) -> p s w", s=STEPS)
        keep_a = R.take(HALF * P // 2).bitcast(BF16)
        keep_b = R.take((BODY - HALF) * P // 2).bitcast(BF16)
        hot_at = R.at
        hot_col = R.take(GPS * 2 * NW // 2).bitcast(BF16).rearrange("p (g w n) -> p g w n", g=GPS, w=2)
        hot_lo = R.take(GPS * 2 * P // 2).bitcast(BF16).rearrange("p (g w n) -> p g w n", g=GPS, w=2)
        hot_hi = R.take(GPS * 2 * 50 // 2).bitcast(BF16).rearrange("p (g w n) -> p g w n", g=GPS, w=2)

        s_tiles = sem("s_tiles")
        s_load = sem("s_load")
        s_gates = sem("s_gates")
        s_const = sem("s_const")
        s_dve = sem("s_dve")
        s_scr = sem("s_scr")
        s_got = sem("s_got")
        s_back = sem("s_back")
        step_dve = sem("step_dve")
        step_pe = sem("step_pe")
        step_ev = sem("step_ev")
        step_act = sem("step_act")
        chain = [0]

        def link(dve, ins):
            chain[0] += 1
            ins.then_inc(s_dve, 1)
            dve.wait_ge(s_dve, chain[0])

        S = Region()
        tab = S.take(5 * TPAD).bitcast(I32).rearrange("p (k c e) -> p k c e", k=5, c=TC)
        f_a, f_b, f_c, f_d = (S.take(TPAD).rearrange("p (c e) -> p c e", c=TC) for _ in range(4))
        keep_m = S.take(TPAD // 2).bitcast(BF16).rearrange("p (c e) -> p c e", c=TC)
        keep_s = S.take(TPAD // 2).bitcast(BF16).rearrange("p (c e) -> p c e", c=TC)
        src_t = S.take(TPAD).bitcast(I32)
        first_col = S.take(TC)
        gload = S.take(2 * D).rearrange("p (k d) -> p k d", k=2)
        first_all = S.take(TPAD)
        setup2_at = S.at
        FULL = EDGE_ROWS // P
        with nc.Block() as block:
            @block.sync
            def _(sp):
                sp.wait_ge(s_const, 1)
                for k, t in enumerate((src_in, rel_in, dst_in, before_in, after_in)):
                    sp.dma_start(tab[:, k, 0:FULL, :],
                                 t[0:FULL * P, :].rearrange("(c p) e -> p c e", p=P)).then_inc(s_tiles, 16)
                    sp.dma_start(tab[0:EDGE_ROWS - FULL * P, k, FULL, :],
                                 t[FULL * P:EDGE_ROWS, :]).then_inc(s_tiles, 16)
                sp.dma_start(gload[:, 0, :], gate_w1).then_inc(s_gates, 16)
                sp.dma_start(gload[:, 1, :], gate_w2).then_inc(s_gates, 16)
                sp.dma_start(xres[:, 0:NODE_TILES - 1, :],
                             x[0:(NODE_TILES - 1) * P, :].rearrange("(t p) d -> p t d", p=P)).then_inc(s_load, 16)
                sp.dma_start(xres[0:LAST, NODE_TILES - 1, :], x[(NODE_TILES - 1) * P:N, :]).then_inc(s_load, 16)
                sp.dma_start(conv_sb[:, :, :], conv_w.rearrange("l i o -> i l o")).then_inc(s_load, 16)
                with nc.allow_non_contiguous_dma(reason="five bias columns"):
                    for l in range(LAYERS):
                        sp.dma_start(bcols[:, l:l + 1], conv_b[l, :].unsqueeze(1)).then_inc(s_load, 16)
                    sp.dma_start(bcols[:, LAYERS:LAYERS + 1], gate_b.unsqueeze(1)).then_inc(s_load, 16)
                sp.wait_ge(step_dve, 2)
                sp.dma_start(keep_max.rearrange("(c p) e -> p c e", p=P), keep_m).then_inc(s_scr, 16)
                sp.dma_start(keep_sum.rearrange("(c p) e -> p c e", p=P), keep_s).then_inc(s_scr, 16)
                sp.wait_ge(step_ev, TC)
                sp.dma_start(src_idx, src_t).then_inc(s_scr, 16)
                sp.wait_ge(s_scr, 48)
                sp.wait_ge(s_load, 16 * 8)

            @block.gpsimd
            def _(pool):
                pool.memset(tab[:, 0:2, TC - 1, :], 0)
                pool.memset(tab[:, 2:5, TC - 1, :], N)
                pool.memset(xres[:, NODE_TILES - 1, :], 0.0).then_inc(s_const, 1)
                pool.memset(ident[:, :], 0.0).then_inc(s_const, 1)
                pool.iota(iota_h, [[1, 512]], base=0, channel_multiplier=0, allow_small_or_imprecise_dtypes=True)
                pool.wait_ge(s_const, 2)
                pool.affine_select(out=ident[:, :], in_=ident[:, :], compare_op=ALU.not_equal, fill=1.0,
                                   base=0, pattern=[[-1, P]], channel_multiplier=1).then_inc(s_const, 1)

            @block.vector
            def _(dve):
                def L(ins):
                    link(dve, ins)

                src, rel, dst, before, after = (tab[:, k, :, :] for k in range(5))
                dve.wait_ge(s_const, 3)
                dve.wait_ge(s_tiles, 160)
                dve.tensor_copy(first_col, dst[:, :, 0]).then_inc(step_dve, 1)
                L(dve.tensor_tensor(f_a, before, dst, ALU.is_equal))
                L(dve.tensor_copy(keep_s, f_a))
                L(dve.tensor_scalar(f_b, f_a, 2.0, 1.0, ALU.mult, ALU.subtract))
                dve.tensor_scalar(keep_m, f_b, BIG, None, ALU.mult).then_inc(step_dve, 1)
                L(dve.scalar_tensor_tensor(f_a, src, float(RELS), rel, ALU.mult, ALU.add))
                L(dve.tensor_scalar(f_c, rel, 0.0, None, ALU.is_ge))
                L(dve.scalar_tensor_tensor(f_d, rel, float(RELS - 1), f_c, ALU.is_le, ALU.mult))
                L(dve.scalar_tensor_tensor(f_c, f_a, float(ZERO_ROW), f_d, ALU.subtract, ALU.mult))
                L(dve.tensor_scalar(f_a, f_c, float(ZERO_ROW), None, ALU.add))
                dve.tensor_copy(f_d, src).then_inc(step_dve, 1)
                dve.wait_ge(step_pe, 1)
                dve.tensor_copy(first_all[:, 0:512], bank[0][:, :])
                dve.tensor_copy(first_all[:, 512:TPAD], bank[1][:, 0:TPAD - 512])
                for c in range(TC):
                    dve.wait_ge(step_pe, c + 2)
                    dve.tensor_copy(idx_msg[:, c * P:(c + 1) * P], bank[2 + c % 2][:, 0:P])
                    dve.tensor_copy(src_t[:, c * P:(c + 1) * P], bank[2 + c % 2][:, P:2 * P]).then_inc(step_ev, 1)
                dve.wait_ge(step_pe, TC + 2)
                dve.tensor_copy(g1T[:, :], bank[4][:, 0:P])
                dve.tensor_copy(g2T[:, :], bank[4][:, P:2 * P])

            @block.tensor
            def _(pe):
                pe.wait_ge(s_const, 3)
                pe.wait_ge(step_dve, 1)
                for c in range(TC):
                    mm = pe.matmul(bank[c // 4][:, (c % 4) * P:(c % 4 + 1) * P],
                                   first_col[:, c:c + 1].to_broadcast([P, P]), ident[:, :], start=True, stop=True)
                mm.then_inc(step_pe, 1)
                pe.wait_ge(step_dve, 3)
                for c in range(TC):
                    if c >= 2:
                        pe.wait_ge(step_ev, c - 1)
                    pe.transpose(bank[2 + c % 2][:, 0:P], f_a[:, c, :], ident[:, :])
                    pe.transpose(bank[2 + c % 2][:, P:2 * P], f_d[:, c, :], ident[:, :]).then_inc(step_pe, 1)
                pe.wait_ge(s_gates, 32)
                pe.transpose(bank[4][:, 0:P], gload[:, 0, :], ident[:, :])
                pe.transpose(bank[4][:, P:2 * P], gload[:, 1, :], ident[:, :]).then_inc(step_pe, 1)

        S = Region(0)
        brow_at = S.take(VN * P).bitcast(I32).rearrange("p (t e) -> p t e", t=VN)
        S2 = Region(setup2_at)
        node = S2.take(VN)
        tcount = S2.take(VN)
        trow = S2.take(VN).bitcast(I32)
        inner = S2.take(VN)
        bnd = S2.take(VN)
        bnd_i = S2.take(P).bitcast(I32)
        nxt = S2.take(NODE_TILES).bitcast(I32)
        g_lo = S2.take(GC).bitcast(I32)
        g_hi = S2.take(GC).bitcast(I32)
        g_id = S2.take(GC)
        g_row = S2.take(GC).bitcast(I32)
        g_tmp = S2.take(4 * GC).rearrange("p (k c) -> p k c", k=4)
        over = S2.take(2)
        f_deg = S2.take(2 * NODE_TILES).rearrange("p (k t) -> p k t", k=2)
        junk = S2.take(EDGE_TILES)
        hit = S2.take(VN * P).rearrange("p (t e) -> p t e", t=VN)
        assert VN * P <= 5 * TPAD + 4 * TPAD and S2.at <= NODE_TILES * CW, S2.at
        with nc.Block() as block:
            @block.gpsimd
            def _(pool):
                pool.iota(node, [[P, VN]], base=0, channel_multiplier=1, allow_small_or_imprecise_dtypes=True)
                pool.iota(g_id, [[P, GC]], base=0, channel_multiplier=1,
                          allow_small_or_imprecise_dtypes=True).then_inc(s_const, 1)
                for t in range(VN):
                    if t % 17 == 0:
                        pool.wait_ge(step_dve, 4 + t // 17)
                    pool.indirect_dma_start(brow_at[:, t, :], None, dst_in,
                                            bass.IndirectOffsetOnAxis(ap=trow[:, t:t + 1], axis=0)
                                            ).then_inc(s_got, 16)

            @block.vector
            def _(dve):
                def L(ins):
                    link(dve, ins)

                dve.wait_ge(s_const, 4)
                for h in range(3):
                    sl = slice(17 * h, 17 * h + 17)
                    for t in range(17 * h, 17 * h + 17):
                        L(dve.tensor_scalar(junk, first_all[:, 0:EDGE_TILES], node[:, t:t + 1], 0.0,
                                            ALU.is_lt, ALU.add, accum_out=tcount[:, t:t + 1]))
                    L(dve.tensor_scalar(inner[:, sl], tcount[:, sl], 1.0, 0.0, ALU.subtract, ALU.max))
                    dve.tensor_copy(trow[:, sl], inner[:, sl]).then_inc(step_dve, 1)
                dve.wait_ge(s_got, 16 * VN)
                L(dve.tensor_tensor(hit, brow_at, node.unsqueeze(2).to_broadcast([P, VN, P]), ALU.is_lt))
                L(dve.tensor_reduce(bnd, hit, AX_X, ALU.add))
                L(dve.scalar_tensor_tensor(bnd, inner, float(P), bnd, ALU.mult, ALU.add))
                dve.tensor_copy(junk[:, 0:1], bnd[:, 0:1]).then_inc(step_dve, 1)
                dve.wait_ge(step_pe, TC + 3)
                dve.tensor_copy(bnd_i[0:VN, :], bank[0][0:VN, 0:P]).then_inc(step_dve, 1)
                dve.wait_ge(s_back, 48)
                L(dve.tensor_tensor(deg[:, 1, :], nxt, bnd[:, 0:NODE_TILES], ALU.subtract))
                L(dve.tensor_scalar(f_deg[:, 0, :], deg[:, 1, :], 0.0, None, ALU.is_gt))
                L(dve.scalar_tensor_tensor(f_deg[:, 1, :], nxt, float(ZERO_EDGE + 1), f_deg[:, 0, :],
                                           ALU.subtract, ALU.mult))
                L(dve.tensor_scalar(idx_end[:, :], f_deg[:, 1, :], float(ZERO_EDGE), None, ALU.add))
                L(dve.tensor_scalar(g_row, g_lo, ALIGN_SHIFT, None, ALU.arith_shift_right))
                L(dve.scalar_tensor_tensor(g_tmp[:, 0, :], g_row, float(-ALIGN), g_hi, ALU.mult, ALU.add))
                L(dve.tensor_scalar(g_tmp[:, 1, :], g_id, float(N // GW), None, ALU.is_lt))
                L(dve.scalar_tensor_tensor(g_tmp[:, 2, :], g_tmp[:, 0, :], float(WIN), g_tmp[:, 1, :],
                                           ALU.is_gt, ALU.mult))
                L(dve.tensor_reduce(over[:, 0:1], g_tmp[:, 2, :], AX_X, ALU.max))
                L(dve.tensor_scalar(g_tmp[:, 3, :], g_row, float(WIN_ROWS - 1), None, ALU.min))
                dve.tensor_copy(g_row, g_tmp[:, 3, :]).then_inc(step_dve, 1)
                dve.wait_ge(step_pe, TC + 4)
                dve.tensor_reduce(flag[:, :], bank[1][0:1, 0:P], AX_X, ALU.max)

            @block.tensor
            def _(pe):
                pe.wait_ge(step_dve, 7)
                pe.transpose(bank[0][0:VN, 0:P], bnd, ident[:, :]).then_inc(step_pe, 1)
                pe.wait_ge(step_dve, 9)
                pe.transpose(bank[1][0:1, 0:P], over[:, 0:1], ident[:, :]).then_inc(step_pe, 1)

            @block.sync
            def _(sp):
                sp.wait_ge(step_dve, 8)
                sp.dma_start(bounds, bnd_i[0:VN, :]).then_inc(s_scr, 16)
                sp.wait_ge(s_scr, 64)
                flat = bounds.rearrange("t p -> (t p)")
                with nc.allow_non_contiguous_dma(reason="bounds in node-major and group-major layout"):
                    sp.dma_start(nxt, flat[1:1 + NPAD].rearrange("(t p) -> p t", p=P)).then_inc(s_back, 16)
                    sp.dma_start(g_lo, flat[0:GC * P * GW].rearrange("(c p g) -> p c g", p=P, g=GW)[:, :, 0]
                                 ).then_inc(s_back, 16)
                    sp.dma_start(g_hi, flat[GW:GW + GC * P * GW].rearrange("(c p g) -> p c g", p=P, g=GW)[:, :, 0]
                                 ).then_inc(s_back, 16)
                sp.wait_ge(s_back, 48)

        S = Region(0)
        win = S.take(GC * 2 * WIN).bitcast(I32).rearrange("p (c k e) -> p c k e", c=GC, k=2)
        assert S.at <= setup2_at
        hi_i = hit.rearrange("p t e -> p (t e)")[:, 0:GC * WIN].bitcast(I32).rearrange("p (c e) -> p c e", c=GC)
        lo_i = hit.rearrange("p t e -> p (t e)")[:, GC * WIN:2 * GC * WIN].bitcast(I32).rearrange("p (c e) -> p c e", c=GC)
        w_a, w_b, w_c = (hit.rearrange("p t e -> p (t e)")[:, k * GC * WIN:(k + 1) * GC * WIN]
                         .rearrange("p (c e) -> p c e", c=GC) for k in (2, 3, 4))
        S = Region(S2.at)
        w_d, w_e = (S.take(GC * WIN).rearrange("p (c e) -> p c e", c=GC) for _ in range(2))
        assert S.at <= NODE_TILES * CW and 5 * GC * WIN <= VN * P
        with nc.Block() as block:
            @block.gpsimd
            def _(pool):
                for c in range(GC):
                    pool.indirect_dma_start(win[:, c, :, :].rearrange("p k e -> p (k e)"), None, windows,
                                            bass.IndirectOffsetOnAxis(ap=g_row[:, c:c + 1], axis=0)
                                            ).then_inc(s_got, 16)

            @block.vector
            def _(dve):
                def L(ins):
                    link(dve, ins)

                def wide(v):
                    return v.unsqueeze(2).to_broadcast([P, GC, WIN])

                src, dst = win[:, :, 0, :], win[:, :, 1, :]
                L(dve.tensor_scalar(g_tmp[:, 0, :], g_id, float(GW), None, ALU.mult))
                dve.wait_ge(s_got, 16 * (VN + GC))
                L(dve.tensor_tensor(w_a, dst, wide(g_tmp[:, 0, :]), ALU.subtract))
                L(dve.tensor_scalar(w_b, w_a, 0.0, None, ALU.is_ge))
                L(dve.scalar_tensor_tensor(w_c, w_a, float(GW), w_b, ALU.is_lt, ALU.mult))
                L(dve.scalar_tensor_tensor(w_b, dst, float(N), w_c, ALU.is_lt, ALU.mult))
                L(dve.tensor_scalar(hi_i, src, 7, None, ALU.arith_shift_right))
                L(dve.tensor_scalar(lo_i, src, P - 1, None, ALU.bitwise_and))
                L(dve.scalar_tensor_tensor(w_c, hi_i, float(GW), w_a, ALU.mult, ALU.add))
                L(dve.scalar_tensor_tensor(w_d, w_c, 1.0, w_b, ALU.add, ALU.mult))
                L(dve.tensor_scalar(w_a, w_d, 1.0, None, ALU.subtract))
                L(dve.scalar_tensor_tensor(w_d, lo_i, 1.0, w_b, ALU.add, ALU.mult))
                L(dve.tensor_scalar(w_c, w_d, 1.0, None, ALU.subtract))
                L(dve.scalar_tensor_tensor(w_d, hi_i, 1.0, w_b, ALU.add, ALU.mult))
                dve.tensor_scalar(w_e, w_d, 1.0, None, ALU.subtract).then_inc(step_dve, 1)
                for c in range(GC):
                    for w in range(2):
                        n = 2 * c + w
                        dve.wait_ge(step_pe, TC + 5 + n)
                        dve.tensor_copy(keyt[:, c * P:(c + 1) * P, w, :].rearrange("p g k -> p k g"),
                                        bank[n % 2][:, 0:3 * P].rearrange("p (k g) -> p k g", k=3)
                                        ).then_inc(step_ev, 1)

            @block.tensor
            def _(pe):
                pe.wait_ge(step_dve, 10)
                for c in range(GC):
                    for w in range(2):
                        n = 2 * c + w
                        if n >= 2:
                            pe.wait_ge(step_ev, TC + n - 1)
                        for k, t in enumerate((w_a, w_c, w_e)):
                            mm = pe.transpose(bank[n % 2][:, k * P:(k + 1) * P], t[:, c, w * P:(w + 1) * P],
                                              ident[:, :])
                        mm.then_inc(step_pe, 1)

        ln_stat = sem("ln_stat")
        ln_tiles = sem("ln_tiles")
        ln_rows = sem("ln_rows")
        ln_t = sem("ln_t")
        ln_ev = sem("ln_ev")
        S = Region(0)
        stats = S.take(NODE_TILES * 6).rearrange("p (t k) -> p t k", k=6)
        rows = [S.take(W4).rearrange("p (t d) -> p t d", t=CHUNK) for _ in range(2)]
        tstage = [S.take(W4) for _ in range(4)]
        zrow = S.take(P)
        w0_sb = S.take((RELS + 1) * D).rearrange("p (r d) -> p r d", r=RELS + 1)
        brow = S.take((RELS + 1) * D)

        def ln_dve_stats(dve, use):
            base = use * 5
            for t in range(NODE_TILES):
                dve.bn_stats(stats[:, t, :], xres[:, t, :]).then_inc(ln_tiles, 1)
            dve.wait_ge(ln_tiles, (use + 1) * NODE_TILES)
            for t in range(NODE_TILES):
                last = dve.bn_aggr(mv[:, t, :], stats[:, t, :])
            last.then_inc(ln_stat, 1)
            dve.wait_ge(ln_stat, base + 1)
            dve.tensor_scalar(rstd[:, :], mv[:, :, 1], EPS, None, ALU.add).then_inc(ln_stat, 1)
            dve.wait_ge(ln_stat, base + 3)
            dve.reciprocal(rstd[:, :], rstd[:, :]).then_inc(ln_stat, 1)
            dve.wait_ge(ln_stat, base + 4)
            dve.scalar_tensor_tensor(nmr[:, :], mv[:, :, 0], -1.0, rstd[:, :], ALU.mult, ALU.mult
                                     ).then_inc(ln_stat, 1)

        def ln_act(act, use):
            base = use * 5
            act.wait_ge(ln_stat, base + 2)
            act.activation(rstd[:, :], rstd[:, :], ACT.Sqrt).then_inc(ln_stat, 1)
            act.wait_ge(ln_stat, base + 5)

        def ln_act_rows(act, use, c):
            if c >= 2:
                act.wait_ge(ln_t, use * CHUNKS + c - 1)
            for k in range(chunk_tiles(c)):
                t = c * CHUNK + k
                last = act.activation(rows[c % 2][:, k, :], xres[:, t, :], ACT.Relu,
                                      bias=nmr[:, t:t + 1], scale=rstd[:, t:t + 1])
            last.then_inc(ln_rows, 1)

        def ln_pe(pe, use, c):
            pe.wait_ge(ln_rows, use * CHUNKS + c + 1)
            if c >= 2:
                pe.wait_ge(ln_ev, use * CHUNKS + c - 1)
            for k in range(chunk_tiles(c)):
                mm = pe.transpose(bank[c % 2][:, k * P:(k + 1) * P], rows[c % 2][:, k, :], ident[:, :])
            mm.then_inc(ln_t, 1)

        def cols(c):
            return slice(c * CHUNK * P, c * CHUNK * P + chunk_tiles(c) * P)

        def ln_dve_cols(dve, use, c):
            dve.wait_ge(ln_t, use * CHUNKS + c + 1)
            dve.tensor_copy(xT[:, cols(c)], bank[c % 2][:, 0:chunk_tiles(c) * P]).then_inc(ln_ev, 1)

        tab_mm = sem("tab_mm")
        tab_ev = sem("tab_ev")
        tab_out = [sem(f"tab_out{k}") for k in range(4)]
        zero_out = sem("zero_out")
        s_w0 = sem("s_w0")
        self_mm = sem("self_mm")
        self_ev = sem("self_ev")
        self_bias = sem("self_bias")
        with nc.Block() as block:
            @block.sync
            def _(sp):
                sp.dma_start(w0_sb, w0.rearrange("r i o -> i r o")).then_inc(s_w0, 16)
                sp.dma_start(brow, b0.rearrange("r d -> (r d)").partition_broadcast(P)).then_inc(s_w0, 16)
                sp.wait_ge(zero_out, 1)
                sp.dma_start(msg_table[ZERO_ROW:ZERO_ROW + P, :], zrow).then_inc(s_scr, 16)
                sp.dma_start(edge_rows[ZERO_EDGE:ZERO_EDGE + P, :], zrow).then_inc(s_scr, 16)
                for t in range(NODE_TILES):
                    sp.wait_ge(tab_ev, t + 1)
                    sp.dma_start(msg_table[t * P * RELS:(t + 1) * P * RELS, :].rearrange("(p r) d -> p (r d)", r=RELS),
                                 tstage[t % 4]).then_inc(tab_out[t % 4], 16)
                for k in range(4):
                    sp.wait_ge(tab_out[k], 16 * len(range(k, NODE_TILES, 4)))
                sp.wait_ge(s_scr, 96)

            @block.vector
            def _(dve):
                dve.memset(zrow, 0.0).then_inc(zero_out, 1)
                ln_dve_stats(dve, 0)

                def table(c):
                    for k in range(chunk_tiles(c)):
                        t = c * CHUNK + k
                        dve.wait_ge(tab_mm, t + 1)
                        if t >= 4:
                            dve.wait_ge(tab_out[t % 4], 16 * (t // 4))
                        dve.tensor_tensor(tstage[t % 4], bank[2 + t % 2][:, :], brow[:, 0:RELS * D],
                                          ALU.add).then_inc(tab_ev, 1)

                def self_term(c):
                    k = chunk_tiles(c)
                    dve.wait_ge(self_mm, c + 1)
                    xc = xres[:, c * CHUNK:c * CHUNK + k, :].rearrange("p t d -> p (t d)")
                    dve.tensor_tensor(xc, xc, bank[4 + c % 2][:, 0:k * P], ALU.add).then_inc(self_ev, 1)

                dve.wait_ge(s_w0, 32)
                for c in range(CHUNKS):
                    ln_dve_cols(dve, 0, c)
                    if c:
                        table(c - 1)
                        self_term(c - 1)
                table(CHUNKS - 1)
                self_term(CHUNKS - 1)
                dve.wait_ge(self_ev, CHUNKS)
                xa = xres[:, :, :]
                dve.tensor_tensor(xa, xa, brow[:, RELS * D:].unsqueeze(1).to_broadcast([P, NODE_TILES, D]), ALU.add)

            @block.scalar
            def _(act):
                ln_act(act, 0)
                for c in range(CHUNKS):
                    ln_act_rows(act, 0, c)

            @block.tensor
            def _(pe):
                def products(c):
                    pe.wait_ge(ln_ev, c + 1)
                    if c >= 2:
                        pe.wait_ge(self_ev, c - 1)
                    for k in range(chunk_tiles(c)):
                        t = c * CHUNK + k
                        if t >= 2:
                            pe.wait_ge(tab_ev, t - 1)
                        pe.matmul(bank[2 + t % 2][:, :], xT[:, t * P:(t + 1) * P],
                                  w0_sb[:, 0:RELS, :].rearrange("p r d -> p (r d)"),
                                  start=True, stop=True).then_inc(tab_mm, 1)
                    for k in range(chunk_tiles(c)):
                        t = c * CHUNK + k
                        mm = pe.matmul(bank[4 + c % 2][:, k * P:(k + 1) * P], xT[:, t * P:(t + 1) * P],
                                       w0_sb[:, RELS, :], start=True, stop=True)
                    mm.then_inc(self_mm, 1)

                pe.wait_ge(s_w0, 32)
                for c in range(CHUNKS):
                    ln_pe(pe, 0, c)
                    if c:
                        products(c - 1)
                products(CHUNKS - 1)

        landed = [sem(f"landed{s}") for s in range(BODY)]
        idx_ready_a = sem("idx_ready_a")
        idx_ready_b = sem("idx_ready_b")
        bodies = sem("bodies")
        keep_ready_a = sem("keep_ready_a")
        keep_ready_b = sem("keep_ready_b")
        turned = sem("turned")
        scan_done = sem("scan_done")
        back = sem("back")
        evac = sem("evac")
        rows_out = [sem(f"rows_out{s}") for s in range(STEPS)]
        hot_ready = sem("hot_ready")
        slab_mm = sem("slab_mm")
        slab_ev = sem("slab_ev")
        chunk_out = [sem(f"chunk_out{h}") for h in range(2)]
        hist_zero = sem("hist_zero")
        hist = bank[7]

        def edge_pass(use, table, idx, keep, ops, adjacency):
            ibase = use * ITERS
            sbase = ibase * STEPS

            with nc.Block() as block:
                @block.gpsimd
                def _(pool):
                    with pool.Fori(0, ITERS) as i:
                        for ready, buf, lo, hi in ((idx_ready_a, idx_a, 0, HALF), (idx_ready_b, idx_b, HALF, BODY)):
                            pool.wait_ge(ready, i + (1 + use * (ITERS + 1)))
                            pool.sem_inc(bodies, 1)
                            for s in range(lo, hi):
                                pool.indirect_dma_start(ring[:, s, :], None, table,
                                                        bass.IndirectOffsetOnAxis(ap=buf[:, s - lo:s - lo + 1], axis=0)
                                                        ).then_inc(landed[s], 16)

                @block.sync
                def _(sp):
                    def load_keep(i, lo, hi, dst, done):
                        v = keep[bass.ds(i * BODY + lo, hi - lo), :].rearrange("v e -> (v e)")
                        sp.dma_start(dst, v.partition_broadcast(P)).then_inc(done, 16)

                    def store(i, s):
                        sp.wait_ge(evac, i * STEPS + (s + 1 + sbase))
                        rows_at = edge_rows[bass.ds(i * (BODY * P) + s * W4, W4), :]
                        sp.dma_start(rows_at.rearrange("(t p) d -> p t d", p=P),
                                     ends[:, s, :].rearrange("p (t d) -> p t d", t=QUAD)).then_inc(rows_out[s], 16)

                    load_keep(0, 0, HALF, keep_a, keep_ready_a)
                    load_keep(0, HALF, BODY, keep_b, keep_ready_b)
                    with sp.Fori(0, ITERS) as i:
                        store(i, 0)
                        store(i, 1)
                        load_keep(i + 1, 0, HALF, keep_a, keep_ready_a)
                        store(i, 2)
                        load_keep(i + 1, HALF, BODY, keep_b, keep_ready_b)
                    for s in range(STEPS):
                        sp.wait_ge(rows_out[s], 16 * (ibase + ITERS))
                    sp.wait_ge(keep_ready_a, 16 * (use + 1) * (ITERS + 1))
                    sp.wait_ge(keep_ready_b, 16 * (use + 1) * (ITERS + 1))

                @block.scalar
                def _(act):
                    def copy_idx_a(i):
                        act.activation(idx_a[:, :], idx[:, bass.ds(i * BODY, HALF)], ACT.Copy).then_inc(idx_ready_a, 1)

                    def copy_idx_b(i):
                        act.activation(idx_b[:, :], idx[:, bass.ds(i * BODY + HALF, BODY - HALF)],
                                       ACT.Copy).then_inc(idx_ready_b, 1)

                    def body(i, first, h, j):
                        for s in range(STEPS):
                            act.wait_ge(back, i * STEPS + (s + 1 + sbase))
                            if not (first and use == 0):
                                act.wait_ge(rows_out[s], i * 16 + 16 * ibase)
                            act.activation(ends[:, s, :], bank[s][:, :], ACT.Copy).then_inc(evac, 1)
                            if s == 1:
                                copy_idx_a(i + 1)
                            if s == 2:
                                copy_idx_b(i + 1)
                            if adjacency:
                                for g in range(GPS):
                                    act.wait_ge(slab_mm, i * 9 + (GPS * s + g + 1))
                                    dst = stage[:, h, :, bass.ds(j * (9 * GW) + (GPS * s + g) * GW, GW)]
                                    act.activation(dst, bank[3 + g][:, 0:NW].rearrange("p (s w) -> p s w", w=GW),
                                                   ACT.Copy).then_inc(slab_ev, 1)

                    def store_chunk(c, h):
                        act.wait_ge(slab_ev, c * CG + CG)
                        at = adj[bass.ds(c, 1), :, :, :].rearrange("o p s w -> (o p) (s w)")
                        act.dma_start(at, stage[:, h, :, :].rearrange("p s w -> p (s w)")).then_inc(chunk_out[h], 16)

                    copy_idx_a(0)
                    copy_idx_b(0)
                    if not adjacency:
                        body(0, True, 0, 0)
                        with act.Fori(1, ITERS) as i:
                            body(i, False, 0, 0)
                        return
                    body(0, True, 0, 0)
                    with act.Fori(1, CB) as j:
                        body(j, False, 0, j)
                    store_chunk(0, 0)
                    with act.Fori(0, CB) as j:
                        body(j + CB, False, 1, j)
                    store_chunk(1, 1)
                    with act.Fori(1, CHUNKS_A // 2) as p:
                        for h in range(2):
                            act.wait_ge(chunk_out[h], p * 16)
                            with act.Fori(0, CB) as j:
                                body(p * (2 * CB) + j + h * CB, False, h, j)
                            store_chunk(p * 2 + h, h)
                    for h in range(2):
                        act.wait_ge(chunk_out[h], 16 * CHUNKS_A // 2)

                @block.tensor
                def _(pe):
                    def body(i, first):
                        for s in range(STEPS):
                            for k in range(QUAD):
                                pe.wait_ge(landed[QUAD * s + k], i * 16 + (16 + 16 * ibase))
                            if not (first and use == 0):
                                pe.wait_ge(evac, i * STEPS + (s + 1 - STEPS + sbase))
                            for k in range(QUAD):
                                mm = pe.transpose(bank[s][:, k * P:(k + 1) * P], ring[:, QUAD * s + k, :], ident[:, :])
                            mm.then_inc(turned, 1)
                            if adjacency:
                                for g in range(GPS):
                                    n = GPS * s + g
                                    pe.wait_ge(hot_ready, i * 9 + (n + 1))
                                    if not (first and n < GPS):
                                        pe.wait_ge(slab_ev, i * 9 + (n + 1 - GPS))
                                    for w in range(2):
                                        pe.matmul(bank[3 + g][:, 0:NW], hot_lo[:, g, w, :], hot_col[:, g, w, :],
                                                  start=(w == 0), stop=(w == 1))
                                        mm = pe.matmul(hist[:, 0:NODE_TILES], hot_lo[:, g, w, :],
                                                       hot_hi[:, g, w, 0:NODE_TILES], start=False, stop=False,
                                                       skip_group_check=True)
                                    mm.then_inc(slab_mm, 1)
                            pe.wait_ge(scan_done, i * STEPS + (s + 1 + sbase))
                            for k in range(QUAD):
                                mm = pe.transpose(bank[s][:, k * P:(k + 1) * P], scanned[:, s, k * P:(k + 1) * P],
                                                  ident[:, :])
                            mm.then_inc(back, 1)

                    if adjacency:
                        pe.wait_ge(hist_zero, 2)
                        pe.matmul(hist[:, 0:NODE_TILES], hot_lo[:, 0, 0, :], hot_hi[:, 0, 0, 0:NODE_TILES],
                                  start=True, stop=False, skip_group_check=True).then_inc(hist_zero, 1)
                    body(0, True)
                    with pe.Fori(1, ITERS) as i:
                        body(i, False)
                    if adjacency:
                        pe.wait_ge(hist_zero, 5)
                        pe.matmul(hist[:, 0:NODE_TILES], hot_lo[:, 0, 0, :], hot_hi[:, 0, 0, 0:NODE_TILES],
                                  start=False, stop=True, skip_group_check=True).then_inc(hist_zero, 1)

                @block.vector
                def _(dve):
                    def body(i, first):
                        for s in range(STEPS):
                            dve.wait_ge(turned, i * STEPS + (s + 1 + sbase))
                            if s != 1:
                                ready = keep_ready_a if s == 0 else keep_ready_b
                                dve.wait_ge(ready, i * 16 + (16 + 16 * use * (ITERS + 1)))
                            if not (first and s == 0):
                                dve.wait_ge(scan_done, i * STEPS + (s + sbase))
                            if not (first and use == 0):
                                dve.wait_ge(back, i * STEPS + (s + 1 - STEPS + sbase))
                            flags = keep_a[:, s * W4:(s + 1) * W4] if s < 2 else keep_b
                            carry = (-BIG if ops[0] == ALU.min else 0.0) if first and s == 0 else \
                                scanned[:, (s - 1) % STEPS, W4 - 1:W4]
                            dve.tensor_tensor_scan(scanned[:, s, :], flags, bank[s][:, :], carry, ops[0], ops[1]
                                                   ).then_inc(scan_done, 1)
                            if adjacency:
                                for g in range(GPS):
                                    n = GPS * s + g
                                    if first and n == 0:
                                        dve.wait_ge(hist_zero, 3)
                                    if not (first and n < GPS):
                                        dve.wait_ge(slab_mm, i * 9 + (n + 1 - GPS))
                                    for w in range(2):
                                        for k, (hot, width) in enumerate(((hot_col, NW), (hot_lo, P), (hot_hi, 50))):
                                            key = keyt[:, bass.ds(i * 9 + n, 1), w, k:k + 1].rearrange("p a b -> p (a b)")
                                            ins = dve.tensor_scalar(hot[:, g, w, :], iota_h[:, 0:width], key, None,
                                                                    ALU.is_equal)
                                    ins.then_inc(hot_ready, 1)

                    if adjacency:
                        dve.memset(hot_lo[:, 0, 0, :], 0.0).then_inc(hist_zero, 1)
                        dve.memset(hot_hi[:, 0, 0, :], 0.0).then_inc(hist_zero, 1)
                    body(0, True)
                    with dve.Fori(1, ITERS) as i:
                        body(i, False)
                    if adjacency:
                        dve.wait_ge(slab_mm, GROUPS)
                        dve.memset(hot_lo[:, 0, 0, :], 0.0).then_inc(hist_zero, 1)
                        dve.memset(hot_hi[:, 0, 0, :], 0.0).then_inc(hist_zero, 1)
                        dve.wait_ge(hist_zero, 6)
                        dve.tensor_copy(deg[:, 0, :], hist[:, 0:NODE_TILES])

        edge_pass(0, msg_table, idx_msg, keep_max, (ALU.min, ALU.max), True)

        last_rows = sem("last_rows")
        res_add = sem("res_add")
        inv_step = sem("inv_step")
        inv_out_s = sem("inv_out_s")
        res_out = sem("res_out")
        S = Region(10 * W4)
        got = S.take(NODE_TILES * D).rearrange("p (t d) -> p t d", t=NODE_TILES)
        inv_rows = S.take(P)[0:2 * NODE_TILES, :]
        with nc.Block() as block:
            @block.gpsimd
            def _(pool):
                for t in range(NODE_TILES):
                    pool.indirect_dma_start(got[:, t, :], None, edge_rows,
                                            bass.IndirectOffsetOnAxis(ap=idx_end[:, t:t + 1], axis=0)
                                            ).then_inc(last_rows, 16)

            @block.vector
            def _(dve):
                d = deg[:, :, :].rearrange("p k t -> p (k t)")
                dve.tensor_scalar(d, d, 1.0, 1.0, ALU.add, ALU.max).then_inc(inv_step, 1)
                dve.wait_ge(inv_step, 2)
                dve.reciprocal(d, d).then_inc(inv_step, 1)
                dve.wait_ge(inv_step, 4)
                dve.tensor_copy(inv_rows, bank[4][0:2 * NODE_TILES, 0:P]).then_inc(inv_step, 1)
                dve.wait_ge(last_rows, 16 * NODE_TILES)
                dve.tensor_tensor(xres[:, :, :], xres[:, :, :], got[:, :, :], ALU.add).then_inc(res_add, 1)
                dve.wait_ge(res_add, 1)
                ln_dve_stats(dve, 1)
                for c in range(CHUNKS):
                    ln_dve_cols(dve, 1, c)

            @block.scalar
            def _(act):
                act.wait_ge(inv_step, 1)
                d = deg[:, :, :].rearrange("p k t -> p (k t)")
                act.activation(d, d, ACT.Sqrt).then_inc(inv_step, 1)
                ln_act(act, 1)
                for c in range(CHUNKS):
                    ln_act_rows(act, 1, c)

            @block.tensor
            def _(pe):
                pe.wait_ge(inv_step, 3)
                pe.transpose(bank[4][0:2 * NODE_TILES, 0:P], deg[:, :, :].rearrange("p k t -> p (k t)"),
                             ident[:, :]).then_inc(inv_step, 1)
                for c in range(CHUNKS):
                    ln_pe(pe, 1, c)

            @block.sync
            def _(sp):
                sp.wait_ge(inv_step, 5)
                sp.dma_start(inv_dram.rearrange("k (t p) -> (k t) p", p=P), inv_rows).then_inc(inv_out_s, 16)
                sp.wait_ge(res_add, 1)
                sp.dma_start(res_dram.rearrange("t p d -> p t d"), xres[:, :, :]).then_inc(res_out, 16)
                sp.wait_ge(inv_out_s, 16)
                sp.wait_ge(res_out, 16)

        conv_mm = sem("conv_mm")
        conv_ev = sem("conv_ev")
        leaky = sem("leaky")
        less = sem("less")
        gate_mm = sem("gate_mm")
        gate_ev = sem("gate_ev")
        mixed = sem("mixed")
        state = sem("state")
        scaled = sem("scaled")

        def dense_layers():
            PROD = LAYERS * CHUNKS_A
            R = Region()
            abuf = R.take(S_A * CW).bitcast(BF16).rearrange("p (b s w) -> p b s w", b=2, s=S_A)
            parts = R.take(NODE_TILES * 3 * P).bitcast(BF16).rearrange("p (b s k d) -> p b s k d", b=2,
                                                                       s=NODE_TILES, k=3)
            agg, loop, hid, sca, mix, invi = ([R.take(CW) for _ in range(2)] for _ in range(6))
            invo = [R.take(CW + P) for _ in range(2)]
            hs, rest, rows_o, rows_r = ([R.take(W4) for _ in range(2)] for _ in range(4))

            a_in = [sem(f"a_in{h}") for h in range(2)]
            a_used = [sem(f"a_used{h}") for h in range(2)]
            invo_in = [sem(f"invo_in{k}") for k in range(2)]
            invi_in = [sem(f"invi_in{k}") for k in range(2)]
            res_in = [sem(f"res_in{k}") for k in range(2)]
            rows_saved = [sem(f"rows_saved{k}") for k in range(2)]
            looped = sem("looped")
            summed = sem("summed")
            normed = sem("normed")
            turned_n = sem("turned_n")
            hi_done = sem("hi_done")
            rest_done = sem("rest_done")
            mid_done = sem("mid_done")
            lo_done = sem("lo_done")
            rows_done = sem("rows_done")

            def split(m):
                return divmod(m, CHUNKS_A)

            def width(c):
                return min(CW, NPAD - c * CW)

            def cols(c):
                return slice(c * CW, c * CW + width(c))

            def tiles(c):
                return tiles_done(c), tiles_done(c + 1)

            def tile_cols(c):
                return slice(tiles_done(c) * P, tiles_done(c + 1) * P)

            def pub_part(n, k):
                l, c = split(n)
                t0, t1 = tiles(c)
                return parts[:, l % 2, t0:t1, k, :]

            def pub_bank(n):
                t0, t1 = tiles(n % CHUNKS_A)
                return bank[4 + n % 2][:, 0:(t1 - t0) * P].rearrange("p (t d) -> p t d", d=P)

            def pub_rest(n):
                t0, t1 = tiles(n % CHUNKS_A)
                return rest[n % 2][:, 0:(t1 - t0) * P].rearrange("p (t d) -> p t d", d=P)

            with nc.Block() as block:
                @block.sync
                def _(sp):
                    for m in range(PROD):
                        for h, (lo, hi) in enumerate(((0, S_A), (S_A, NODE_TILES))):
                            if m >= 1:
                                sp.wait_ge(a_used[h], m * (4 if h == 0 else 1))
                            sp.dma_start(abuf[:, h, 0:hi - lo, :], adj[m % CHUNKS_A, :, lo:hi, :]).then_inc(a_in[h], 16)
                    for h in range(2):
                        sp.wait_ge(a_in[h], 16 * PROD)

                @block.gpsimd
                def _(pool):
                    def load_invo(n):
                        c = n % CHUNKS_A
                        lo, hi = tiles_done(c) * P, min(NPAD, (c + 1) * CW)
                        if n >= 2:
                            pool.wait_ge(scaled, min(n - 1, LAYERS * CHUNKS_A))
                        if n > CHUNKS_A + 1:
                            pool.wait_ge(looped, n - 1 - CHUNKS_A)
                        pool.dma_start(invo[n % 2][:, 0:hi - lo], inv_dram[0, lo:hi].partition_broadcast(P)
                                       ).then_inc(invo_in[n % 2], 16)

                    def load_invi(m):
                        c = m % CHUNKS_A
                        if m >= 2:
                            pool.wait_ge(normed, m - 1)
                        pool.dma_start(invi[m % 2][:, 0:width(c)], inv_dram[1, cols(c)].partition_broadcast(P)
                                       ).then_inc(invi_in[m % 2], 16)

                    def scale(n):
                        c = n % CHUNKS_A
                        w = tile_cols(c).stop - tile_cols(c).start
                        if n >= 2:
                            pool.wait_ge(turned_n, n - 1)
                        pool.tensor_tensor(hs[n % 2][:, 0:w], xT[:, tile_cols(c)], invo[n % 2][:, 0:w],
                                           ALU.mult).then_inc(scaled, 1)

                    load_invo(0)
                    for n in range(CHUNKS_A):
                        load_invo(n + 1)
                        pool.wait_ge(invo_in[n % 2], 16 * (n // 2 + 1))
                        scale(n)
                    load_invi(0)
                    for m in range(PROD):
                        l, c = split(m)
                        n = m + CHUNKS_A
                        last = l == LAYERS - 1
                        off = c * CW - tiles_done(c) * P
                        pool.wait_ge(invo_in[n % 2], 16 * (n // 2 + 1))
                        if l:
                            pool.wait_ge(state, m - CHUNKS_A + 1)
                        if m >= 2:
                            pool.wait_ge(summed, m - 1)
                        pool.tensor_tensor(loop[m % 2][:, 0:width(c)], xT[:, cols(c)],
                                           invo[n % 2][:, off:off + width(c)], ALU.mult).then_inc(looped, 1)
                        if last:
                            t0, t1 = tiles(c)
                            if c >= 2:
                                pool.wait_ge(rows_done, c - 1)
                            pool.dma_start(rows_r[c % 2][:, 0:(t1 - t0) * P].rearrange("p (t d) -> p t d", d=P),
                                           res_dram[t0:t1, :, :].rearrange("t p d -> p t d")
                                           ).then_inc(res_in[c % 2], 16)
                        if m < PROD - 1:
                            load_invo(n + 1)
                            load_invi(m + 1)
                        if not last:
                            pool.wait_ge(state, m + 1)
                            scale(n)

                @block.tensor
                def _(pe):
                    def turn(n):
                        last = n >= LAYERS * CHUNKS_A
                        t0, t1 = tiles(n % CHUNKS_A)
                        if last:
                            pe.wait_ge(state, n - CHUNKS_A + 1)
                        else:
                            pe.wait_ge(scaled, n + 1)
                        if n - 2 >= LAYERS * CHUNKS_A:
                            pe.wait_ge(rows_done, n - 1 - LAYERS * CHUNKS_A)
                        elif n >= 2:
                            pe.wait_ge(rest_done, n - 1)
                        for t in range(t0, t1):
                            rows = xT[:, t * P:(t + 1) * P] if last else hs[n % 2][:, (t - t0) * P:(t - t0 + 1) * P]
                            mm = pe.transpose(bank[4 + n % 2][:, (t - t0) * P:(t - t0 + 1) * P], rows, ident[:, :])
                        mm.then_inc(turned_n, 1)

                    def products(m, h, s, n, start=False, stop=False):
                        l = m // CHUNKS_A
                        for j in range(n):
                            for k in range(3):
                                lhs = parts[:, l % 2, bass.ds(s + j, 1), k, :].rearrange("p a d -> p (a d)")
                                rhs = abuf[:, h, bass.ds(s + j - h * S_A, 1), :].rearrange("p a w -> p (a w)")
                                mm = pe.matmul(bank[m % 2][:, 0:CW], lhs, rhs, start=start and j == k == 0,
                                               stop=stop and j == n - 1 and k == 2, skip_group_check=True)
                        return mm

                    def conv(m):
                        c = m % CHUNKS_A
                        pe.wait_ge(normed, m + 1)
                        if m >= 1:
                            pe.wait_ge(conv_ev, m)
                        pe.matmul(bank[2][:, 0:width(c)], conv_sb[:, m // CHUNKS_A, :], agg[m % 2][:, 0:width(c)],
                                  start=True, stop=True).then_inc(conv_mm, 1)

                    def gate_x(m):
                        c = m % CHUNKS_A
                        if m >= 1:
                            pe.wait_ge(gate_ev, m)
                        pe.matmul(bank[3][:, 0:width(c)], g1T[:, :], xT[:, cols(c)], start=True, stop=False)

                    def gate_h(m):
                        c = m % CHUNKS_A
                        pe.wait_ge(leaky, m + 1)
                        pe.matmul(bank[3][:, 0:width(c)], g2T[:, :], hid[m % 2][:, 0:width(c)],
                                  start=False, stop=True).then_inc(gate_mm, 1)

                    for n in range(CHUNKS_A):
                        turn(n)
                    for m in range(PROD):
                        l, c = split(m)
                        pe.wait_ge(a_in[0], 16 * (m + 1))
                        if m >= 2:
                            pe.wait_ge(summed, m - 1)
                        if c == 0:
                            pe.wait_ge(lo_done, l * CHUNKS_A + 8)
                        products(m, 0, 0, 1, start=True)
                        with pe.Fori(0, 4) as i:
                            products(m, 0, i * 6 + 1, 6).then_inc(a_used[0], 1)
                        if m:
                            conv(m - 1)
                            gate_x(m - 1)
                        pe.wait_ge(a_in[1], 16 * (m + 1))
                        if c == 0:
                            pe.wait_ge(lo_done, l * CHUNKS_A + 13)
                        with pe.Fori(0, 3) as i:
                            products(m, 1, i * 3 + 25, 3)
                        if m:
                            gate_h(m - 1)
                        with pe.Fori(0, 3) as i:
                            products(m, 1, i * 3 + 34, 3)
                        if m:
                            turn(m - 1 + CHUNKS_A)
                        if c == 0:
                            pe.wait_ge(lo_done, (l + 1) * CHUNKS_A)
                        products(m, 1, 43, 6, stop=True).then_inc(a_used[1], 1)
                    conv(PROD - 1)
                    gate_x(PROD - 1)
                    gate_h(PROD - 1)
                    turn(PROD - 1 + CHUNKS_A)

                @block.scalar
                def _(act):
                    def hi_part(n):
                        act.wait_ge(turned_n, n + 1)
                        act.activation(pub_part(n, 0), pub_bank(n), ACT.Copy).then_inc(hi_done, 1)

                    def mid_part(n):
                        act.wait_ge(rest_done, n + 1)
                        act.activation(pub_part(n, 1), pub_rest(n), ACT.Copy).then_inc(mid_done, 1)

                    for n in range(CHUNKS_A):
                        hi_part(n)
                        if n:
                            mid_part(n - 1)
                    mid_part(CHUNKS_A - 1)
                    for m in range(PROD):
                        l, c = split(m)
                        act.wait_ge(conv_mm, m + 1)
                        if m >= 2:
                            act.wait_ge(state, m - 1)
                        act.activation(hid[m % 2][:, 0:width(c)], bank[2][:, 0:width(c)], ACT.Identity,
                                       bias=bcols[:, l:l + 1]).then_inc(conv_ev, 1)
                        act.wait_ge(gate_mm, m + 1)
                        act.activation(sca[m % 2][:, 0:width(c)], bank[3][:, 0:width(c)], ACT.Sigmoid,
                                       bias=bcols[:, LAYERS:LAYERS + 1]).then_inc(gate_ev, 1)
                        if l < LAYERS - 1:
                            hi_part(m + CHUNKS_A)
                            mid_part(m + CHUNKS_A)
                            continue
                        act.wait_ge(rows_done, c + 1)
                        t0, t1 = tiles(c)
                        k = t1 - t0
                        if c < CHUNKS_A - 1:
                            act.dma_start(out[t0 * P:t1 * P, :].rearrange("(t p) d -> p t d", p=P),
                                          rows_o[c % 2][:, 0:k * P].rearrange("p (t d) -> p t d", t=k)
                                          ).then_inc(rows_saved[c % 2], 16)
                        else:
                            act.dma_start(out[t0 * P:(t1 - 1) * P, :].rearrange("(t p) d -> p t d", p=P),
                                          rows_o[c % 2][:, 0:(k - 1) * P].rearrange("p (t d) -> p t d", t=k - 1)
                                          ).then_inc(rows_saved[c % 2], 16)
                            act.dma_start(out[(t1 - 1) * P:N, :], rows_o[c % 2][0:LAST, (k - 1) * P:k * P]
                                          ).then_inc(rows_saved[c % 2], 16)
                    act.wait_ge(rows_saved[0], 16 * (CHUNKS_A // 2))
                    act.wait_ge(rows_saved[1], 16 * (CHUNKS_A // 2 + 1))

                @block.vector
                def _(dve):
                    def rest_part(n):
                        dve.wait_ge(hi_done, n + 1)
                        if n >= 2:
                            dve.wait_ge(lo_done, n - 1)
                        dve.tensor_tensor(pub_rest(n), pub_bank(n), pub_part(n, 0), ALU.subtract
                                          ).then_inc(rest_done, 1)

                    def lo_part(n):
                        dve.wait_ge(mid_done, n + 1)
                        dve.tensor_tensor(pub_part(n, 2), pub_rest(n), pub_part(n, 1), ALU.subtract
                                          ).then_inc(lo_done, 1)

                    for n in range(CHUNKS_A):
                        rest_part(n)
                        if n:
                            lo_part(n - 1)
                    lo_part(CHUNKS_A - 1)
                    for m in range(PROD):
                        l, c = split(m)
                        w = width(c)
                        a, h, x_h, g = (v[m % 2][:, 0:w] for v in (agg, hid, mix, sca))
                        dve.wait_ge(a_used[1], m + 1)
                        dve.wait_ge(looped, m + 1)
                        if m >= 2:
                            dve.wait_ge(conv_mm, m - 1)
                        dve.tensor_tensor(a, bank[m % 2][:, 0:w], loop[m % 2][:, 0:w], ALU.add).then_inc(summed, 1)
                        dve.wait_ge(summed, m + 1)
                        dve.wait_ge(invi_in[m % 2], 16 * (m // 2 + 1))
                        dve.tensor_tensor(a, a, invi[m % 2][:, 0:w], ALU.mult).then_inc(normed, 1)
                        dve.wait_ge(conv_ev, m + 1)
                        dve.scalar_tensor_tensor(h, h, SLOPE, h, ALU.mult, ALU.max).then_inc(leaky, 1)
                        dve.wait_ge(leaky, m + 1)
                        if m >= 2:
                            dve.wait_ge(state, m - 1)
                        dve.tensor_tensor(x_h, xT[:, cols(c)], h, ALU.subtract).then_inc(less, 1)
                        dve.wait_ge(gate_ev, m + 1)
                        dve.wait_ge(less, m + 1)
                        dve.tensor_tensor(x_h, x_h, g, ALU.mult).then_inc(mixed, 1)
                        dve.wait_ge(mixed, m + 1)
                        dve.tensor_tensor(xT[:, cols(c)], h, x_h, ALU.add).then_inc(state, 1)
                        if l < LAYERS - 1:
                            rest_part(m + CHUNKS_A)
                            lo_part(m + CHUNKS_A)
                            continue
                        t0, t1 = tiles(c)
                        k = (t1 - t0) * P
                        dve.wait_ge(turned_n, m + CHUNKS_A + 1)
                        dve.wait_ge(res_in[c % 2], 16 * (c // 2 + 1))
                        if c >= 2:
                            dve.wait_ge(rows_saved[c % 2], 16 * (c // 2))
                        dve.tensor_tensor(rows_o[c % 2][:, 0:k], bank[4 + c % 2][:, 0:k], rows_r[c % 2][:, 0:k],
                                          ALU.add).then_inc(rows_done, 1)

        def gather_layers():
            R = Region()
            acc, inv_out, inv_in = (R.take(NPAD) for _ in range(3))
            assert R.at <= NODE_TILES * CW
            R = Region(NODE_TILES * CW + NODE_TILES * D)
            idx_src = R.take(TPAD).bitcast(I32)
            key_i = R.take(TPAD).bitcast(I32)
            key_lo, key_hi = R.take(TPAD), R.take(TPAD)
            assert R.at <= NODE_TILES * CW + NODE_TILES * D + GC * P * 6
            work = Region(hot_at).take(11 * W4).rearrange("p (k w) -> p k w", k=11)
            rows_in = xres

            key_ready = sem("key_ready")
            key_hot = sem("key_hot")
            key_mm = sem("key_mm")
            out_deg = sem("out_deg")
            tables_in = sem("tables_in")
            ends_in = sem("ends_in")
            ends_t = sem("ends_t")
            acc_add = sem("acc_add")
            res_back = sem("res_back")
            LAST_EDGES = E - (EDGE_TILES - 1) * P
            PAIRS = (EDGE_TILES - 1) // 2
            assert EDGE_TILES % 2 == 1

            norm_in = sem("norm_in")
            out_ev = sem("out_ev")
            final = [sem(f"final{k}") for k in range(2)]

            def update(layer):
                last = layer == LAYERS - 1
                b = layer * CHUNKS
                agg = [work[:, k, :] for k in range(3)]
                hid = [work[:, 3 + k, :] for k in range(2)]
                sca = [work[:, 5 + k, :] for k in range(2)]
                mix = [work[:, 7 + k, :] for k in range(2)]

                def wd(c):
                    return chunk_tiles(c) * P

                with nc.Block() as block:
                    @block.gpsimd
                    def _(pool):
                        for c in range(CHUNKS + 3):
                            if c < CHUNKS:
                                if c >= 3:
                                    pool.wait_ge(conv_mm, b + c - 2)
                                pool.tensor_tensor(agg[c % 3][:, 0:wd(c)], acc[:, cols(c)], inv_in[:, cols(c)],
                                                   ALU.mult).then_inc(norm_in, 1)
                            if c >= 3 and not last:
                                pool.wait_ge(state, b + c - 2)
                                pool.wait_ge(norm_in, b + c - 2)
                                pub_scale(pool, c - 3)

                    @block.tensor
                    def _(pe):
                        def conv(c):
                            pe.wait_ge(norm_in, b + c + 1)
                            if b + c >= 2:
                                pe.wait_ge(conv_ev, b + c - 1)
                            pe.matmul(bank[c % 2][:, 0:wd(c)], conv_sb[:, layer, :], agg[c % 3][:, 0:wd(c)],
                                      start=True, stop=True).then_inc(conv_mm, 1)

                        def gate(c):
                            if b + c >= 2:
                                pe.wait_ge(gate_ev, b + c - 1)
                            pe.matmul(bank[2 + c % 2][:, 0:wd(c)], g1T[:, :], xT[:, cols(c)], start=True, stop=False)
                            pe.wait_ge(leaky, b + c + 1)
                            pe.matmul(bank[2 + c % 2][:, 0:wd(c)], g2T[:, :], hid[c % 2][:, 0:wd(c)],
                                      start=False, stop=True).then_inc(gate_mm, 1)

                        def turn(c):
                            if last:
                                pe.wait_ge(state, b + c + 1)
                                if c >= 2:
                                    pe.wait_ge(out_ev, c - 1)
                                for k in range(chunk_tiles(c)):
                                    t = c * CHUNK + k
                                    mm = pe.transpose(bank[4 + c % 2][:, k * P:(k + 1) * P], xT[:, t * P:(t + 1) * P],
                                                      ident[:, :])
                                mm.then_inc(tab_t, 1)
                            else:
                                pe.wait_ge(scaled, b + CHUNKS + c + 1)
                                pub_turn(pe, layer + 1, c, acc)

                        for c in range(CHUNKS + 4):
                            if c < CHUNKS:
                                conv(c)
                            if 1 <= c <= CHUNKS:
                                gate(c - 1)
                            if c >= 4:
                                turn(c - 4)

                    @block.scalar
                    def _(act):
                        for c in range(CHUNKS + 5):
                            if c < CHUNKS:
                                act.wait_ge(conv_mm, b + c + 1)
                                if b + c >= 2:
                                    act.wait_ge(state, b + c - 1)
                                act.activation(hid[c % 2][:, 0:wd(c)], bank[c % 2][:, 0:wd(c)], ACT.Identity,
                                               bias=bcols[:, layer:layer + 1]).then_inc(conv_ev, 1)
                            if 1 <= c <= CHUNKS:
                                act.wait_ge(gate_mm, b + c)
                                if b + c >= 3:
                                    act.wait_ge(mixed, b + c - 2)
                                act.activation(sca[(c - 1) % 2][:, 0:wd(c - 1)], bank[2 + (c - 1) % 2][:, 0:wd(c - 1)],
                                               ACT.Sigmoid, bias=bcols[:, LAYERS:LAYERS + 1]).then_inc(gate_ev, 1)
                            if c >= 5 and not last:
                                pub_rows(act, layer + 1, c - 5)

                    @block.vector
                    def _(dve):
                        if last:
                            dve.wait_ge(res_back, 16)
                        for c in range(CHUNKS + 5):
                            if c < CHUNKS:
                                h, m = hid[c % 2][:, 0:wd(c)], mix[c % 2][:, 0:wd(c)]
                                dve.wait_ge(conv_ev, b + c + 1)
                                dve.scalar_tensor_tensor(h, h, SLOPE, h, ALU.mult, ALU.max).then_inc(leaky, 1)
                                dve.wait_ge(leaky, b + c + 1)
                                dve.tensor_tensor(m, xT[:, cols(c)], h, ALU.subtract).then_inc(less, 1)
                            if 1 <= c <= CHUNKS:
                                d = c - 1
                                h, m, g = hid[d % 2][:, 0:wd(d)], mix[d % 2][:, 0:wd(d)], sca[d % 2][:, 0:wd(d)]
                                dve.wait_ge(gate_ev, b + d + 1)
                                dve.wait_ge(less, b + d + 1)
                                dve.tensor_tensor(m, m, g, ALU.mult).then_inc(mixed, 1)
                                dve.wait_ge(mixed, b + d + 1)
                                dve.tensor_tensor(xT[:, cols(d)], h, m, ALU.add).then_inc(state, 1)
                            if c >= 5 and last:
                                d = c - 5
                                k = chunk_tiles(d)
                                dve.wait_ge(tab_t, (LAYERS * CHUNKS) + d + 1)
                                if d >= 2:
                                    dve.wait_ge(final[d % 2], 16 * (d // 2))
                                dve.tensor_tensor(row_stage[d % 2][:, 0:k * P],
                                                  xres[:, d * CHUNK:d * CHUNK + k, :].rearrange("p t d -> p (t d)"),
                                                  bank[4 + d % 2][:, 0:k * P], ALU.add).then_inc(out_ev, 1)

                    @block.sync
                    def _(sp):
                        if last:
                            sp.dma_start(xres[:, :, :], res_dram.rearrange("t p d -> p t d")).then_inc(res_back, 16)
                        for c in range(CHUNKS):
                            if not last:
                                pub_store(sp, layer + 1, c)
                            elif c < CHUNKS - 1:
                                sp.wait_ge(out_ev, c + 1)
                                sp.dma_start(out[c * CHUNK * P:(c + 1) * CHUNK * P, :].rearrange("(t p) d -> p t d", p=P),
                                             row_stage[c % 2].rearrange("p (t d) -> p t d", t=CHUNK)).then_inc(final[c % 2], 16)
                            else:
                                sp.wait_ge(out_ev, c + 1)
                                sp.dma_start(out[(NODE_TILES - 1) * P:N, :], row_stage[c % 2][0:LAST, 0:D]).then_inc(final[c % 2], 16)
                        if last:
                            for k in range(2):
                                sp.wait_ge(final[k], 16 * len(range(k, CHUNKS, 2)))
                        else:
                            for k in range(2):
                                sp.wait_ge(row_out[k], 16 * stores_before(layer + 2, k))

            tab_t = sem("tab_t")
            row_ev = sem("row_ev")
            row_out = [sem(f"row_out{k}") for k in range(2)]
            row_stage = [work[:, 9, :], work[:, 10, :]]

            def stores_before(use, c):
                return use * len(range(c % 2, CHUNKS, 2)) + c // 2

            def pub_scale(pool, c):
                pool.tensor_tensor(acc[:, cols(c)], xT[:, cols(c)], inv_out[:, cols(c)], ALU.mult).then_inc(scaled, 1)

            def pub_turn(pe, use, c, src):
                if use * CHUNKS + c >= 2:
                    pe.wait_ge(row_ev, use * CHUNKS + c - 1)
                for k in range(chunk_tiles(c)):
                    t = c * CHUNK + k
                    mm = pe.transpose(bank[4 + c % 2][:, k * P:(k + 1) * P], src[:, t * P:(t + 1) * P], ident[:, :])
                mm.then_inc(tab_t, 1)

            def pub_rows(act, use, c):
                n = use * CHUNKS + c
                act.wait_ge(tab_t, n + 1)
                if stores_before(use, c):
                    act.wait_ge(row_out[c % 2], 16 * stores_before(use, c))
                act.activation(row_stage[c % 2][:, 0:chunk_tiles(c) * P], bank[4 + c % 2][:, 0:chunk_tiles(c) * P],
                               ACT.Copy).then_inc(row_ev, 1)

            def pub_store(sp, use, c):
                k = chunk_tiles(c)
                sp.wait_ge(row_ev, use * CHUNKS + c + 1)
                sp.dma_start(node_table[c * CHUNK * P:(c * CHUNK + k) * P, :].rearrange("(t p) d -> p t d", p=P),
                             row_stage[c % 2][:, 0:k * P].rearrange("p (t d) -> p t d", t=k)).then_inc(row_out[c % 2], 16)

            with nc.Block() as block:
                @block.sync
                def _(sp):
                    sp.dma_start(idx_src, src_idx).then_inc(tables_in, 16)
                    sp.wait_ge(out_deg, 4)
                    sp.dma_start(inv_dram[0, :].rearrange("(t p) -> t p", p=P), inv_rows[0:NODE_TILES, :]
                                 ).then_inc(tables_in, 16)
                    sp.wait_ge(tables_in, 32)
                    sp.dma_start(inv_out, inv_dram[0, :].partition_broadcast(P)).then_inc(tables_in, 16)
                    sp.dma_start(inv_in, inv_dram[1, :].partition_broadcast(P)).then_inc(tables_in, 16)
                    sp.wait_ge(tables_in, 64)

                @block.vector
                def _(dve):
                    def pair(i, first):
                        for k in range(2):
                            if not first:
                                dve.wait_ge(key_mm, i * 2 + (k - 1))
                            one_hots(bass.ds(i * 2 + k, 1), k)

                    def one_hots(column, k):
                        dve.tensor_scalar(hot_lo[:, 0, k, :], iota_h[:, 0:P], key_lo[:, column], None, ALU.is_equal)
                        dve.tensor_scalar(hot_hi[:, 0, k, :], iota_h[:, 0:50], key_hi[:, column], None,
                                          ALU.is_equal).then_inc(key_hot, 1)

                    dve.wait_ge(tables_in, 16)
                    dve.tensor_scalar(key_i, idx_src, P - 1, None, ALU.bitwise_and).then_inc(key_ready, 1)
                    dve.wait_ge(key_ready, 1)
                    dve.tensor_copy(key_lo, key_i).then_inc(key_ready, 1)
                    dve.wait_ge(key_ready, 2)
                    dve.tensor_scalar(key_i, idx_src, 7, None, ALU.arith_shift_right).then_inc(key_ready, 1)
                    dve.wait_ge(key_ready, 3)
                    dve.tensor_copy(key_hi, key_i).then_inc(key_ready, 1)
                    dve.wait_ge(key_ready, 4)
                    pair(0, True)
                    with dve.Fori(1, PAIRS) as i:
                        pair(i, False)
                    dve.wait_ge(key_mm, 2 * PAIRS - 1)
                    one_hots(slice(2 * PAIRS, 2 * PAIRS + 1), 0)
                    dve.wait_ge(key_mm, 2 * PAIRS + 1)
                    d = deg[:, 0, :]
                    dve.tensor_scalar(d, hist[:, 0:NODE_TILES], 1.0, 1.0, ALU.add, ALU.max).then_inc(out_deg, 1)
                    dve.wait_ge(out_deg, 2)
                    dve.reciprocal(d, d).then_inc(key_ready, 1)
                    dve.wait_ge(out_deg, 3)
                    dve.tensor_copy(inv_rows[0:NODE_TILES, :], bank[4][0:NODE_TILES, 0:P]).then_inc(out_deg, 1)

                @block.scalar
                def _(act):
                    act.wait_ge(out_deg, 1)
                    act.activation(deg[:, 0, :], deg[:, 0, :], ACT.Sqrt).then_inc(out_deg, 1)

                @block.tensor
                def _(pe):
                    def count(k, n, **flags):
                        pe.matmul(hist[:, 0:NODE_TILES], hot_lo[0:n, 0, k, :], hot_hi[0:n, 0, k, 0:NODE_TILES],
                                  skip_group_check=True, **flags).then_inc(key_mm, 1)

                    pe.wait_ge(key_hot, 1)
                    count(0, P, start=True, stop=False)
                    pe.wait_ge(key_hot, 2)
                    count(1, P, start=False, stop=False)
                    with pe.Fori(1, PAIRS) as i:
                        for k in range(2):
                            pe.wait_ge(key_hot, i * 2 + (k + 1))
                            count(k, P, start=False, stop=False)
                    pe.wait_ge(key_hot, 2 * PAIRS + 1)
                    count(0, LAST_EDGES, start=False, stop=True)
                    pe.wait_ge(key_ready, 5)
                    pe.transpose(bank[4][0:NODE_TILES, 0:P], deg[:, 0, :], ident[:, :]).then_inc(out_deg, 1)

                @block.gpsimd
                def _(pool):
                    pool.wait_ge(out_deg, 4)

            with nc.Block() as block:
                @block.gpsimd
                def _(pool):
                    for c in range(CHUNKS):
                        pub_scale(pool, c)

                @block.tensor
                def _(pe):
                    for c in range(CHUNKS):
                        pe.wait_ge(scaled, c + 1)
                        pub_turn(pe, 0, c, acc)

                @block.scalar
                def _(act):
                    for c in range(CHUNKS):
                        pub_rows(act, 0, c)

                @block.vector
                def _(dve):
                    dve.wait_ge(row_ev, CHUNKS)

                @block.sync
                def _(sp):
                    for c in range(CHUNKS):
                        pub_store(sp, 0, c)
                    for k in range(2):
                        sp.wait_ge(row_out[k], 16 * stores_before(1, k))

            def last_edges(layer):
                with nc.Block() as block:
                    @block.gpsimd
                    def _(pool):
                        for t in range(NODE_TILES):
                            pool.indirect_dma_start(rows_in[:, t, :], None, edge_rows,
                                                    bass.IndirectOffsetOnAxis(ap=idx_end[:, t:t + 1], axis=0)
                                                    ).then_inc(ends_in, 16)

                    @block.tensor
                    def _(pe):
                        pe.wait_ge(ends_in, 16 * NODE_TILES * (layer + 1))
                        for c in range(CHUNKS):
                            if layer * CHUNKS + c >= 2:
                                pe.wait_ge(acc_add, layer * CHUNKS + c - 1)
                            for k in range(chunk_tiles(c)):
                                mm = pe.transpose(bank[c % 2][:, k * P:(k + 1) * P], rows_in[:, c * CHUNK + k, :],
                                                  ident[:, :])
                            mm.then_inc(ends_t, 1)

                    @block.vector
                    def _(dve):
                        for c in range(CHUNKS):
                            dve.wait_ge(ends_t, layer * CHUNKS + c + 1)
                            dve.tensor_tensor(acc[:, cols(c)], acc[:, cols(c)], bank[c % 2][:, 0:chunk_tiles(c) * P],
                                              ALU.add).then_inc(acc_add, 1)

                    @block.scalar
                    def _(act):
                        act.wait_ge(acc_add, (layer + 1) * CHUNKS)

                    @block.sync
                    def _(sp):
                        sp.wait_ge(acc_add, (layer + 1) * CHUNKS)

            for layer in range(LAYERS):
                edge_pass(layer + 1, node_table, idx_src, keep_sum, (ALU.mult, ALU.add), False)
                last_edges(layer)
                update(layer)

        regs = nc.alloc_registers("overfull")
        nc.regs_load(regs, flag[0:1, 0:1])
        with nc.If_cmp(regs, 0, "IS_EQ"):
            dense_layers()
        with nc.Else():
            gather_layers()
        nc.all_engine_barrier()


def kernel(**inputs):
    import numpy as np
    import concourse.bacc as bacc
    from concourse.bass_utils import run_bass_kernel_spmd as run

    x, src, dst, rel = (np.asarray(inputs[k]) for k in ("x", "src", "dst", "edge_type_4"))

    def padded(a, fill, more=0):
        return np.concatenate([a, np.full(EDGE_ROWS * P - E + more, fill, a.dtype)])

    before = np.concatenate([np.full(1, -1, dst.dtype), dst[:-1]])
    after = np.concatenate([dst[1:], np.full(1, N, dst.dtype)])
    arrays = {"x": x}
    for name, a, fill in (("src", src, 0), ("rel", rel, 0), ("dst", dst, N), ("before", before, N), ("after", after, N)):
        arrays[name] = padded(a, fill).reshape(EDGE_ROWS, P)
    at = np.arange(WIN_ROWS)[:, None] * ALIGN + np.arange(WIN)
    arrays["windows"] = np.concatenate([padded(src, 0, WIN)[at], padded(dst, N, WIN)[at]], axis=1)
    for name, key in (("w0", "L0_gnn_weight"), ("b0", "L0_gnn_bias"), ("conv_w", "L1_gnn_conv_w"),
                      ("conv_b", "L1_gnn_conv_b"), ("gate_w1", "L1_gnn_gate_w1"),
                      ("gate_w2", "L1_gnn_gate_w2"), ("gate_b", "L1_gnn_gate_b")):
        arrays[name] = np.asarray(inputs[key])
    nc = bacc.Bacc("TRN2", target_bir_lowering=False, num_devices=1)
    arrays = {f"in_{k}": np.ascontiguousarray(a) for k, a in arrays.items()}
    args = [nc.dram_tensor(k, a.shape, mybir.dt.from_np(a.dtype), kind="ExternalInput").ap()
            for k, a in arrays.items()]
    out = nc.dram_tensor("out_x", (N, D), F32, kind="ExternalOutput").ap()
    build(nc, *args, out)
    r = run(nc, [arrays], core_ids=[0])
    return r.results[0]["out_x"]
```

```python
from contextlib import ExitStack

import concourse.bass as bass
from concourse import mybir

F32 = mybir.dt.float32
BF16 = mybir.dt.bfloat16
F16 = mybir.dt.float16
I32 = mybir.dt.int32
ALU = mybir.AluOpType
ACT = mybir.ActivationFunctionType
AX_X = mybir.AxisListType.X

P = 128
N = 6250
E = 106250
D = 128
RELS = 4
LAYERS = 4
NODE_TILES = -(-N // P)
NPAD = NODE_TILES * P
LAST = N - (NODE_TILES - 1) * P
EDGE_TILES = -(-E // P)
EDGE_ROWS = EDGE_TILES + 1
QUAD = 4
STEPS = 6
BODY = QUAD * STEPS
ITERS = -(-EDGE_TILES // BODY)
TILES = ITERS * BODY
IDXS = 2 * QUAD
BUFS = 3
TC = -(-(TILES + BODY) // P)
TPAD = TC * P
VN = NODE_TILES + 2
GW = 10
GPS = 3
GPB = STEPS * GPS
GROUPS = ITERS * GPB
GC = -(-GROUPS // P)
WIN = 2 * P
ALIGN = 32
ALIGN_SHIFT = 5
FAR = 1 << 20
OFFSET = 8192.0
WIN_ROWS = EDGE_ROWS * P // ALIGN
CW = 450
CG = CW // GW
PB = 2 * CG // GPB
HB = PB // 2
PARTS = 1 + HB * STEPS // 2
PT = NODE_TILES // PARTS
CHUNKS_A = GROUPS // CG
CHUNK = 4
CHUNKS = -(-NODE_TILES // CHUNK)
ZERO_ROW = NPAD * RELS
ZERO_EDGE = TILES * P
BIG = 3.3895313892515355e38
EPS = 1e-5
LN_MAX = 11.4
LO_SCALE = 4096.0
FP16_TOP = 2.0 ** 14
SCALE_0 = 1024.0
BOUND_MAX = 1e30
EXPONENT = 0x7F800000
SLOPE = 0.01
W4 = QUAD * P
NW = NODE_TILES * GW
S_A = 25
assert STEPS % BUFS == 0 and 2 * CG == PB * GPB and CHUNKS_A * CG == GROUPS and GROUPS * GW >= N and TPAD >= TILES + BODY
assert PB % 2 == 1 and GPB % 2 == 0 and CHUNKS_A % 2 == 0 and PARTS * PT == NODE_TILES


def chunk_tiles(c):
    return min(CHUNK, NODE_TILES - c * CHUNK)


def tiles_done(c):
    return NODE_TILES if c == CHUNKS_A else c * CW // P


def build(nc, x, src_in, rel_in, dst_in, before_in, after_in, windows, w0, b0, conv_w, conv_b,
          gate_w1, gate_w2, gate_b, out):
    with ExitStack() as ctx:
        def sb(name, shape, dt):
            return ctx.enter_context(nc.sbuf_tensor(name, shape, dt))

        def sem(name):
            return ctx.enter_context(nc.semaphore(name))

        def dram(name, shape, dt):
            return nc.dram_tensor(name, shape, dt, kind="Internal").ap()

        msg_table = dram("msg_table", (ZERO_ROW + P, D), F32)
        node_table = dram("node_table", (NPAD, D), F32)
        edge_rows = dram("edge_rows", (ZERO_EDGE + P, D), F32)
        keep_max = dram("keep_max", (TPAD, P), BF16)
        keep_sum = dram("keep_sum", (TPAD, P), BF16)
        bounds = dram("bounds", (VN, P), I32)
        src_idx = dram("src_idx", (P, TPAD), I32)
        adj = dram("adj", (CHUNKS_A, P, NODE_TILES, CW), F16)
        inv_dram = dram("inv_dram", (2, NPAD), F32)
        res_dram = dram("res_dram", (NODE_TILES, P, D), F32)

        xT = sb("xT", [P, NPAD], F32)
        ident = sb("ident", [P, P], F32)
        conv_sb = sb("conv_sb", [P, LAYERS, D], F32)
        g1T = sb("g1T", [P, D], F32)
        g2T = sb("g2T", [P, D], F32)
        bcols = sb("bcols", [P, LAYERS + 1], F32)
        mv = sb("mv", [P, NODE_TILES, 2], F32)
        rstd = sb("rstd", [P, NODE_TILES], F32)
        nmr = sb("nmr", [P, NODE_TILES], F32)
        deg = sb("deg", [P, 2, NODE_TILES], F32)
        idx_end = sb("idx_end", [P, NODE_TILES], I32)
        idx_buf = sb("idx_buf", [P, BODY // IDXS, IDXS], I32)
        flag = sb("flag", [1, 1], I32)
        arena = sb("arena", [P, 44600], F32)

        class Region:

            def __init__(self, at=0):
                self.at = at

            def take(self, words):
                self.at += words
                assert self.at <= 44600, self.at
                return arena[:, self.at - words:self.at]

        bank = [ctx.enter_context(nc.psum_tensor(f"bank{i}", [P, 512], F32)) for i in range(8)]

        R = Region()
        stage = R.take(NODE_TILES * CW).bitcast(F16).rearrange("p (b s w) -> p b s w", b=2, s=NODE_TILES)
        xres = R.take(NODE_TILES * D).rearrange("p (t d) -> p t d", t=NODE_TILES)
        xres_end = R.at
        keyt = R.take(GC * P * 6).rearrange("p (g w k) -> p g w k", w=2, k=3)
        idx_msg = R.take(TPAD).bitcast(I32)
        iota_h = R.take(256).bitcast(F16)
        ring = R.take(BODY * D).rearrange("p (t d) -> p t d", t=BODY)
        scanned_at = R.at
        scanned = R.take(BUFS * W4).rearrange("p (s w) -> p s w", s=BUFS)
        ends = R.take(BUFS * W4).rearrange("p (s w) -> p s w", s=BUFS)
        flags = R.take(STEPS * W4 // 2).bitcast(BF16).rearrange("p (s w) -> p s w", s=STEPS)
        hot_at = R.at
        hot_col = R.take(GPS * 2 * NW // 2).bitcast(BF16).rearrange("p (g w n) -> p g w n", g=GPS, w=2)
        hot_lo = R.take(GPS * 2 * P // 2).bitcast(BF16).rearrange("p (g w n) -> p g w n", g=GPS, w=2)
        hot_hi = R.take(GPS * 2 * 50 // 2).bitcast(BF16).rearrange("p (g w n) -> p g w n", g=GPS, w=2)
        s_tiles = sem("s_tiles")
        s_load = sem("s_load")
        s_gates = sem("s_gates")
        s_const = sem("s_const")
        s_dve = sem("s_dve")
        s_scr = sem("s_scr")
        step_dve = sem("step_dve")
        step_pe = sem("step_pe")
        step_ev = sem("step_ev")
        chain = [0]

        def link(dve, ins):
            chain[0] += 1
            ins.then_inc(s_dve, 1)
            dve.wait_ge(s_dve, chain[0])

        S = Region()
        tab = S.take(5 * TPAD).bitcast(I32).rearrange("p (k c e) -> p k c e", k=5, c=TC)
        f_a, f_b, f_c, f_d = (S.take(TPAD).rearrange("p (c e) -> p c e", c=TC) for _ in range(4))
        keep_m = S.take(TPAD // 2).bitcast(BF16).rearrange("p (c e) -> p c e", c=TC)
        keep_s = S.take(TPAD // 2).bitcast(BF16).rearrange("p (c e) -> p c e", c=TC)
        src_t = S.take(TPAD).bitcast(I32)
        first_lo = S.take(TC).bitcast(I32)
        first_hi = S.take(TC).bitcast(I32)
        gload = S.take(2 * D).rearrange("p (k d) -> p k d", k=2)
        setup2_at = S.at
        S = Region(0)
        brow_at = S.take(VN * P).bitcast(I32).rearrange("p (t e) -> p t e", t=VN)
        S2 = Region(setup2_at)
        node = S2.take(VN)
        first_f = S2.take(2 * TC).rearrange("p (k c) -> p k c", k=2)
        hot_first = S2.take(TC * P // 2).bitcast(BF16).rearrange("p (c n) -> p c n", c=TC)
        hot_block = S2.take(TC * 52 // 2).bitcast(BF16).rearrange("p (c n) -> p c n", c=TC)
        below = S2.take(P)
        ones_f = S2.take(P)
        firsts = S2.take(VN)
        total = S2.take(VN)
        run = S2.take(VN)
        tcount = S2.take(VN)
        trow = S2.take(VN).bitcast(I32)
        inner = S2.take(VN)
        bnd = S2.take(VN)
        bnd_i = S2.take(P).bitcast(I32)
        nxt = S2.take(NODE_TILES).bitcast(I32)
        g_lo = S2.take(GC).bitcast(I32)
        g_hi = S2.take(GC).bitcast(I32)
        g_id = S2.take(GC)
        g_row = S2.take(GC).bitcast(I32)
        g_tmp = S2.take(4 * GC).rearrange("p (k c) -> p k c", k=4)
        over = S2.take(2)
        f_deg = S2.take(2 * NODE_TILES).rearrange("p (k t) -> p k t", k=2)
        hit = S2.take(VN * P).rearrange("p (t e) -> p t e", t=VN)
        w_d, w_e = (S2.take(GC * WIN).rearrange("p (c e) -> p c e", c=GC) for _ in range(2))
        S = Region(0)
        win = S.take(GC * 2 * WIN).bitcast(I32).rearrange("p (c k e) -> p c k e", c=GC, k=2)
        hit_flat = hit.rearrange("p t e -> p (t e)")
        hi_i, lo_i = (hit_flat[:, k * GC * WIN:(k + 1) * GC * WIN].bitcast(I32)
                      .rearrange("p (c e) -> p c e", c=GC) for k in range(2))
        w_a, w_b, w_c = (hit_flat[:, k * GC * WIN:(k + 1) * GC * WIN].rearrange("p (c e) -> p c e", c=GC)
                         for k in (2, 3, 4))
        assert VN * P <= setup2_at and S2.at <= NODE_TILES * CW and 5 * GC * WIN <= VN * P, S2.at

        firsts_hot = sem("firsts_hot")
        firsts_mm = sem("firsts_mm")
        firsts_ev = sem("firsts_ev")
        rows_known = sem("rows_known")
        s_dst = sem("s_dst")
        FULL = EDGE_ROWS // P
        with nc.Block() as block:
            @block.sync
            def _(sp):
                sp.wait_ge(s_const, 1)
                for k, t in ((2, dst_in), (0, src_in), (1, rel_in), (3, before_in), (4, after_in)):
                    arrived = s_dst if k == 2 else s_tiles
                    sp.dma_start(tab[:, k, 0:FULL, :],
                                 t[0:FULL * P, :].rearrange("(c p) e -> p c e", p=P)).then_inc(arrived, 16)
                    sp.dma_start(tab[0:EDGE_ROWS - FULL * P, k, FULL, :],
                                 t[FULL * P:EDGE_ROWS, :]).then_inc(arrived, 16)
                sp.dma_start(gload[:, 0, :], gate_w1).then_inc(s_gates, 16)
                sp.dma_start(gload[:, 1, :], gate_w2).then_inc(s_gates, 16)
                sp.dma_start(xres[:, 0:NODE_TILES - 1, :],
                             x[0:(NODE_TILES - 1) * P, :].rearrange("(t p) d -> p t d", p=P)).then_inc(s_load, 16)
                sp.dma_start(xres[0:LAST, NODE_TILES - 1, :], x[(NODE_TILES - 1) * P:N, :]).then_inc(s_load, 16)
                sp.dma_start(conv_sb[:, :, :], conv_w.rearrange("l i o -> i l o")).then_inc(s_load, 16)
                with nc.allow_non_contiguous_dma(reason="five bias columns"):
                    for l in range(LAYERS):
                        sp.dma_start(bcols[:, l:l + 1], conv_b[l, :].unsqueeze(1)).then_inc(s_load, 16)
                    sp.dma_start(bcols[:, LAYERS:LAYERS + 1], gate_b.unsqueeze(1)).then_inc(s_load, 16)
                sp.wait_ge(step_dve, 1)
                sp.dma_start(keep_max.rearrange("(c p) e -> p c e", p=P), keep_m).then_inc(s_scr, 16)
                sp.dma_start(keep_sum.rearrange("(c p) e -> p c e", p=P), keep_s).then_inc(s_scr, 16)
                sp.wait_ge(step_ev, TC)
                sp.dma_start(src_idx, src_t).then_inc(s_scr, 16)
                sp.wait_ge(s_scr, 48)
                sp.wait_ge(s_load, 16 * 8)

            @block.gpsimd
            def _(pool):
                pool.memset(tab[:, 0:2, TC - 1, :], 0)
                pool.memset(tab[:, 2:5, TC - 1, :], N)
                pool.memset(xres[:, NODE_TILES - 1, :], 0.0).then_inc(s_const, 1)
                pool.memset(ident[:, :], 0.0).then_inc(s_const, 1)
                pool.iota(iota_h, [[1, 512]], base=0, channel_multiplier=0, allow_small_or_imprecise_dtypes=True)
                pool.iota(node, [[P, VN]], base=0, channel_multiplier=1, allow_small_or_imprecise_dtypes=True)
                pool.iota(g_id, [[P, GC]], base=0, channel_multiplier=1,
                          allow_small_or_imprecise_dtypes=True).then_inc(s_const, 1)
                pool.wait_ge(s_const, 2)
                pool.affine_select(out=ident[:, :], in_=ident[:, :], compare_op=ALU.not_equal, fill=1.0,
                                   base=0, pattern=[[-1, P]], channel_multiplier=1).then_inc(s_const, 1)

            @block.vector
            def _(dve):
                def L(ins):
                    link(dve, ins)

                src, rel, dst, before, after = (tab[:, k, :, :] for k in range(5))
                def dst_row_indices():
                    dve.wait_ge(s_const, 4)
                    dve.wait_ge(s_dst, 32)
                    L(dve.tensor_scalar(first_lo, dst[:, :, 0], P - 1, None, ALU.bitwise_and))
                    L(dve.tensor_scalar(first_hi, dst[:, :, 0], 7, None, ALU.arith_shift_right))
                    L(dve.tensor_copy(first_f[:, 0, :], first_lo))
                    L(dve.tensor_copy(first_f[:, 1, :], first_hi))
                    for c in range(TC):
                        dve.tensor_scalar(hot_first[:, c, :], iota_h[:, 0:P], first_f[:, 0, c:c + 1], None, ALU.is_equal)
                        ins = dve.tensor_scalar(hot_block[:, c, :], iota_h[:, 0:52], first_f[:, 1, c:c + 1], None,
                                                ALU.is_equal)
                    dve.tensor_scalar(below, iota_h[:, 0:P], node[:, 0:1], None, ALU.is_gt)
                    dve.memset(ones_f, 1.0).then_inc(firsts_hot, 1)
                    dve.wait_ge(firsts_mm, 1)
                    dve.tensor_copy(firsts, bank[6][:, 0:VN]).then_inc(firsts_ev, 1)
                    dve.wait_ge(firsts_mm, 2)
                    L(dve.tensor_copy(total, bank[7][:, 64:64 + VN]))
                    L(dve.tensor_tensor_scan(run, ones_f[:, 0:VN], total, 0.0, ALU.mult, ALU.add))
                    L(dve.tensor_tensor(run, run, total, ALU.subtract))
                    L(dve.tensor_tensor(tcount, run, bank[7][:, 0:VN], ALU.add))
                    L(dve.tensor_scalar(tcount, tcount, float(EDGE_TILES), None, ALU.min))
                    L(dve.tensor_scalar(inner, tcount, 1.0, 0.0, ALU.subtract, ALU.max))
                    dve.tensor_copy(trow, inner).then_inc(rows_known, 1)

                dst_row_indices()
                dve.wait_ge(s_tiles, 128)
                L(dve.tensor_tensor(f_a, before, dst, ALU.is_equal))
                L(dve.tensor_copy(keep_s, f_a))
                L(dve.tensor_scalar(f_b, f_a, 2.0, 1.0, ALU.mult, ALU.subtract))
                dve.tensor_scalar(keep_m, f_b, BIG, None, ALU.mult).then_inc(step_dve, 1)
                L(dve.scalar_tensor_tensor(f_a, src, float(RELS), rel, ALU.mult, ALU.add))
                L(dve.tensor_scalar(f_c, rel, 0.0, None, ALU.is_ge))
                L(dve.scalar_tensor_tensor(f_d, rel, float(RELS - 1), f_c, ALU.is_le, ALU.mult))
                L(dve.scalar_tensor_tensor(f_c, f_a, float(ZERO_ROW), f_d, ALU.subtract, ALU.mult))
                L(dve.tensor_scalar(f_a, f_c, float(ZERO_ROW), None, ALU.add))
                dve.tensor_copy(f_d, src).then_inc(step_dve, 1)
                for c in range(TC):
                    dve.wait_ge(step_pe, c + 1)
                    dve.tensor_copy(idx_msg[:, c * P:(c + 1) * P], bank[2 + c % 2][:, 0:P])
                    dve.tensor_copy(src_t[:, c * P:(c + 1) * P], bank[2 + c % 2][:, P:2 * P]).then_inc(step_ev, 1)
                dve.wait_ge(step_pe, TC + 1)
                dve.tensor_copy(g1T[:, :], bank[4][:, 0:P])
                dve.tensor_copy(g2T[:, :], bank[4][:, P:2 * P])

            @block.tensor
            def _(pe):
                pe.wait_ge(s_const, 4)
                pe.wait_ge(firsts_hot, 1)
                for c in range(TC):
                    mm = pe.matmul(bank[6][:, 0:VN], hot_first[:, c, :], hot_block[:, c, 0:VN],
                                   start=(c == 0), stop=(c == TC - 1))
                mm.then_inc(firsts_mm, 1)
                pe.wait_ge(firsts_ev, 1)
                pe.matmul(bank[7][:, 0:VN], below, firsts, start=True, stop=True)
                pe.matmul(bank[7][:, 64:64 + VN], ones_f, firsts, start=True, stop=True).then_inc(firsts_mm, 1)
                pe.wait_ge(step_dve, 2)
                for c in range(TC):
                    if c >= 2:
                        pe.wait_ge(step_ev, c - 1)
                    pe.transpose(bank[2 + c % 2][:, 0:P], f_a[:, c, :], ident[:, :])
                    pe.transpose(bank[2 + c % 2][:, P:2 * P], f_d[:, c, :], ident[:, :]).then_inc(step_pe, 1)
                pe.wait_ge(s_gates, 32)
                pe.transpose(bank[4][:, 0:P], gload[:, 0, :], ident[:, :])
                pe.transpose(bank[4][:, P:2 * P], gload[:, 1, :], ident[:, :]).then_inc(step_pe, 1)

        ln_stat = sem("ln_stat")
        ln_tiles = sem("ln_tiles")
        ln_rows = sem("ln_rows")
        ln_t = sem("ln_t")
        ln_ev = sem("ln_ev")
        S = Region(scanned_at)
        stats = S.take(NODE_TILES * 6).rearrange("p (t k) -> p t k", k=6)
        rows = [S.take(W4).rearrange("p (t d) -> p t d", t=CHUNK) for _ in range(2)]
        tstage = [S.take(W4) for _ in range(4)]
        zrow = S.take(P)
        w0_sb = S.take((RELS + 1) * D).rearrange("p (r d) -> p r d", r=RELS + 1)
        brow = S.take((RELS + 1) * D)

        def ln_dve_stats(dve, use):
            base = use * 5
            for t in range(NODE_TILES):
                dve.bn_stats(stats[:, t, :], xres[:, t, :]).then_inc(ln_tiles, 1)
            dve.wait_ge(ln_tiles, (use + 1) * NODE_TILES)
            for t in range(NODE_TILES):
                last = dve.bn_aggr(mv[:, t, :], stats[:, t, :])
            last.then_inc(ln_stat, 1)
            dve.wait_ge(ln_stat, base + 1)
            dve.tensor_scalar(rstd[:, :], mv[:, :, 1], EPS, None, ALU.add).then_inc(ln_stat, 1)
            dve.wait_ge(ln_stat, base + 3)
            dve.reciprocal(rstd[:, :], rstd[:, :]).then_inc(ln_stat, 1)
            dve.wait_ge(ln_stat, base + 4)
            dve.scalar_tensor_tensor(nmr[:, :], mv[:, :, 0], -1.0, rstd[:, :], ALU.mult, ALU.mult
                                     ).then_inc(ln_stat, 1)

        def ln_act(act, use):
            base = use * 5
            act.wait_ge(ln_stat, base + 2)
            act.activation(rstd[:, :], rstd[:, :], ACT.Sqrt).then_inc(ln_stat, 1)
            act.wait_ge(ln_stat, base + 5)

        def ln_act_rows(act, use, c):
            if c >= 2:
                act.wait_ge(ln_t, use * CHUNKS + c - 1)
            for k in range(chunk_tiles(c)):
                t = c * CHUNK + k
                last = act.activation(rows[c % 2][:, k, :], xres[:, t, :], ACT.Relu,
                                      bias=nmr[:, t:t + 1], scale=rstd[:, t:t + 1])
            last.then_inc(ln_rows, 1)

        def ln_pe(pe, use, c):
            pe.wait_ge(ln_rows, use * CHUNKS + c + 1)
            if c >= 2:
                pe.wait_ge(ln_ev, use * CHUNKS + c - 1)
            for k in range(chunk_tiles(c)):
                mm = pe.transpose(bank[c % 2][:, k * P:(k + 1) * P], rows[c % 2][:, k, :], ident[:, :])
            mm.then_inc(ln_t, 1)

        def cols(c):
            return slice(c * CHUNK * P, c * CHUNK * P + chunk_tiles(c) * P)

        def ln_dve_cols(dve, use, c):
            dve.wait_ge(ln_t, use * CHUNKS + c + 1)
            dve.tensor_copy(xT[:, cols(c)], bank[c % 2][:, 0:chunk_tiles(c) * P]).then_inc(ln_ev, 1)

        tab_mm = sem("tab_mm")
        tab_ev = sem("tab_ev")
        tab_out = [sem(f"tab_out{k}") for k in range(4)]
        zero_out = sem("zero_out")
        s_w0 = sem("s_w0")
        self_mm = sem("self_mm")
        self_ev = sem("self_ev")
        dst_rows = sem("dst_rows")
        bnd_done = sem("bnd_done")
        bnd_t = sem("bnd_t")
        bnd_ev = sem("bnd_ev")
        bnd_out = sem("bnd_out")
        bnd_back = sem("bnd_back")
        win_known = sem("win_known")
        over_t = sem("over_t")
        windows_in = sem("windows_in")
        keys_done = sem("keys_done")
        keys_t = sem("keys_t")
        keys_ev = sem("keys_ev")
        AT_BOUNDS, AT_BOUNDS_EV, AT_WINDOWS, AT_FLAG = 7, 8, 11, 12
        with nc.Block() as block:
            @block.sync
            def _(sp):
                sp.dma_start(w0_sb, w0.rearrange("r i o -> i r o")).then_inc(s_w0, 16)
                sp.dma_start(brow, b0.rearrange("r d -> (r d)").partition_broadcast(P)).then_inc(s_w0, 16)
                sp.wait_ge(zero_out, 1)
                sp.dma_start(msg_table[ZERO_ROW:ZERO_ROW + P, :], zrow).then_inc(s_scr, 16)
                sp.dma_start(edge_rows[ZERO_EDGE:ZERO_EDGE + P, :], zrow).then_inc(s_scr, 16)
                for t in range(NODE_TILES):
                    sp.wait_ge(tab_ev, t + 1)
                    sp.dma_start(msg_table[t * P * RELS:(t + 1) * P * RELS, :].rearrange("(p r) d -> p (r d)", r=RELS),
                                 tstage[t % 4]).then_inc(tab_out[t % 4], 16)
                for k in range(4):
                    sp.wait_ge(tab_out[k], 16 * len(range(k, NODE_TILES, 4)))
                sp.wait_ge(s_scr, 80)

            @block.gpsimd
            def _(pool):
                pool.wait_ge(rows_known, 1)
                for t in range(VN):
                    pool.indirect_dma_start(brow_at[:, t, :], None, dst_in,
                                            bass.IndirectOffsetOnAxis(ap=trow[:, t:t + 1], axis=0)
                                            ).then_inc(dst_rows, 16)
                pool.wait_ge(bnd_ev, 1)
                pool.dma_start(bounds, bnd_i[0:VN, :]).then_inc(bnd_out, 16)
                pool.wait_ge(bnd_out, 16)
                flat = bounds.rearrange("t p -> (t p)")
                with nc.allow_non_contiguous_dma(reason="bounds in node-major and group-major layout"):
                    pool.dma_start(nxt, flat[1:1 + NPAD].rearrange("(t p) -> p t", p=P)).then_inc(bnd_back, 16)
                    pool.dma_start(g_lo, flat[0:GC * P * GW].rearrange("(c p g) -> p c g", p=P, g=GW)[:, :, 0]
                                   ).then_inc(bnd_back, 16)
                    pool.dma_start(g_hi, flat[GW:GW + GC * P * GW].rearrange("(c p g) -> p c g", p=P, g=GW)[:, :, 0]
                                   ).then_inc(bnd_back, 16)
                pool.wait_ge(win_known, 1)
                for c in range(GC):
                    pool.indirect_dma_start(win[:, c, :, :].rearrange("p k e -> p (k e)"), None, windows,
                                            bass.IndirectOffsetOnAxis(ap=g_row[:, c:c + 1], axis=0)
                                            ).then_inc(windows_in, 16)
                pool.wait_ge(self_ev, CHUNKS)
                xa = xres[:, :, :]
                pool.tensor_tensor(xa, xa, brow[:, RELS * D:].unsqueeze(1).to_broadcast([P, NODE_TILES, D]), ALU.add)

            @block.vector
            def _(dve):
                def L(ins):
                    link(dve, ins)

                def node_bounds():
                    dve.wait_ge(dst_rows, 16 * VN)
                    L(dve.tensor_tensor(hit, brow_at, node.unsqueeze(2).to_broadcast([P, VN, P]), ALU.is_lt))
                    L(dve.tensor_reduce(bnd, hit, AX_X, ALU.add))
                    dve.scalar_tensor_tensor(bnd, inner, float(P), bnd, ALU.mult, ALU.add).then_inc(bnd_done, 1)

                def node_bounds_out():
                    dve.wait_ge(bnd_t, 1)
                    dve.tensor_copy(bnd_i[0:VN, :], bank[6][0:VN, 0:P]).then_inc(bnd_ev, 1)

                def degrees_and_windows():
                    dve.wait_ge(bnd_back, 48)
                    L(dve.tensor_tensor(deg[:, 1, :], nxt, bnd[:, 0:NODE_TILES], ALU.subtract))
                    L(dve.tensor_scalar(f_deg[:, 0, :], deg[:, 1, :], 0.0, None, ALU.is_gt))
                    L(dve.scalar_tensor_tensor(f_deg[:, 1, :], nxt, float(ZERO_EDGE + 1), f_deg[:, 0, :],
                                               ALU.subtract, ALU.mult))
                    L(dve.tensor_scalar(idx_end[:, :], f_deg[:, 1, :], float(ZERO_EDGE), None, ALU.add))
                    L(dve.tensor_scalar(g_row, g_lo, ALIGN_SHIFT, None, ALU.arith_shift_right))
                    L(dve.scalar_tensor_tensor(g_tmp[:, 0, :], g_row, float(-ALIGN), g_hi, ALU.mult, ALU.add))
                    L(dve.tensor_scalar(g_tmp[:, 1, :], g_id, float(N // GW), None, ALU.is_lt))
                    L(dve.scalar_tensor_tensor(g_tmp[:, 2, :], g_tmp[:, 0, :], float(WIN), g_tmp[:, 1, :],
                                               ALU.is_gt, ALU.mult))
                    L(dve.tensor_reduce(over[:, 0:1], g_tmp[:, 2, :], AX_X, ALU.max))
                    L(dve.tensor_scalar(g_tmp[:, 3, :], g_row, float(WIN_ROWS - 1), None, ALU.min))
                    dve.tensor_copy(g_row, g_tmp[:, 3, :]).then_inc(win_known, 1)

                def overflow_flag():
                    dve.wait_ge(over_t, 1)
                    dve.tensor_reduce(flag[:, :], bank[7][0:1, 0:P], AX_X, ALU.max)

                def one_hot_keys():
                    def wide(v):
                        return v.unsqueeze(2).to_broadcast([P, GC, WIN])

                    src, dst = win[:, :, 0, :], win[:, :, 1, :]
                    L(dve.tensor_scalar(g_tmp[:, 0, :], g_id, float(GW), None, ALU.mult))
                    dve.wait_ge(windows_in, 16 * GC)
                    L(dve.tensor_tensor(w_a, dst, wide(g_tmp[:, 0, :]), ALU.subtract))
                    L(dve.tensor_scalar(w_d, w_a, 0.0, None, ALU.is_ge))
                    L(dve.scalar_tensor_tensor(w_e, w_a, float(GW), w_d, ALU.is_lt, ALU.mult))
                    L(dve.tensor_scalar(hi_i, src, 7, None, ALU.arith_shift_right))
                    L(dve.tensor_scalar(lo_i, src, P - 1, None, ALU.bitwise_and))
                    L(dve.scalar_tensor_tensor(w_d, hi_i, float(GW), w_a, ALU.mult, ALU.add))
                    L(dve.scalar_tensor_tensor(w_a, w_e, OFFSET, w_d, ALU.mult, ALU.add))
                    L(dve.scalar_tensor_tensor(w_b, w_e, OFFSET, lo_i, ALU.mult, ALU.add))
                    dve.scalar_tensor_tensor(w_c, w_e, OFFSET, hi_i, ALU.mult, ALU.add).then_inc(keys_done, 1)

                def table(c):
                    for k in range(chunk_tiles(c)):
                        t = c * CHUNK + k
                        dve.wait_ge(tab_mm, t + 1)
                        if t >= 4:
                            dve.wait_ge(tab_out[t % 4], 16 * (t // 4))
                        dve.tensor_tensor(tstage[t % 4], bank[2 + t % 2][:, :], brow[:, 0:RELS * D],
                                          ALU.add).then_inc(tab_ev, 1)

                def self_term(c):
                    k = chunk_tiles(c)
                    dve.wait_ge(self_mm, c + 1)
                    xc = xres[:, c * CHUNK:c * CHUNK + k, :].rearrange("p t d -> p (t d)")
                    dve.tensor_tensor(xc, xc, bank[4 + c % 2][:, 0:k * P], ALU.add).then_inc(self_ev, 1)

                dve.memset(zrow, 0.0).then_inc(zero_out, 1)
                ln_dve_stats(dve, 0)
                dve.wait_ge(s_w0, 32)
                for c in range(CHUNKS):
                    if c == AT_BOUNDS:
                        node_bounds()
                    if c == AT_BOUNDS_EV:
                        node_bounds_out()
                    if c == AT_WINDOWS:
                        degrees_and_windows()
                    if c == AT_FLAG:
                        overflow_flag()
                    ln_dve_cols(dve, 0, c)
                    if c:
                        table(c - 1)
                        self_term(c - 1)
                table(CHUNKS - 1)
                self_term(CHUNKS - 1)
                one_hot_keys()

            @block.scalar
            def _(act):
                ln_act(act, 0)
                for c in range(CHUNKS):
                    ln_act_rows(act, 0, c)
                for c in range(GC):
                    for w in range(2):
                        n = 2 * c + w
                        act.wait_ge(keys_t, n + 1)
                        act.activation(keyt[:, c * P:(c + 1) * P, w, :].rearrange("p g k -> p k g"),
                                       bank[6 + n % 2][:, 0:3 * P].rearrange("p (k g) -> p k g", k=3),
                                       ACT.Copy, bias=-OFFSET).then_inc(keys_ev, 1)

            @block.tensor
            def _(pe):
                def products(c):
                    pe.wait_ge(ln_ev, c + 1)
                    if c >= 2:
                        pe.wait_ge(self_ev, c - 1)
                    for k in range(chunk_tiles(c)):
                        t = c * CHUNK + k
                        if t >= 2:
                            pe.wait_ge(tab_ev, t - 1)
                        pe.matmul(bank[2 + t % 2][:, :], xT[:, t * P:(t + 1) * P],
                                  w0_sb[:, 0:RELS, :].rearrange("p r d -> p (r d)"),
                                  start=True, stop=True).then_inc(tab_mm, 1)
                    for k in range(chunk_tiles(c)):
                        t = c * CHUNK + k
                        mm = pe.matmul(bank[4 + c % 2][:, k * P:(k + 1) * P], xT[:, t * P:(t + 1) * P],
                                       w0_sb[:, RELS, :], start=True, stop=True)
                    mm.then_inc(self_mm, 1)

                pe.wait_ge(s_w0, 32)
                for c in range(CHUNKS):
                    if c == AT_BOUNDS + 1:
                        pe.wait_ge(bnd_done, 1)
                        pe.transpose(bank[6][0:VN, 0:P], bnd, ident[:, :]).then_inc(bnd_t, 1)
                    if c == AT_WINDOWS:
                        pe.wait_ge(win_known, 1)
                        pe.transpose(bank[7][0:1, 0:P], over[:, 0:1], ident[:, :]).then_inc(over_t, 1)
                    ln_pe(pe, 0, c)
                    if c:
                        products(c - 1)
                products(CHUNKS - 1)
                pe.wait_ge(keys_done, 1)
                for c in range(GC):
                    for w in range(2):
                        n = 2 * c + w
                        if n >= 2:
                            pe.wait_ge(keys_ev, n - 1)
                        for k, t in enumerate((w_a, w_b, w_c)):
                            mm = pe.transpose(bank[6 + n % 2][:, k * P:(k + 1) * P], t[:, c, w * P:(w + 1) * P],
                                              ident[:, :])
                        mm.then_inc(keys_t, 1)

        landed = [sem(f"landed{s}") for s in range(BODY)]
        idx_ready = sem("idx_ready")
        thirds = sem("thirds")
        flags_in = [sem(f"flags_in{s}") for s in range(STEPS)]
        turned = sem("turned")
        scan_done = sem("scan_done")
        back = sem("back")
        evac = sem("evac")
        rows_out = [sem(f"rows_out{b}") for b in range(BUFS)]
        hot_ready = sem("hot_ready")
        slab_mm = sem("slab_mm")
        slab_ev = sem("slab_ev")
        chunk_out = [sem(f"chunk_out{h}") for h in range(2)]
        hist_zero = sem("hist_zero")
        hist = bank[7]
        THIRDS = BODY // IDXS

        def landed_before(use, slot):
            return 16 * (use * ITERS + (chunk_tiles(slot) if use and slot < CHUNKS else 0))

        def edge_pass(use, table, idx, keep, ops, adjacency):
            ibase = use * ITERS
            sbase = ibase * STEPS

            with nc.Block() as block:
                @block.gpsimd
                def _(pool):
                    with pool.Fori(0, ITERS) as i:
                        for q in range(THIRDS):
                            pool.wait_ge(idx_ready, i * THIRDS + (q + 1 + use * (ITERS + 1) * THIRDS))
                            pool.sem_inc(thirds, 1)
                            for j in range(IDXS):
                                slot = q * IDXS + j
                                pool.indirect_dma_start(ring[:, slot, :], None, table,
                                                        bass.IndirectOffsetOnAxis(ap=idx_buf[:, q, j:j + 1], axis=0)
                                                        ).then_inc(landed[slot], 16)

                @block.sync
                def _(sp):
                    def load_flags(i, s):
                        v = keep[bass.ds(i * BODY + s * QUAD, QUAD), :].rearrange("v e -> (v e)")
                        sp.dma_start(flags[:, s, :], v.partition_broadcast(P)).then_inc(flags_in[s], 16)

                    for s in range(STEPS):
                        load_flags(0, s)
                    with sp.Fori(0, ITERS) as i:
                        for s in range(STEPS):
                            sp.wait_ge(evac, i * STEPS + (s + 1 + sbase))
                            rows_at = edge_rows[bass.ds(i * (BODY * P) + s * W4, W4), :]
                            sp.dma_start(rows_at.rearrange("(t p) d -> p t d", p=P),
                                         ends[:, s % BUFS, :].rearrange("p (t d) -> p t d", t=QUAD)
                                         ).then_inc(rows_out[s % BUFS], 16)
                            load_flags(i + 1, s)
                    for b in range(BUFS):
                        sp.wait_ge(rows_out[b], 16 * (use + 1) * ITERS * STEPS // BUFS)
                    for s in range(STEPS):
                        sp.wait_ge(flags_in[s], 16 * (use + 1) * (ITERS + 1))

                @block.scalar
                def _(act):
                    def copy_idx(i, q):
                        act.activation(idx_buf[:, q, :], idx[:, bass.ds(i * BODY + q * IDXS, IDXS)],
                                       ACT.Copy).then_inc(idx_ready, 1)

                    def rows_of_step(i, s, first):
                        act.wait_ge(back, i * STEPS + (s + 1 + sbase))
                        if not (first and use == 0 and s < BUFS):
                            act.wait_ge(rows_out[s % BUFS], i * (16 * STEPS // BUFS)
                                        + 16 * (s // BUFS + ibase * STEPS // BUFS))
                        act.activation(ends[:, s % BUFS, :], bank[s % BUFS][:, :], ACT.Copy).then_inc(evac, 1)
                        if s % 2:
                            copy_idx(i + 1, s // 2)

                    def slab(i, n, h, place):
                        act.wait_ge(slab_mm, i * GPB + (n + 1))
                        act.activation(stage[:, h, :, bass.ds(place, GW)],
                                       bank[3 + n % GPS][:, 0:NW].rearrange("p (s w) -> p s w", w=GW),
                                       ACT.Copy).then_inc(slab_ev, 1)

                    def body(i, first, h, place, chunk=None, part=0):
                        for s in range(STEPS):
                            rows_of_step(i, s, first)
                            if chunk is not None and s % 2:
                                store_part(chunk, 1 - h, part + (1 + s // 2))
                            if adjacency:
                                for g in range(GPS):
                                    slab(i, GPS * s + g, h, place + (GPS * s + g) * GW)

                    def store_part(chunk, h, part):
                        at = adj[bass.ds(chunk, 1), :, bass.ds(part * PT, PT), :]
                        act.dma_start(at.rearrange("o p s w -> (o p) (s w)"),
                                      stage[:, h, bass.ds(part * PT, PT), :].rearrange("p s w -> p (s w)")
                                      ).then_inc(chunk_out[h], 16)

                    def middle_body(i, pair, first_pair):
                        for s in range(STEPS):
                            rows_of_step(i, s, False)
                            for g in range(GPS):
                                n = GPS * s + g
                                h = n // (GPB // 2)
                                if n == GPB // 2:
                                    act.wait_ge(slab_ev, pair * (2 * CG) + CG)
                                    store_part(pair * 2, 0, 0)
                                    if not first_pair:
                                        act.wait_ge(chunk_out[1], pair * (16 * PARTS))
                                slab(i, n, h, (CW - GPB // 2 * GW + n * GW) % CW)

                    for q in range(THIRDS):
                        copy_idx(0, q)
                    if not adjacency:
                        body(0, True, 0, 0)
                        with act.Fori(1, ITERS) as i:
                            body(i, False, 0, 0)
                        return
                    def last_bodies(pair):
                        with act.Fori(0, HB) as j:
                            body(pair * PB + j + (HB + 1), False, 1, j * (GPB * GW) + GPB // 2 * GW,
                                 pair * 2, j * (STEPS // 2))
                        act.wait_ge(slab_ev, pair * (2 * CG) + 2 * CG)
                        store_part(pair * 2 + 1, 1, 0)

                    body(0, True, 0, 0)
                    with act.Fori(1, HB) as j:
                        body(j, False, 0, j * (GPB * GW))
                    middle_body(HB, 0, True)
                    last_bodies(0)
                    with act.Fori(1, CHUNKS_A // 2) as pair:
                        act.wait_ge(chunk_out[0], pair * (16 * PARTS))
                        with act.Fori(0, HB) as j:
                            body(pair * PB + j, False, 0, j * (GPB * GW), pair * 2 - 1, j * (STEPS // 2))
                        middle_body(pair * PB + HB, pair, False)
                        last_bodies(pair)
                    for part in range(1, PARTS):
                        store_part(CHUNKS_A - 1, 1, part)
                    act.wait_ge(chunk_out[0], 16 * PARTS * CHUNKS_A // 2)

                @block.tensor
                def _(pe):
                    def turn(i, s, first):
                        for k in range(QUAD):
                            pe.wait_ge(landed[QUAD * s + k], i * 16 + (16 + landed_before(use, QUAD * s + k)))
                        if not (first and use == 0 and s < BUFS):
                            pe.wait_ge(evac, i * STEPS + (s + 1 - BUFS + sbase))
                        for k in range(QUAD):
                            mm = pe.transpose(bank[s % BUFS][:, k * P:(k + 1) * P], ring[:, QUAD * s + k, :], ident[:, :])
                        mm.then_inc(turned, 1)

                    def slabs(i, s, first):
                        for g in range(GPS):
                            n = GPS * s + g
                            pe.wait_ge(hot_ready, i * GPB + (n + 1))
                            if not (first and n < GPS):
                                pe.wait_ge(slab_ev, i * GPB + (n + 1 - GPS))
                            for w in range(2):
                                pe.matmul(bank[3 + g][:, 0:NW], hot_lo[:, g, w, :], hot_col[:, g, w, :],
                                          start=(w == 0), stop=(w == 1))
                                mm = pe.matmul(hist[:, 0:NODE_TILES], hot_lo[:, g, w, :],
                                               hot_hi[:, g, w, 0:NODE_TILES], start=False, stop=False,
                                               skip_group_check=True)
                            mm.then_inc(slab_mm, 1)

                    def turn_back(i, s):
                        pe.wait_ge(scan_done, i * STEPS + (s + 1 + sbase))
                        for k in range(QUAD):
                            mm = pe.transpose(bank[s % BUFS][:, k * P:(k + 1) * P],
                                              scanned[:, s % BUFS, k * P:(k + 1) * P], ident[:, :])
                        mm.then_inc(back, 1)

                    def body(i, first, last):
                        for s in range(STEPS):
                            if s < STEPS - 1:
                                turn(i, s + 1, first)
                            elif not last:
                                turn(i + 1, 0, False)
                            if adjacency:
                                slabs(i, s, first)
                            turn_back(i, s)

                    if adjacency:
                        pe.wait_ge(hist_zero, 2)
                        pe.matmul(hist[:, 0:NODE_TILES], hot_lo[:, 0, 0, :], hot_hi[:, 0, 0, 0:NODE_TILES],
                                  start=True, stop=False, skip_group_check=True).then_inc(hist_zero, 1)
                    turn(0, 0, True)
                    body(0, True, False)
                    with pe.Fori(1, ITERS - 1) as i:
                        body(i, False, False)
                    body(ITERS - 1, False, True)
                    if adjacency:
                        pe.wait_ge(hist_zero, 5)
                        pe.matmul(hist[:, 0:NODE_TILES], hot_lo[:, 0, 0, :], hot_hi[:, 0, 0, 0:NODE_TILES],
                                  start=False, stop=True, skip_group_check=True).then_inc(hist_zero, 1)

                @block.vector
                def _(dve):
                    def body(i, first):
                        for s in range(STEPS):
                            dve.wait_ge(turned, i * STEPS + (s + 1 + sbase))
                            dve.wait_ge(flags_in[s], i * 16 + (16 + 16 * use * (ITERS + 1)))
                            if not (first and s == 0):
                                dve.wait_ge(scan_done, i * STEPS + (s + sbase))
                            if not (first and use == 0 and s < BUFS):
                                dve.wait_ge(back, i * STEPS + (s + 1 - BUFS + sbase))
                            carry = (-BIG if ops[0] == ALU.min else 0.0) if first and s == 0 else \
                                scanned[:, (s - 1) % BUFS, W4 - 1:W4]
                            dve.tensor_tensor_scan(scanned[:, s % BUFS, :], flags[:, s, :], bank[s % BUFS][:, :], carry,
                                                   ops[0], ops[1]).then_inc(scan_done, 1)
                            if adjacency:
                                for g in range(GPS):
                                    n = GPS * s + g
                                    if first and n == 0:
                                        dve.wait_ge(hist_zero, 3)
                                    if not (first and n < GPS):
                                        dve.wait_ge(slab_mm, i * GPB + (n + 1 - GPS))
                                    for w in range(2):
                                        for k, (hot, width) in enumerate(((hot_col, NW), (hot_lo, P), (hot_hi, 50))):
                                            key = keyt[:, bass.ds(i * GPB + n, 1), w, k:k + 1].rearrange("p a b -> p (a b)")
                                            ins = dve.tensor_scalar(hot[:, g, w, :], iota_h[:, 0:width], key, None,
                                                                    ALU.is_equal)
                                    ins.then_inc(hot_ready, 1)

                    if adjacency:
                        dve.memset(hot_lo[:, 0, 0, :], 0.0).then_inc(hist_zero, 1)
                        dve.memset(hot_hi[:, 0, 0, :], 0.0).then_inc(hist_zero, 1)
                    body(0, True)
                    with dve.Fori(1, ITERS) as i:
                        body(i, False)
                    if adjacency:
                        dve.wait_ge(slab_mm, GROUPS)
                        dve.memset(hot_lo[:, 0, 0, :], 0.0).then_inc(hist_zero, 1)
                        dve.memset(hot_hi[:, 0, 0, :], 0.0).then_inc(hist_zero, 1)
                        dve.wait_ge(hist_zero, 6)
                        dve.tensor_copy(deg[:, 0, :], hist[:, 0:NODE_TILES])

        edge_pass(0, msg_table, idx_msg, keep_max, (ALU.min, ALU.max), True)

        conv_mm = sem("conv_mm")
        conv_ev = sem("conv_ev")
        leaky = sem("leaky")
        less = sem("less")
        gate_mm = sem("gate_mm")
        gate_ev = sem("gate_ev")
        mixed = sem("mixed")
        state = sem("state")
        scaled = sem("scaled")

        D_ = Region(0)
        parts = D_.take(NODE_TILES * 2 * P).bitcast(F16).rearrange("p (b s k d) -> p b s k d", b=2, s=NODE_TILES, k=2)
        inv_out = D_.take(NPAD)
        assert NODE_TILES * P <= NODE_TILES * CW // 2
        abuf = D_.take(S_A * CW).bitcast(F16).rearrange("p (b s w) -> p b s w", b=2, s=S_A)
        free_at = D_.at
        got = Region(xres_end).take(NODE_TILES * D).rearrange("p (t d) -> p t d", t=NODE_TILES)
        assert free_at <= xres_end + NODE_TILES * D <= scanned_at
        D_ = Region(scanned_at + NODE_TILES * 6 + 2 * W4)
        hs, rest = ([D_.take(W4) for _ in range(2)] for _ in range(2))
        inv_rows = D_.take(P)[0:2 * NODE_TILES, :]
        dense_at = D_.at
        node_rows = sem("node_rows")
        stat_done = sem("stat_done")
        aggr_done = sem("aggr_done")
        eps_done = sem("eps_done")
        root_done = sem("root_done")
        rstd_done = sem("rstd_done")
        nmr_done = sem("nmr_done")
        norm_rows = sem("norm_rows")
        norm_t = sem("norm_t")
        norm_cols = sem("norm_cols")
        inv_step = sem("inv_step")
        a_in = [sem(f"a_in{h}") for h in range(2)]
        inv_saved = sem("inv_saved")
        inv_out_in = sem("inv_out_in")
        res_out = [sem(f"res_out{k}") for k in range(2)]
        EARLY = -(-((free_at - S_A * CW // 2) - (xres_end - NODE_TILES * D)) // W4)
        turned_n = sem("turned_n")
        hi_done = sem("hi_done")
        rest_done = sem("rest_done")
        lo_done = sem("lo_done")

        def tiles(c):
            return tiles_done(c), tiles_done(c + 1)

        def tile_cols(c):
            return slice(tiles_done(c) * P, tiles_done(c + 1) * P)

        def pub_part(n, k):
            l, c = divmod(n, CHUNKS_A)
            t0, t1 = tiles(c)
            return parts[:, l % 2, t0:t1, k, :]

        def pub_bank(n):
            t0, t1 = tiles(n % CHUNKS_A)
            return bank[4 + n % 2][:, 0:(t1 - t0) * P].rearrange("p (t d) -> p t d", d=P)

        def pub_rest(n):
            t0, t1 = tiles(n % CHUNKS_A)
            return rest[n % 2][:, 0:(t1 - t0) * P].rearrange("p (t d) -> p t d", d=P)

        def publications(c):
            return [n for n in range(CHUNKS_A) if -(-tiles_done(n + 1) // CHUNK) - 1 == c]

        with nc.Block() as block:
            @block.gpsimd
            def _(pool):
                for t in range(NODE_TILES):
                    pool.indirect_dma_start(got[:, t, :], None, edge_rows,
                                            bass.IndirectOffsetOnAxis(ap=idx_end[:, t:t + 1], axis=0)
                                            ).then_inc(landed[t // CHUNK], 16)

            @block.sync
            def _(sp):
                sp.wait_ge(inv_step, 5)
                sp.dma_start(inv_dram.rearrange("k (t p) -> (k t) p", p=P), inv_rows).then_inc(inv_saved, 16)
                sp.wait_ge(inv_saved, 16)
                sp.wait_ge(chunk_out[1], 16 * PARTS * CHUNKS_A // 2)
                sp.dma_start(inv_out, inv_dram[0, :].partition_broadcast(P)).then_inc(inv_out_in, 16)
                for c in range(CHUNKS):
                    ts = slice(c * CHUNK, c * CHUNK + chunk_tiles(c))
                    sp.wait_ge(node_rows, c + 1)
                    sp.dma_start(res_dram[ts, :, :].rearrange("t p d -> p t d"), xres[:, ts, :]
                                 ).then_inc(res_out[c >= EARLY], 16)
                    if c == EARLY + 1:
                        sp.wait_ge(res_out[0], 16 * EARLY)
                        sp.wait_ge(norm_rows, EARLY)
                        sp.dma_start(abuf[:, 0, :, :], adj[0, :, 0:S_A, :]).then_inc(a_in[0], 16)
                sp.wait_ge(inv_out_in, 16)
                sp.wait_ge(res_out[1], 16 * (CHUNKS - EARLY))
                sp.wait_ge(a_in[0], 16)

            @block.vector
            def _(dve):
                def stats_of(c):
                    ts = slice(c * CHUNK, c * CHUNK + chunk_tiles(c))
                    dve.wait_ge(landed[c], 16 * (ITERS + chunk_tiles(c)))
                    dve.tensor_tensor(xres[:, ts, :], xres[:, ts, :], got[:, ts, :], ALU.add).then_inc(node_rows, 1)
                    dve.wait_ge(node_rows, c + 1)
                    for t in range(ts.start, ts.stop):
                        last = dve.bn_stats(stats[:, t, :], xres[:, t, :])
                    last.then_inc(stat_done, 1)
                    dve.wait_ge(stat_done, c + 1)
                    for t in range(ts.start, ts.stop):
                        last = dve.bn_aggr(mv[:, t, :], stats[:, t, :])
                    last.then_inc(aggr_done, 1)
                    dve.wait_ge(aggr_done, c + 1)
                    dve.tensor_scalar(rstd[:, ts], mv[:, ts, 1], EPS, None, ALU.add).then_inc(eps_done, 1)

                def scale_of(c):
                    ts = slice(c * CHUNK, c * CHUNK + chunk_tiles(c))
                    dve.wait_ge(root_done, c + 1)
                    dve.reciprocal(rstd[:, ts], rstd[:, ts]).then_inc(rstd_done, 1)
                    dve.wait_ge(rstd_done, c + 1)
                    dve.scalar_tensor_tensor(nmr[:, ts], mv[:, ts, 0], -1.0, rstd[:, ts], ALU.mult, ALU.mult
                                             ).then_inc(nmr_done, 1)

                def times_inv_out(n, c):
                    w = tile_cols(n).stop - tile_cols(n).start
                    dve.wait_ge(norm_cols, c + 1)
                    if n == 0:
                        dve.wait_ge(inv_out_in, 16)
                    if n >= 2:
                        dve.wait_ge(turned_n, n - 1)
                    dve.tensor_tensor(hs[n % 2][:, 0:w], xT[:, tile_cols(n)], inv_out[:, tile_cols(n)],
                                      ALU.mult).then_inc(scaled, 1)

                def rest_part(n):
                    dve.wait_ge(hi_done, n + 1)
                    if n >= 2:
                        dve.wait_ge(lo_done, n - 1)
                    dve.scalar_tensor_tensor(pub_rest(n), pub_bank(n), SCALE_0, pub_part(n, 0),
                                             ALU.mult, ALU.subtract).then_inc(rest_done, 1)

                d = deg[:, :, :].rearrange("p k t -> p (k t)")
                dve.tensor_scalar(d, d, 1.0, 1.0, ALU.add, ALU.max).then_inc(inv_step, 1)
                dve.wait_ge(inv_step, 2)
                dve.reciprocal(d, d).then_inc(inv_step, 1)
                dve.wait_ge(inv_step, 4)
                dve.tensor_copy(inv_rows, bank[4][0:2 * NODE_TILES, 0:P]).then_inc(inv_step, 1)
                for c in range(CHUNKS + 3):
                    if c < CHUNKS:
                        stats_of(c)
                    if 1 <= c <= CHUNKS:
                        scale_of(c - 1)
                    for n in publications(c - 3):
                        rest_part(n)
                    for n in publications(c - 2):
                        times_inv_out(n, c - 2)

            @block.scalar
            def _(act):
                act.wait_ge(inv_step, 1)
                d = deg[:, :, :].rearrange("p k t -> p (k t)")
                act.activation(d, d, ACT.Sqrt).then_inc(inv_step, 1)
                for c in range(CHUNKS + 3):
                    if c < CHUNKS:
                        ts = slice(c * CHUNK, c * CHUNK + chunk_tiles(c))
                        act.wait_ge(eps_done, c + 1)
                        act.activation(rstd[:, ts], rstd[:, ts], ACT.Sqrt).then_inc(root_done, 1)
                    if 1 <= c <= CHUNKS:
                        b = c - 1
                        act.wait_ge(nmr_done, b + 1)
                        if b >= 2:
                            act.wait_ge(norm_t, b - 1)
                        for k in range(chunk_tiles(b)):
                            t = b * CHUNK + k
                            last = act.activation(rows[b % 2][:, k, :], xres[:, t, :], ACT.Relu,
                                                  bias=nmr[:, t:t + 1], scale=rstd[:, t:t + 1])
                        last.then_inc(norm_rows, 1)
                        act.wait_ge(norm_t, b + 1)
                        act.activation(xT[:, cols(b)], bank[b % 2][:, 0:chunk_tiles(b) * P], ACT.Copy
                                       ).then_inc(norm_cols, 1)
                    for n in publications(c - 3):
                        act.wait_ge(rest_done, n + 1)
                        act.activation(pub_part(n, 1), pub_rest(n), ACT.Copy, scale=LO_SCALE).then_inc(lo_done, 1)
                    for n in publications(c - 2):
                        act.wait_ge(turned_n, n + 1)
                        act.activation(pub_part(n, 0), pub_bank(n), ACT.Copy, scale=SCALE_0).then_inc(hi_done, 1)

            @block.tensor
            def _(pe):
                pe.wait_ge(inv_step, 3)
                pe.transpose(bank[4][0:2 * NODE_TILES, 0:P], deg[:, :, :].rearrange("p k t -> p (k t)"),
                             ident[:, :]).then_inc(inv_step, 1)
                for c in range(CHUNKS + 3):
                    if 1 <= c <= CHUNKS:
                        b = c - 1
                        pe.wait_ge(norm_rows, b + 1)
                        if b >= 2:
                            pe.wait_ge(norm_cols, b - 1)
                        for k in range(chunk_tiles(b)):
                            mm = pe.transpose(bank[b % 2][:, k * P:(k + 1) * P], rows[b % 2][:, k, :], ident[:, :])
                        mm.then_inc(norm_t, 1)
                    for n in publications(c - 2):
                        t0, t1 = tiles(n)
                        pe.wait_ge(scaled, n + 1)
                        if n >= 2:
                            pe.wait_ge(rest_done, n - 1)
                        for t in range(t0, t1):
                            mm = pe.transpose(bank[4 + n % 2][:, (t - t0) * P:(t - t0 + 1) * P],
                                              hs[n % 2][:, (t - t0) * P:(t - t0 + 1) * P], ident[:, :])
                        mm.then_inc(turned_n, 1)

        def dense_layers():
            PROD = LAYERS * CHUNKS_A
            R = Region(free_at)
            agg, loop, hid, sca, mix, invi = ([R.take(CW) for _ in range(2)] for _ in range(6))
            babs = R.take(LAYERS * D).rearrange("p (l d) -> p l d", l=LAYERS)
            assert R.at <= scanned_at
            R = Region(dense_at)
            wsum = R.take(LAYERS * D).rearrange("p (l d) -> p l d", l=LAYERS)
            ones = R.take(P)
            bound, scale, unscale, unscale_lo = (R.take(LAYERS) for _ in range(4))
            inmin, growth, reach, top = (R.take(1) for _ in range(4))
            rows_o, rows_r = ([R.take(W4) for _ in range(2)] for _ in range(2))

            a_used = [sem(f"a_used{h}") for h in range(2)]
            cb_in = sem("cb_in")
            bound_step = sem("bound_step")
            bound_dve = sem("bound_dve")
            scales = sem("scales")
            lo_added = sem("lo_added")
            invi_in = [sem(f"invi_in{k}") for k in range(2)]
            res_in = [sem(f"res_in{k}") for k in range(2)]
            rows_saved = [sem(f"rows_saved{k}") for k in range(2)]
            looped = sem("looped")
            summed = sem("summed")
            normed = sem("normed")
            rows_done = sem("rows_done")

            def split(m):
                return divmod(m, CHUNKS_A)

            def width(c):
                return min(CW, NPAD - c * CW)

            def cols(c):
                return slice(c * CW, c * CW + width(c))

            with nc.Block() as block:
                @block.sync
                def _(sp):
                    for m in range(PROD):
                        for h, (lo, hi) in enumerate(((0, S_A), (S_A, NODE_TILES))):
                            if m == h == 0:
                                continue
                            if m >= 1:
                                sp.wait_ge(a_used[h], m * (4 if h == 0 else 1))
                            sp.dma_start(abuf[:, h, 0:hi - lo, :], adj[m % CHUNKS_A, :, lo:hi, :]).then_inc(a_in[h], 16)
                    for h in range(2):
                        sp.wait_ge(a_in[h], 16 * PROD)

                @block.gpsimd
                def _(pool):
                    def load_invi(m):
                        c = m % CHUNKS_A
                        if m >= 2:
                            pool.wait_ge(normed, m - 1)
                        pool.dma_start(invi[m % 2][:, 0:width(c)], inv_dram[1, cols(c)].partition_broadcast(P)
                                       ).then_inc(invi_in[m % 2], 16)

                    def times_inv_out(n):
                        c = n % CHUNKS_A
                        w = tile_cols(c).stop - tile_cols(c).start
                        if n >= 2:
                            pool.wait_ge(turned_n, n - 1)
                        pool.tensor_tensor(hs[n % 2][:, 0:w], xT[:, tile_cols(c)], inv_out[:, tile_cols(c)],
                                           ALU.mult).then_inc(scaled, 1)

                    pool.dma_start(babs.rearrange("p l d -> p (l d)"),
                                   conv_b.rearrange("l d -> (l d)").partition_broadcast(P)).then_inc(cb_in, 16)
                    load_invi(0)
                    for m in range(PROD):
                        l, c = split(m)
                        n = m + CHUNKS_A
                        last = l == LAYERS - 1
                        if l:
                            pool.wait_ge(state, m - CHUNKS_A + 1)
                        if m >= 2:
                            pool.wait_ge(summed, m - 1)
                        pool.tensor_tensor(loop[m % 2][:, 0:width(c)], xT[:, cols(c)],
                                           inv_out[:, cols(c)], ALU.mult).then_inc(looped, 1)
                        if last:
                            t0, t1 = tiles(c)
                            if c >= 2:
                                pool.wait_ge(rows_done, c - 1)
                            pool.dma_start(rows_r[c % 2][:, 0:(t1 - t0) * P].rearrange("p (t d) -> p t d", d=P),
                                           res_dram[t0:t1, :, :].rearrange("t p d -> p t d")
                                           ).then_inc(res_in[c % 2], 16)
                        if m < PROD - 1:
                            load_invi(m + 1)
                        if not last:
                            pool.wait_ge(state, m + 1)
                            times_inv_out(n)

                @block.tensor
                def _(pe):
                    def turn(n):
                        last = n >= LAYERS * CHUNKS_A
                        t0, t1 = tiles(n % CHUNKS_A)
                        if last:
                            pe.wait_ge(state, n - CHUNKS_A + 1)
                        else:
                            pe.wait_ge(scaled, n + 1)
                        if n - 2 >= LAYERS * CHUNKS_A:
                            pe.wait_ge(rows_done, n - 1 - LAYERS * CHUNKS_A)
                        elif n >= 2:
                            pe.wait_ge(rest_done, n - 1)
                        for t in range(t0, t1):
                            rows = xT[:, t * P:(t + 1) * P] if last else hs[n % 2][:, (t - t0) * P:(t - t0 + 1) * P]
                            mm = pe.transpose(bank[4 + n % 2][:, (t - t0) * P:(t - t0 + 1) * P], rows, ident[:, :])
                        mm.then_inc(turned_n, 1)

                    def products(m, h, s, n, start=False, stop=False):
                        l = m // CHUNKS_A
                        for j in range(n):
                            for k in range(2):
                                lhs = parts[:, l % 2, bass.ds(s + j, 1), k, :].rearrange("p a d -> p (a d)")
                                rhs = abuf[:, h, bass.ds(s + j - h * S_A, 1), :].rearrange("p a w -> p (a w)")
                                mm = pe.matmul(bank[6 * k + m % 2][:, 0:CW], lhs, rhs, start=start and j == 0,
                                               stop=stop and j == n - 1, skip_group_check=True)
                        return mm

                    def conv(m):
                        c = m % CHUNKS_A
                        pe.wait_ge(normed, m + 1)
                        if m == 0:
                            pe.wait_ge(scales, 1)
                        if m >= 1:
                            pe.wait_ge(conv_ev, m)
                        pe.matmul(bank[2][:, 0:width(c)], conv_sb[:, m // CHUNKS_A, :], agg[m % 2][:, 0:width(c)],
                                  start=True, stop=True).then_inc(conv_mm, 1)

                    def gate_x(m):
                        c = m % CHUNKS_A
                        if m >= 1:
                            pe.wait_ge(gate_ev, m)
                        pe.matmul(bank[3][:, 0:width(c)], g1T[:, :], xT[:, cols(c)], start=True, stop=False)

                    def gate_h(m):
                        c = m % CHUNKS_A
                        pe.wait_ge(leaky, m + 1)
                        pe.matmul(bank[3][:, 0:width(c)], g2T[:, :], hid[m % 2][:, 0:width(c)],
                                  start=False, stop=True).then_inc(gate_mm, 1)

                    pe.wait_ge(bound_step, 1)
                    pe.matmul(bank[2][:, :], ones, wsum.rearrange("p l d -> p (l d)"), start=True, stop=True)
                    pe.matmul(bank[3][:, 0:P], inmin.to_broadcast([P, P]), ident[:, :],
                              start=True, stop=True).then_inc(bound_step, 1)
                    for m in range(PROD):
                        l, c = split(m)
                        pe.wait_ge(a_in[0], 16 * (m + 1))
                        if m >= 2:
                            pe.wait_ge(summed, m - 1)
                        if c == 0:
                            pe.wait_ge(lo_done, l * CHUNKS_A + 8)
                        products(m, 0, 0, 1, start=True)
                        with pe.Fori(0, 4) as i:
                            products(m, 0, i * 6 + 1, 6).then_inc(a_used[0], 1)
                        if m:
                            conv(m - 1)
                            gate_x(m - 1)
                        pe.wait_ge(a_in[1], 16 * (m + 1))
                        if c == 0:
                            pe.wait_ge(lo_done, l * CHUNKS_A + 13)
                        products(m, 1, S_A, 9)
                        if m:
                            gate_h(m - 1)
                        products(m, 1, S_A + 9, 9)
                        if m:
                            turn(m - 1 + CHUNKS_A)
                        if c == 0:
                            pe.wait_ge(lo_done, (l + 1) * CHUNKS_A)
                        products(m, 1, S_A + 18, NODE_TILES - S_A - 18, stop=True).then_inc(a_used[1], 1)
                    conv(PROD - 1)
                    gate_x(PROD - 1)
                    gate_h(PROD - 1)
                    turn(PROD - 1 + CHUNKS_A)

                @block.scalar
                def _(act):
                    def hi_part(n):
                        l = n // CHUNKS_A
                        act.wait_ge(turned_n, n + 1)
                        act.activation(pub_part(n, 0), pub_bank(n), ACT.Copy, scale=scale[:, l:l + 1]
                                       ).then_inc(hi_done, 1)

                    def lo_part(n):
                        act.wait_ge(rest_done, n + 1)
                        act.activation(pub_part(n, 1), pub_rest(n), ACT.Copy, scale=LO_SCALE).then_inc(lo_done, 1)

                    act.wait_ge(scales, 1)
                    for m in range(PROD):
                        l, c = split(m)
                        act.wait_ge(conv_mm, m + 1)
                        if m >= 2:
                            act.wait_ge(state, m - 1)
                        act.activation(hid[m % 2][:, 0:width(c)], bank[2][:, 0:width(c)], ACT.Identity,
                                       bias=bcols[:, l:l + 1]).then_inc(conv_ev, 1)
                        act.wait_ge(gate_mm, m + 1)
                        act.activation(sca[m % 2][:, 0:width(c)], bank[3][:, 0:width(c)], ACT.Sigmoid,
                                       bias=bcols[:, LAYERS:LAYERS + 1]).then_inc(gate_ev, 1)
                        if l < LAYERS - 1:
                            hi_part(m + CHUNKS_A)
                            lo_part(m + CHUNKS_A)
                            continue
                        act.wait_ge(rows_done, c + 1)
                        t0, t1 = tiles(c)
                        k = t1 - t0
                        if c < CHUNKS_A - 1:
                            act.dma_start(out[t0 * P:t1 * P, :].rearrange("(t p) d -> p t d", p=P),
                                          rows_o[c % 2][:, 0:k * P].rearrange("p (t d) -> p t d", t=k)
                                          ).then_inc(rows_saved[c % 2], 16)
                        else:
                            act.dma_start(out[t0 * P:(t1 - 1) * P, :].rearrange("(t p) d -> p t d", p=P),
                                          rows_o[c % 2][:, 0:(k - 1) * P].rearrange("p (t d) -> p t d", t=k - 1)
                                          ).then_inc(rows_saved[c % 2], 16)
                            act.dma_start(out[(t1 - 1) * P:N, :], rows_o[c % 2][0:LAST, (k - 1) * P:k * P]
                                          ).then_inc(rows_saved[c % 2], 16)
                    act.wait_ge(rows_saved[0], 16 * (CHUNKS_A // 2))
                    act.wait_ge(rows_saved[1], 16 * (CHUNKS_A // 2 + 1))

                @block.vector
                def _(dve):
                    def rest_part(n):
                        l = n // CHUNKS_A
                        dve.wait_ge(hi_done, n + 1)
                        if n >= 2:
                            dve.wait_ge(lo_done, n - 1)
                        dve.scalar_tensor_tensor(pub_rest(n), pub_bank(n), scale[:, l:l + 1], pub_part(n, 0),
                                                 ALU.mult, ALU.subtract).then_inc(rest_done, 1)

                    bound_links = [0]

                    def L(ins):
                        bound_links[0] += 1
                        ins.then_inc(bound_dve, 1)
                        dve.wait_ge(bound_dve, bound_links[0])

                    dve.memset(ones, 1.0)
                    dve.memset(bound[:, 0:1], LN_MAX)
                    dve.memset(unscale[:, 0:1], 1.0 / SCALE_0)
                    dve.memset(unscale_lo[:, 0:1], 1.0 / SCALE_0 / LO_SCALE)
                    dve.scalar_tensor_tensor(wsum, conv_sb[:, :, :], -1.0, conv_sb[:, :, :], ALU.mult, ALU.max)
                    dve.tensor_reduce(inmin, deg[:, 1, :], AX_X, ALU.min).then_inc(bound_step, 1)
                    dve.wait_ge(bound_step, 2)
                    dve.wait_ge(cb_in, 16)
                    L(dve.tensor_reduce(top, bank[3][:, 0:P], AX_X, ALU.min))
                    L(dve.reciprocal(growth, top))
                    L(dve.tensor_copy(wsum.rearrange("p l d -> p (l d)"), bank[2][:, :]))
                    L(dve.scalar_tensor_tensor(babs, babs, -1.0, babs, ALU.mult, ALU.max))
                    for l in range(LAYERS - 1):
                        L(dve.tensor_tensor(reach, growth, bound[:, l:l + 1], ALU.mult))
                        L(dve.scalar_tensor_tensor(wsum[:, l, :], wsum[:, l, :], reach, babs[:, l, :],
                                                   ALU.mult, ALU.add))
                        L(dve.tensor_reduce(top, wsum[:, l, :], AX_X, ALU.max))
                        L(dve.tensor_tensor(top, top, bound[:, l:l + 1], ALU.max))
                        L(dve.tensor_scalar(bound[:, l + 1:l + 2], top, BOUND_MAX, None, ALU.min))
                    new = slice(1, LAYERS)
                    L(dve.reciprocal(bound[:, new], bound[:, new]))
                    L(dve.tensor_scalar(bound[:, new], bound[:, new], FP16_TOP, None, ALU.mult))
                    L(dve.tensor_scalar(scale[:, new].bitcast(I32), bound[:, new].bitcast(I32), EXPONENT, None,
                                        ALU.bitwise_and))
                    L(dve.reciprocal(unscale[:, new], scale[:, new]))
                    dve.tensor_scalar(unscale_lo[:, new], unscale[:, new], 1.0 / LO_SCALE, None, ALU.mult
                                      ).then_inc(scales, 1)
                    for m in range(PROD):
                        l, c = split(m)
                        w = width(c)
                        a, h, x_h, g = (v[m % 2][:, 0:w] for v in (agg, hid, mix, sca))
                        dve.wait_ge(a_used[1], m + 1)
                        dve.wait_ge(looped, m + 1)
                        if m >= 2:
                            dve.wait_ge(conv_mm, m - 1)
                        if m == 0:
                            dve.wait_ge(scales, 1)
                        dve.scalar_tensor_tensor(a, bank[6 + m % 2][:, 0:w], unscale_lo[:, l:l + 1],
                                                 loop[m % 2][:, 0:w], ALU.mult, ALU.add).then_inc(lo_added, 1)
                        dve.wait_ge(lo_added, m + 1)
                        dve.scalar_tensor_tensor(a, bank[m % 2][:, 0:w], unscale[:, l:l + 1], a,
                                                 ALU.mult, ALU.add).then_inc(summed, 1)
                        dve.wait_ge(summed, m + 1)
                        dve.wait_ge(invi_in[m % 2], 16 * (m // 2 + 1))
                        dve.tensor_tensor(a, a, invi[m % 2][:, 0:w], ALU.mult).then_inc(normed, 1)
                        dve.wait_ge(conv_ev, m + 1)
                        dve.scalar_tensor_tensor(h, h, SLOPE, h, ALU.mult, ALU.max).then_inc(leaky, 1)
                        dve.wait_ge(leaky, m + 1)
                        if m >= 2:
                            dve.wait_ge(state, m - 1)
                        dve.tensor_tensor(x_h, xT[:, cols(c)], h, ALU.subtract).then_inc(less, 1)
                        dve.wait_ge(gate_ev, m + 1)
                        dve.wait_ge(less, m + 1)
                        dve.tensor_tensor(x_h, x_h, g, ALU.mult).then_inc(mixed, 1)
                        dve.wait_ge(mixed, m + 1)
                        dve.tensor_tensor(xT[:, cols(c)], h, x_h, ALU.add).then_inc(state, 1)
                        if l < LAYERS - 1:
                            rest_part(m + CHUNKS_A)
                            continue
                        t0, t1 = tiles(c)
                        k = (t1 - t0) * P
                        dve.wait_ge(turned_n, m + CHUNKS_A + 1)
                        dve.wait_ge(res_in[c % 2], 16 * (c // 2 + 1))
                        if c >= 2:
                            dve.wait_ge(rows_saved[c % 2], 16 * (c // 2))
                        dve.tensor_tensor(rows_o[c % 2][:, 0:k], bank[4 + c % 2][:, 0:k], rows_r[c % 2][:, 0:k],
                                          ALU.add).then_inc(rows_done, 1)

        def gather_layers():
            R = Region()
            acc, inv_o, inv_in = (R.take(NPAD) for _ in range(3))
            work = [R.take(W4) for _ in range(5)]
            assert R.at <= NODE_TILES * CW
            R = Region(hot_at)
            work += [R.take(W4) for _ in range(6)]
            R = Region(NODE_TILES * CW + NODE_TILES * D)
            idx_src = R.take(TPAD).bitcast(I32)
            key_i = R.take(TPAD).bitcast(I32)
            key_lo, key_hi = R.take(TPAD), R.take(TPAD)
            assert R.at <= NODE_TILES * CW + NODE_TILES * D + GC * P * 6
            rows_in = xres

            scaled_table = sem("scaled_table")
            key_ready = sem("key_ready")
            key_hot = sem("key_hot")
            key_mm = sem("key_mm")
            out_deg = sem("out_deg")
            tables_in = sem("tables_in")
            ends_in = sem("ends_in")
            ends_t = sem("ends_t")
            acc_add = sem("acc_add")
            res_back = sem("res_back")
            LAST_EDGES = E - (EDGE_TILES - 1) * P
            PAIRS = (EDGE_TILES - 1) // 2
            assert EDGE_TILES % 2 == 1

            norm_in = sem("norm_in")
            out_ev = sem("out_ev")
            final = [sem(f"final{k}") for k in range(2)]

            def update(layer):
                last = layer == LAYERS - 1
                b = layer * CHUNKS
                agg = [work[k] for k in range(3)]
                hid = [work[3 + k] for k in range(2)]
                sca = [work[5 + k] for k in range(2)]
                mix = [work[7 + k] for k in range(2)]

                def wd(c):
                    return chunk_tiles(c) * P

                with nc.Block() as block:
                    @block.gpsimd
                    def _(pool):
                        for c in range(CHUNKS + 3):
                            if c < CHUNKS:
                                if c >= 3:
                                    pool.wait_ge(conv_mm, b + c - 2)
                                pool.tensor_tensor(agg[c % 3][:, 0:wd(c)], acc[:, cols(c)], inv_in[:, cols(c)],
                                                   ALU.mult).then_inc(norm_in, 1)
                            if c >= 3 and not last:
                                pool.wait_ge(state, b + c - 2)
                                pool.wait_ge(norm_in, b + c - 2)
                                pub_scale(pool, c - 3)

                    @block.tensor
                    def _(pe):
                        def conv(c):
                            pe.wait_ge(norm_in, b + c + 1)
                            if b + c >= 2:
                                pe.wait_ge(conv_ev, b + c - 1)
                            pe.matmul(bank[c % 2][:, 0:wd(c)], conv_sb[:, layer, :], agg[c % 3][:, 0:wd(c)],
                                      start=True, stop=True).then_inc(conv_mm, 1)

                        def gate(c):
                            if b + c >= 2:
                                pe.wait_ge(gate_ev, b + c - 1)
                            pe.matmul(bank[2 + c % 2][:, 0:wd(c)], g1T[:, :], xT[:, cols(c)], start=True, stop=False)
                            pe.wait_ge(leaky, b + c + 1)
                            pe.matmul(bank[2 + c % 2][:, 0:wd(c)], g2T[:, :], hid[c % 2][:, 0:wd(c)],
                                      start=False, stop=True).then_inc(gate_mm, 1)

                        def turn(c):
                            if last:
                                pe.wait_ge(state, b + c + 1)
                                if c >= 2:
                                    pe.wait_ge(out_ev, c - 1)
                                for k in range(chunk_tiles(c)):
                                    t = c * CHUNK + k
                                    mm = pe.transpose(bank[4 + c % 2][:, k * P:(k + 1) * P], xT[:, t * P:(t + 1) * P],
                                                      ident[:, :])
                                mm.then_inc(tab_t, 1)
                            else:
                                pe.wait_ge(scaled_table, b + CHUNKS + c + 1)
                                pub_turn(pe, layer + 1, c, acc)

                        for c in range(CHUNKS + 4):
                            if c < CHUNKS:
                                conv(c)
                            if 1 <= c <= CHUNKS:
                                gate(c - 1)
                            if c >= 4:
                                turn(c - 4)

                    @block.scalar
                    def _(act):
                        for c in range(CHUNKS + 5):
                            if c < CHUNKS:
                                act.wait_ge(conv_mm, b + c + 1)
                                if b + c >= 2:
                                    act.wait_ge(state, b + c - 1)
                                act.activation(hid[c % 2][:, 0:wd(c)], bank[c % 2][:, 0:wd(c)], ACT.Identity,
                                               bias=bcols[:, layer:layer + 1]).then_inc(conv_ev, 1)
                            if 1 <= c <= CHUNKS:
                                act.wait_ge(gate_mm, b + c)
                                if b + c >= 3:
                                    act.wait_ge(mixed, b + c - 2)
                                act.activation(sca[(c - 1) % 2][:, 0:wd(c - 1)], bank[2 + (c - 1) % 2][:, 0:wd(c - 1)],
                                               ACT.Sigmoid, bias=bcols[:, LAYERS:LAYERS + 1]).then_inc(gate_ev, 1)
                            if c >= 5 and not last:
                                pub_rows(act, layer + 1, c - 5)

                    @block.vector
                    def _(dve):
                        if last:
                            dve.wait_ge(res_back, 16)
                        for c in range(CHUNKS + 5):
                            if c < CHUNKS:
                                h, m = hid[c % 2][:, 0:wd(c)], mix[c % 2][:, 0:wd(c)]
                                dve.wait_ge(conv_ev, b + c + 1)
                                dve.scalar_tensor_tensor(h, h, SLOPE, h, ALU.mult, ALU.max).then_inc(leaky, 1)
                                dve.wait_ge(leaky, b + c + 1)
                                dve.tensor_tensor(m, xT[:, cols(c)], h, ALU.subtract).then_inc(less, 1)
                            if 1 <= c <= CHUNKS:
                                d = c - 1
                                h, m, g = hid[d % 2][:, 0:wd(d)], mix[d % 2][:, 0:wd(d)], sca[d % 2][:, 0:wd(d)]
                                dve.wait_ge(gate_ev, b + d + 1)
                                dve.wait_ge(less, b + d + 1)
                                dve.tensor_tensor(m, m, g, ALU.mult).then_inc(mixed, 1)
                                dve.wait_ge(mixed, b + d + 1)
                                dve.tensor_tensor(xT[:, cols(d)], h, m, ALU.add).then_inc(state, 1)
                            if c >= 5 and last:
                                d = c - 5
                                k = chunk_tiles(d)
                                dve.wait_ge(tab_t, (LAYERS * CHUNKS) + d + 1)
                                if d >= 2:
                                    dve.wait_ge(final[d % 2], 16 * (d // 2))
                                dve.tensor_tensor(row_stage[d % 2][:, 0:k * P],
                                                  xres[:, d * CHUNK:d * CHUNK + k, :].rearrange("p t d -> p (t d)"),
                                                  bank[4 + d % 2][:, 0:k * P], ALU.add).then_inc(out_ev, 1)

                    @block.sync
                    def _(sp):
                        if last:
                            sp.dma_start(xres[:, :, :], res_dram.rearrange("t p d -> p t d")).then_inc(res_back, 16)
                        for c in range(CHUNKS):
                            if not last:
                                pub_store(sp, layer + 1, c)
                            elif c < CHUNKS - 1:
                                sp.wait_ge(out_ev, c + 1)
                                sp.dma_start(out[c * CHUNK * P:(c + 1) * CHUNK * P, :].rearrange("(t p) d -> p t d", p=P),
                                             row_stage[c % 2].rearrange("p (t d) -> p t d", t=CHUNK)).then_inc(final[c % 2], 16)
                            else:
                                sp.wait_ge(out_ev, c + 1)
                                sp.dma_start(out[(NODE_TILES - 1) * P:N, :], row_stage[c % 2][0:LAST, 0:D]).then_inc(final[c % 2], 16)
                        if last:
                            for k in range(2):
                                sp.wait_ge(final[k], 16 * len(range(k, CHUNKS, 2)))
                        else:
                            for k in range(2):
                                sp.wait_ge(row_out[k], 16 * stores_before(layer + 2, k))

            tab_t = sem("tab_t")
            row_ev = sem("row_ev")
            row_out = [sem(f"row_out{k}") for k in range(2)]
            row_stage = [work[9], work[10]]

            def stores_before(use, c):
                return use * len(range(c % 2, CHUNKS, 2)) + c // 2

            def pub_scale(pool, c):
                pool.tensor_tensor(acc[:, cols(c)], xT[:, cols(c)], inv_o[:, cols(c)], ALU.mult).then_inc(scaled_table, 1)

            def pub_turn(pe, use, c, src):
                if use * CHUNKS + c >= 2:
                    pe.wait_ge(row_ev, use * CHUNKS + c - 1)
                for k in range(chunk_tiles(c)):
                    t = c * CHUNK + k
                    mm = pe.transpose(bank[4 + c % 2][:, k * P:(k + 1) * P], src[:, t * P:(t + 1) * P], ident[:, :])
                mm.then_inc(tab_t, 1)

            def pub_rows(act, use, c):
                n = use * CHUNKS + c
                act.wait_ge(tab_t, n + 1)
                if stores_before(use, c):
                    act.wait_ge(row_out[c % 2], 16 * stores_before(use, c))
                act.activation(row_stage[c % 2][:, 0:chunk_tiles(c) * P], bank[4 + c % 2][:, 0:chunk_tiles(c) * P],
                               ACT.Copy).then_inc(row_ev, 1)

            def pub_store(sp, use, c):
                k = chunk_tiles(c)
                sp.wait_ge(row_ev, use * CHUNKS + c + 1)
                sp.dma_start(node_table[c * CHUNK * P:(c * CHUNK + k) * P, :].rearrange("(t p) d -> p t d", p=P),
                             row_stage[c % 2][:, 0:k * P].rearrange("p (t d) -> p t d", t=k)).then_inc(row_out[c % 2], 16)

            with nc.Block() as block:
                @block.sync
                def _(sp):
                    sp.dma_start(idx_src, src_idx).then_inc(tables_in, 16)
                    sp.wait_ge(out_deg, 4)
                    sp.dma_start(inv_dram[0, :].rearrange("(t p) -> t p", p=P), inv_rows[0:NODE_TILES, :]
                                 ).then_inc(tables_in, 16)
                    sp.wait_ge(tables_in, 32)
                    sp.dma_start(inv_o, inv_dram[0, :].partition_broadcast(P)).then_inc(tables_in, 16)
                    sp.dma_start(inv_in, inv_dram[1, :].partition_broadcast(P)).then_inc(tables_in, 16)
                    sp.wait_ge(tables_in, 64)

                @block.vector
                def _(dve):
                    def pair(i, first):
                        for k in range(2):
                            if not first:
                                dve.wait_ge(key_mm, i * 2 + (k - 1))
                            one_hots(bass.ds(i * 2 + k, 1), k)

                    def one_hots(column, k):
                        dve.tensor_scalar(hot_lo[:, 0, k, :], iota_h[:, 0:P], key_lo[:, column], None, ALU.is_equal)
                        dve.tensor_scalar(hot_hi[:, 0, k, :], iota_h[:, 0:50], key_hi[:, column], None,
                                          ALU.is_equal).then_inc(key_hot, 1)

                    dve.wait_ge(tables_in, 16)
                    dve.wait_ge(s_const, 5)
                    dve.tensor_scalar(key_i, idx_src, P - 1, None, ALU.bitwise_and).then_inc(key_ready, 1)
                    dve.wait_ge(key_ready, 1)
                    dve.tensor_copy(key_lo, key_i).then_inc(key_ready, 1)
                    dve.wait_ge(key_ready, 2)
                    dve.tensor_scalar(key_i, idx_src, 7, None, ALU.arith_shift_right).then_inc(key_ready, 1)
                    dve.wait_ge(key_ready, 3)
                    dve.tensor_copy(key_hi, key_i).then_inc(key_ready, 1)
                    dve.wait_ge(key_ready, 4)
                    pair(0, True)
                    with dve.Fori(1, PAIRS) as i:
                        pair(i, False)
                    dve.wait_ge(key_mm, 2 * PAIRS - 1)
                    one_hots(slice(2 * PAIRS, 2 * PAIRS + 1), 0)
                    dve.wait_ge(key_mm, 2 * PAIRS + 1)
                    d = deg[:, 0, :]
                    dve.tensor_scalar(d, hist[:, 0:NODE_TILES], 1.0, 1.0, ALU.add, ALU.max).then_inc(out_deg, 1)
                    dve.wait_ge(out_deg, 2)
                    dve.reciprocal(d, d).then_inc(key_ready, 1)
                    dve.wait_ge(out_deg, 3)
                    dve.tensor_copy(inv_rows[0:NODE_TILES, :], bank[4][0:NODE_TILES, 0:P]).then_inc(out_deg, 1)

                @block.scalar
                def _(act):
                    act.wait_ge(out_deg, 1)
                    act.activation(deg[:, 0, :], deg[:, 0, :], ACT.Sqrt).then_inc(out_deg, 1)

                @block.tensor
                def _(pe):
                    def count(k, n, **flags):
                        pe.matmul(hist[:, 0:NODE_TILES], hot_lo[0:n, 0, k, :], hot_hi[0:n, 0, k, 0:NODE_TILES],
                                  skip_group_check=True, **flags).then_inc(key_mm, 1)

                    pe.wait_ge(key_hot, 1)
                    count(0, P, start=True, stop=False)
                    pe.wait_ge(key_hot, 2)
                    count(1, P, start=False, stop=False)
                    with pe.Fori(1, PAIRS) as i:
                        for k in range(2):
                            pe.wait_ge(key_hot, i * 2 + (k + 1))
                            count(k, P, start=False, stop=False)
                    pe.wait_ge(key_hot, 2 * PAIRS + 1)
                    count(0, LAST_EDGES, start=False, stop=True)
                    pe.wait_ge(key_ready, 5)
                    pe.transpose(bank[4][0:NODE_TILES, 0:P], deg[:, 0, :], ident[:, :]).then_inc(out_deg, 1)

                @block.gpsimd
                def _(pool):
                    pool.iota(iota_h, [[1, 512]], base=0, channel_multiplier=0,
                              allow_small_or_imprecise_dtypes=True).then_inc(s_const, 1)
                    pool.wait_ge(out_deg, 4)

            with nc.Block() as block:
                @block.gpsimd
                def _(pool):
                    for c in range(CHUNKS):
                        pub_scale(pool, c)

                @block.tensor
                def _(pe):
                    for c in range(CHUNKS):
                        pe.wait_ge(scaled_table, c + 1)
                        pub_turn(pe, 0, c, acc)

                @block.scalar
                def _(act):
                    for c in range(CHUNKS):
                        pub_rows(act, 0, c)

                @block.vector
                def _(dve):
                    dve.wait_ge(row_ev, CHUNKS)

                @block.sync
                def _(sp):
                    for c in range(CHUNKS):
                        pub_store(sp, 0, c)
                    for k in range(2):
                        sp.wait_ge(row_out[k], 16 * stores_before(1, k))

            def last_edges(layer):
                with nc.Block() as block:
                    @block.gpsimd
                    def _(pool):
                        for t in range(NODE_TILES):
                            pool.indirect_dma_start(rows_in[:, t, :], None, edge_rows,
                                                    bass.IndirectOffsetOnAxis(ap=idx_end[:, t:t + 1], axis=0)
                                                    ).then_inc(ends_in, 16)

                    @block.tensor
                    def _(pe):
                        pe.wait_ge(ends_in, 16 * NODE_TILES * (layer + 1))
                        for c in range(CHUNKS):
                            if layer * CHUNKS + c >= 2:
                                pe.wait_ge(acc_add, layer * CHUNKS + c - 1)
                            for k in range(chunk_tiles(c)):
                                mm = pe.transpose(bank[c % 2][:, k * P:(k + 1) * P], rows_in[:, c * CHUNK + k, :],
                                                  ident[:, :])
                            mm.then_inc(ends_t, 1)

                    @block.vector
                    def _(dve):
                        for c in range(CHUNKS):
                            dve.wait_ge(ends_t, layer * CHUNKS + c + 1)
                            dve.tensor_tensor(acc[:, cols(c)], acc[:, cols(c)], bank[c % 2][:, 0:chunk_tiles(c) * P],
                                              ALU.add).then_inc(acc_add, 1)

                    @block.scalar
                    def _(act):
                        act.wait_ge(acc_add, (layer + 1) * CHUNKS)

                    @block.sync
                    def _(sp):
                        sp.wait_ge(acc_add, (layer + 1) * CHUNKS)

            for layer in range(LAYERS):
                edge_pass(layer + 1, node_table, idx_src, keep_sum, (ALU.mult, ALU.add), False)
                last_edges(layer)
                update(layer)

        regs = nc.alloc_registers("overfull")
        nc.regs_load(regs, flag[0:1, 0:1])
        with nc.If_cmp(regs, 0, "IS_EQ"):
            dense_layers()
        with nc.Else():
            gather_layers()
        nc.all_engine_barrier()


def kernel(**inputs):
    import numpy as np
    import concourse.bacc as bacc
    from concourse.bass_utils import run_bass_kernel_spmd as run

    x, src, dst, rel = (np.asarray(inputs[k]) for k in ("x", "src", "dst", "edge_type_4"))

    def padded(a, fill, more=0):
        return np.concatenate([a, np.full(EDGE_ROWS * P - E + more, fill, a.dtype)])

    before = np.concatenate([np.full(1, -1, dst.dtype), dst[:-1]])
    after = np.concatenate([dst[1:], np.full(1, N, dst.dtype)])
    arrays = {"x": x}
    for name, a, fill in (("src", src, 0), ("rel", rel, 0), ("dst", dst, N), ("before", before, N), ("after", after, N)):
        arrays[name] = padded(a, fill).reshape(EDGE_ROWS, P)
    at = np.arange(WIN_ROWS)[:, None] * ALIGN + np.arange(WIN)
    arrays["windows"] = np.concatenate([padded(src, 0, WIN)[at], padded(dst, FAR, WIN)[at]], axis=1)
    for name, key in (("w0", "L0_gnn_weight"), ("b0", "L0_gnn_bias"), ("conv_w", "L1_gnn_conv_w"),
                      ("conv_b", "L1_gnn_conv_b"), ("gate_w1", "L1_gnn_gate_w1"),
                      ("gate_w2", "L1_gnn_gate_w2"), ("gate_b", "L1_gnn_gate_b")):
        arrays[name] = np.asarray(inputs[key])
    nc = bacc.Bacc("TRN2", target_bir_lowering=False, num_devices=1)
    arrays = {f"in_{k}": np.ascontiguousarray(a) for k, a in arrays.items()}
    args = [nc.dram_tensor(k, a.shape, mybir.dt.from_np(a.dtype), kind="ExternalInput").ap()
            for k, a in arrays.items()]
    out = nc.dram_tensor("out_x", (N, D), F32, kind="ExternalOutput").ap()
    build(nc, *args, out)
    r = run(nc, [arrays], core_ids=[0])
    return r.results[0]["out_x"]
```
